# Optimizing a Trainium2 kernel written in Bass

```python
import numpy as np
import jax
import jax.numpy as jnp

def _softmax(x, axis=-1):
    return jax.nn.softmax(x, axis=axis)

def _gelu(x):
    return jax.nn.gelu(x, approximate=True)

def _silu(x):
    return jax.nn.silu(x)

def _sigmoid(x):
    return jax.nn.sigmoid(x)

def _layernorm(x, axis=-1, eps=1e-05):
    m = jnp.mean(x, axis=axis, keepdims=True)
    v = jnp.var(x, axis=axis, keepdims=True)
    return (x - m) / jnp.sqrt(v + eps)

def _scatter_add(tgt, idx, src, axis=0):
    return tgt.at[idx].add(src)

def _segment_sum(src, seg, n):
    return jax.ops.segment_sum(src, seg, n)
kernel_name = 'mk_seq_postln_d2_jaxref_r8_0514da'

def setup_inputs(seed: int=0):
    np.random.seed(seed)
    _w = jnp.asarray

    def _L0_attn_setup():
        import jax, jax.numpy as jnp
        import numpy as np
        NUM_HEADS = 8
        SCALE_BASE = 512.0
        GN_EPS = 1e-05

        def rotate_every_two(x):
            x1 = x[..., ::2]
            x2 = x[..., 1::2]
            return jnp.stack([-x2, x1], axis=-1).reshape(x.shape)

        def xpos_apply(x, downscale):
            L, D = (x.shape[1], x.shape[2])
            half = D // 2
            scale_vec = (jnp.arange(0, D, 2, dtype=jnp.float32) + 0.4 * D) / (1.4 * D)
            pos = jnp.arange(L, dtype=jnp.float32)
            scale = scale_vec[None, :] ** (pos[:, None] / SCALE_BASE)
            inv_freq = 1.0 / 10000.0 ** (jnp.arange(half, dtype=jnp.float32) / half)
            sinusoid = pos[:, None] * inv_freq[None, :]
            sin, cos = (jnp.sin(sinusoid), jnp.cos(sinusoid))
            if downscale:
                scale = 1.0 / scale
            sin_s = jnp.repeat(sin * scale, 2, axis=-1)
            cos_s = jnp.repeat(cos * scale, 2, axis=-1)
            return x * cos_s + rotate_every_two(x) * sin_s

        def decay_mask_fn(T, num_heads):
            s, e = (np.log(1.0 / 32.0), np.log(1.0 / 512.0))
            gamma = 1.0 - jnp.exp(jnp.linspace(s, e, num_heads).astype(jnp.float32))
            log_decay = jnp.log(gamma)
            idx = jnp.arange(T)
            expo = (idx[:, None] - idx[None, :]).astype(jnp.float32)
            tri = idx[:, None] >= idx[None, :]
            expo_safe = jnp.where(tri, expo, 0.0)
            mask = jnp.exp(log_decay[:, None, None] * expo_safe) * tri
            scale = jnp.sqrt(mask.sum(axis=-1, keepdims=True))
            return mask / scale

        def _reference_tuple_inner(hidden_states, w_qkv, b_qkv, w_g, b_g, w_p, b_p):
            B, T, E = hidden_states.shape
            H = NUM_HEADS
            V = 2 * E
            dk, dv = (E // H, V // H)
            qkv = hidden_states @ w_qkv + b_qkv
            q, k, v = (qkv[..., :E], qkv[..., E:2 * E], qkv[..., 2 * E:])
            q = xpos_apply(q, downscale=False)
            k = xpos_apply(k, downscale=True)
            q = q.reshape(B, T, H, dk).transpose(0, 2, 1, 3)
            k = k.reshape(B, T, H, dk).transpose(0, 2, 1, 3)
            v = v.reshape(B, T, H, dv).transpose(0, 2, 1, 3)
            mask = decay_mask_fn(T, H)
            retention = jnp.einsum('bhid,bhjd->bhij', q, k) * dk ** (-0.5)
            retention = retention * mask[None]
            out = jnp.einsum('bhij,bhjv->bhiv', retention, v)
            curr_kv = jnp.einsum('hj,bhjk,bhjv->bhkv', mask[:, -1, :], k, v)
            retention_out = out.transpose(0, 2, 1, 3).reshape(B, T, V)
            g = retention_out.reshape(B * T, H, dv)
            mu = g.mean(axis=-1, keepdims=True)
            var = ((g - mu) ** 2).mean(axis=-1, keepdims=True)
            normed = ((g - mu) / jnp.sqrt(var + GN_EPS)).reshape(B, T, V)
            gated = jax.nn.silu(hidden_states @ w_g + b_g) * normed
            proj = gated @ w_p + b_p
            return (proj, curr_kv)
        key = jax.random.key(seed)
        ks = jax.random.split(key, 4)
        B, T, E = (2, 256, 128)
        V = 2 * E
        return {'hidden_states': jax.random.normal(ks[0], (B, T, E), dtype=jnp.float32), 'w_qkv': jax.random.normal(ks[1], (E, 2 * E + V), dtype=jnp.float32) * 0.02, 'b_qkv': jnp.zeros((2 * E + V,), dtype=jnp.float32), 'w_g': jax.random.normal(ks[2], (E, V), dtype=jnp.float32) * 0.02, 'b_g': jnp.zeros((V,), dtype=jnp.float32), 'w_p': jax.random.normal(ks[3], (V, E), dtype=jnp.float32) * 0.02, 'b_p': jnp.zeros((E,), dtype=jnp.float32)}
    _L0_attn_in = _L0_attn_setup()

    def _L0_ffn_setup():
        import jax, jax.numpy as jnp
        import numpy as np
        B, S, D, E, F = (2, 256, 128, 8, 512)
        key = jax.random.key(seed)
        ks = jax.random.split(key, 4)
        return {'hidden_states': jax.random.normal(ks[0], (B, S, D), dtype=jnp.float32), 'Wr': jax.random.normal(ks[1], (D, E), dtype=jnp.float32) * (1.0 / np.sqrt(D)), 'W1': jax.random.normal(ks[2], (E, D, F), dtype=jnp.float32) * (1.0 / np.sqrt(D)), 'b1': jnp.zeros((E, F), dtype=jnp.float32), 'W2': jax.random.normal(ks[3], (E, F, D), dtype=jnp.float32) * (1.0 / np.sqrt(F)), 'b2': jnp.zeros((E, D), dtype=jnp.float32)}
    _L0_ffn_in = _L0_ffn_setup()

    def _L1_attn_setup():
        import jax, jax.numpy as jnp
        import numpy as np
        N, L, D, A, F, B = (4, 512, 128, 128, 512, 8)
        EPS_LN = 1e-06
        EPS_Z = 1e-06

        def _layernorm(x, scale, bias):
            m = jnp.mean(x, axis=-1, keepdims=True)
            v = jnp.mean(jnp.square(x - m), axis=-1, keepdims=True)
            return (x - m) * jax.lax.rsqrt(v + EPS_LN) * scale + bias

        def _block(x, p):
            Wq, bq, Wk, bk, Wv, bv, Wo, bo, ln1_s, ln1_b, Wf1, bf1, Wf2, bf2, ln2_s, ln2_b = p
            residual = x
            q = jnp.einsum('nld,da->nla', x, Wq) + bq
            k = jnp.einsum('nld,da->nla', x, Wk) + bk
            v = jnp.einsum('nld,da->nla', x, Wv) + bv
            Q = jax.nn.elu(q) + 1.0
            K = jax.nn.elu(k) + 1.0
            KV = jnp.einsum('nsh,nsh->nh', K, v)
            Ksum = jnp.sum(K, axis=1)
            Z = 1.0 / (Q * Ksum[:, None, :] + EPS_Z)
            V = Q * KV[:, None, :] * Z
            attn = jax.nn.gelu(jnp.einsum('nla,ad->nld', V, Wo) + bo)
            x = _layernorm(attn + residual, ln1_s, ln1_b)
            residual = x
            h = jax.nn.gelu(jnp.einsum('nld,df->nlf', x, Wf1) + bf1)
            ff = jax.nn.gelu(jnp.einsum('nlf,fd->nld', h, Wf2) + bf2)
            x = _layernorm(ff + residual, ln2_s, ln2_b)
            return (x, None)
        key = jax.random.key(seed)
        ks = jax.random.split(key, 10)
        s = 0.02
        x = jax.random.normal(ks[0], (N, L, D), dtype=jnp.float32)
        Wq = jax.random.normal(ks[1], (B, D, A), dtype=jnp.float32) * s
        Wk = jax.random.normal(ks[2], (B, D, A), dtype=jnp.float32) * s
        Wv = jax.random.normal(ks[3], (B, D, A), dtype=jnp.float32) * s
        Wo = jax.random.normal(ks[4], (B, A, D), dtype=jnp.float32) * s
        Wf1 = jax.random.normal(ks[5], (B, D, F), dtype=jnp.float32) * s
        Wf2 = jax.random.normal(ks[6], (B, F, D), dtype=jnp.float32) * s
        return {'x': x, 'Wq': Wq, 'bq': jnp.zeros((B, A), jnp.float32), 'Wk': Wk, 'bk': jnp.zeros((B, A), jnp.float32), 'Wv': Wv, 'bv': jnp.zeros((B, A), jnp.float32), 'Wo': Wo, 'bo': jnp.zeros((B, D), jnp.float32), 'ln1_s': jnp.ones((B, D), jnp.float32), 'ln1_b': jnp.zeros((B, D), jnp.float32), 'Wf1': Wf1, 'bf1': jnp.zeros((B, F), jnp.float32), 'Wf2': Wf2, 'bf2': jnp.zeros((B, D), jnp.float32), 'ln2_s': jnp.ones((B, D), jnp.float32), 'ln2_b': jnp.zeros((B, D), jnp.float32)}
    _L1_attn_in = _L1_attn_setup()

    def _L1_ffn_setup():
        import jax, jax.numpy as jnp
        import numpy as np
        DIM = 128
        DEPTH = 2
        HEADS = 8
        DIM_HEAD = 64
        WINDOW = 64
        INNER = HEADS * DIM_HEAD
        HID = int(DIM * 4 * 2 / 3)
        B, N = (2, 1024)
        QK_SCALE = 8.0

        def shift_token(t):
            t1, t2 = jnp.split(t, 2, axis=-1)
            t2 = jnp.pad(t2, ((0, 0), (1, 0), (0, 0)))[:, :-1]
            return jnp.concatenate([t1, t2], axis=-1)

        def l2norm(t):
            return t / jnp.clip(jnp.linalg.norm(t, axis=-1, keepdims=True), 1e-12)

        def rotate_half(x):
            x1, x2 = jnp.split(x, 2, axis=-1)
            return jnp.concatenate([-x2, x1], axis=-1)

        def rotary_xpos(q, k):
            n = q.shape[-2]
            half_idx = jnp.arange(0, DIM_HEAD, 2, dtype=jnp.float32)
            inv_freq = 1.0 / 10000.0 ** (half_idx / DIM_HEAD)
            t = jnp.arange(n, dtype=jnp.float32)
            freqs = t[:, None] * inv_freq[None, :]
            freqs = jnp.concatenate([freqs, freqs], axis=-1)
            base = (half_idx + 0.4 * DIM_HEAD) / (1.4 * DIM_HEAD)
            power = (t - n // 2) / float(WINDOW // 2)
            scale = base[None, :] ** power[:, None]
            scale = jnp.concatenate([scale, scale], axis=-1)
            cos, sin = (jnp.cos(freqs), jnp.sin(freqs))
            q = q * cos * scale + rotate_half(q) * sin * scale
            k = k * cos / scale + rotate_half(k) * sin / scale
            return (q, k)

        def local_attention(q, k, v):
            b, h, n, d = q.shape
            w = n // WINDOW
            bq = q.reshape(b, h, w, WINDOW, d) * QK_SCALE
            bk = k.reshape(b, h, w, WINDOW, d)
            bv = v.reshape(b, h, w, WINDOW, d)

            def look_around(t):
                p = jnp.pad(t, ((0, 0), (0, 0), (1, 0), (0, 0), (0, 0)))
                return jnp.concatenate([p[:, :, :w], p[:, :, 1:]], axis=3)
            bk, bv = (look_around(bk), look_around(bv))
            bt = jnp.arange(n).reshape(w, WINDOW)
            btp = jnp.pad(bt, ((1, 0), (0, 0)), constant_values=-1)
            btk = jnp.concatenate([btp[:w], btp[1:]], axis=1)
            sim = jnp.einsum('bhwid,bhwjd->bhwij', bq, bk)
            i = bt[:, :, None]
            j = btk[:, None, :]
            mask = (i < j) | (i > j + WINDOW) | (j == -1)
            sim = jnp.where(mask, -jnp.finfo(sim.dtype).max, sim)
            attn = jax.nn.softmax(sim, axis=-1)
            out = jnp.einsum('bhwij,bhwjd->bhwid', attn, bv)
            return out.reshape(b, h, n, d)

        def _layer(x, wqkv, qs, ksc, wo, lg, lb, w1, b1, w2, b2):
            b, n, _ = x.shape
            h = shift_token(x)
            qkv = h @ wqkv
            q, k, v = jnp.split(qkv, 3, axis=-1)
            to_heads = lambda t: t.reshape(b, n, HEADS, DIM_HEAD).transpose(0, 2, 1, 3)
            q, k, v = (to_heads(q), to_heads(k), to_heads(v))
            q = l2norm(q) * qs
            k = l2norm(k) * ksc
            q, k = rotary_xpos(q, k)
            o = local_attention(q, k, v)
            o = o.transpose(0, 2, 1, 3).reshape(b, n, INNER)
            x = x + o @ wo
            h = shift_token(x)
            mu = h.mean(-1, keepdims=True)
            var = h.var(-1, keepdims=True)
            h = (h - mu) / jnp.sqrt(var + 1e-05) * lg + lb
            h = h @ w1 + b1
            a, g = jnp.split(h, 2, axis=-1)
            h = a * jax.nn.gelu(g, approximate=False)
            x = x + h @ w2 + b2
            return x
        key = jax.random.key(seed)
        ks = jax.random.split(key, 6)
        return {'x': jax.random.normal(ks[0], (B, N, DIM), jnp.float32), 'wqkv': jax.random.normal(ks[1], (DEPTH, DIM, 3 * INNER), jnp.float32) * 0.02, 'q_scale': jnp.ones((DEPTH, DIM_HEAD), jnp.float32), 'k_scale': jnp.ones((DEPTH, DIM_HEAD), jnp.float32), 'wo': jax.random.normal(ks[2], (DEPTH, INNER, DIM), jnp.float32) * 0.02, 'ln_g': jnp.ones((DEPTH, DIM), jnp.float32), 'ln_b': jnp.zeros((DEPTH, DIM), jnp.float32), 'w1': jax.random.normal(ks[3], (DEPTH, DIM, 2 * HID), jnp.float32) * 0.02, 'b1': jnp.zeros((DEPTH, 2 * HID), jnp.float32), 'w2': jax.random.normal(ks[4], (DEPTH, HID, DIM), jnp.float32) * 0.02, 'b2': jnp.zeros((DEPTH, DIM), jnp.float32)}
    _L1_ffn_in = _L1_ffn_setup()
    _d = {'L0_attn_hidden_states': _L0_attn_in['hidden_states'], 'L0_attn_w_qkv': _L0_attn_in['w_qkv'], 'L0_attn_b_qkv': _L0_attn_in['b_qkv'], 'L0_attn_w_g': _L0_attn_in['w_g'], 'L0_attn_b_g': _L0_attn_in['b_g'], 'L0_attn_w_p': _L0_attn_in['w_p'], 'L0_attn_b_p': _L0_attn_in['b_p'], 'L0_ffn_Wr': _L0_ffn_in['Wr'], 'L0_ffn_W1': _L0_ffn_in['W1'], 'L0_ffn_b1': _L0_ffn_in['b1'], 'L0_ffn_W2': _L0_ffn_in['W2'], 'L0_ffn_b2': _L0_ffn_in['b2'], 'L1_attn_Wq': _L1_attn_in['Wq'], 'L1_attn_bq': _L1_attn_in['bq'], 'L1_attn_Wk': _L1_attn_in['Wk'], 'L1_attn_bk': _L1_attn_in['bk'], 'L1_attn_Wv': _L1_attn_in['Wv'], 'L1_attn_bv': _L1_attn_in['bv'], 'L1_attn_Wo': _L1_attn_in['Wo'], 'L1_attn_bo': _L1_attn_in['bo'], 'L1_attn_ln1_s': _L1_attn_in['ln1_s'], 'L1_attn_ln1_b': _L1_attn_in['ln1_b'], 'L1_attn_Wf1': _L1_attn_in['Wf1'], 'L1_attn_bf1': _L1_attn_in['bf1'], 'L1_attn_Wf2': _L1_attn_in['Wf2'], 'L1_attn_bf2': _L1_attn_in['bf2'], 'L1_attn_ln2_s': _L1_attn_in['ln2_s'], 'L1_attn_ln2_b': _L1_attn_in['ln2_b'], 'L1_ffn_wqkv': _L1_ffn_in['wqkv'], 'L1_ffn_q_scale': _L1_ffn_in['q_scale'], 'L1_ffn_k_scale': _L1_ffn_in['k_scale'], 'L1_ffn_wo': _L1_ffn_in['wo'], 'L1_ffn_ln_g': _L1_ffn_in['ln_g'], 'L1_ffn_ln_b': _L1_ffn_in['ln_b'], 'L1_ffn_w1': _L1_ffn_in['w1'], 'L1_ffn_b1': _L1_ffn_in['b1'], 'L1_ffn_w2': _L1_ffn_in['w2'], 'L1_ffn_b2': _L1_ffn_in['b2']}
    _x0 = _d['L0_attn_hidden_states']
    _d['L0_attn_hidden_states'] = jax.random.normal(jax.random.fold_in(jax.random.key(seed), 1), (16, 512, 128), dtype=_x0.dtype)
    del _x0
    return _d

def reference(L0_attn_hidden_states, L0_attn_w_qkv, L0_attn_b_qkv, L0_attn_w_g, L0_attn_b_g, L0_attn_w_p, L0_attn_b_p, L0_ffn_Wr, L0_ffn_W1, L0_ffn_b1, L0_ffn_W2, L0_ffn_b2, L1_attn_Wq, L1_attn_bq, L1_attn_Wk, L1_attn_bk, L1_attn_Wv, L1_attn_bv, L1_attn_Wo, L1_attn_bo, L1_attn_ln1_s, L1_attn_ln1_b, L1_attn_Wf1, L1_attn_bf1, L1_attn_Wf2, L1_attn_bf2, L1_attn_ln2_s, L1_attn_ln2_b, L1_ffn_wqkv, L1_ffn_q_scale, L1_ffn_k_scale, L1_ffn_wo, L1_ffn_ln_g, L1_ffn_ln_b, L1_ffn_w1, L1_ffn_b1, L1_ffn_w2, L1_ffn_b2):

    def _L0_attn_ref(hidden_states, w_qkv, b_qkv, w_g, b_g, w_p, b_p):
        import jax, jax.numpy as jnp
        import numpy as np
        NUM_HEADS = 8
        SCALE_BASE = 512.0
        GN_EPS = 1e-05

        def rotate_every_two(x):
            x1 = x[..., ::2]
            x2 = x[..., 1::2]
            return jnp.stack([-x2, x1], axis=-1).reshape(x.shape)

        def xpos_apply(x, downscale):
            L, D = (x.shape[1], x.shape[2])
            half = D // 2
            scale_vec = (jnp.arange(0, D, 2, dtype=jnp.float32) + 0.4 * D) / (1.4 * D)
            pos = jnp.arange(L, dtype=jnp.float32)
            scale = scale_vec[None, :] ** (pos[:, None] / SCALE_BASE)
            inv_freq = 1.0 / 10000.0 ** (jnp.arange(half, dtype=jnp.float32) / half)
            sinusoid = pos[:, None] * inv_freq[None, :]
            sin, cos = (jnp.sin(sinusoid), jnp.cos(sinusoid))
            if downscale:
                scale = 1.0 / scale
            sin_s = jnp.repeat(sin * scale, 2, axis=-1)
            cos_s = jnp.repeat(cos * scale, 2, axis=-1)
            return x * cos_s + rotate_every_two(x) * sin_s

        def decay_mask_fn(T, num_heads):
            s, e = (np.log(1.0 / 32.0), np.log(1.0 / 512.0))
            gamma = 1.0 - jnp.exp(jnp.linspace(s, e, num_heads).astype(jnp.float32))
            log_decay = jnp.log(gamma)
            idx = jnp.arange(T)
            expo = (idx[:, None] - idx[None, :]).astype(jnp.float32)
            tri = idx[:, None] >= idx[None, :]
            expo_safe = jnp.where(tri, expo, 0.0)
            mask = jnp.exp(log_decay[:, None, None] * expo_safe) * tri
            scale = jnp.sqrt(mask.sum(axis=-1, keepdims=True))
            return mask / scale

        def _reference_tuple_inner(hidden_states, w_qkv, b_qkv, w_g, b_g, w_p, b_p):
            B, T, E = hidden_states.shape
            H = NUM_HEADS
            V = 2 * E
            dk, dv = (E // H, V // H)
            qkv = hidden_states @ w_qkv + b_qkv
            q, k, v = (qkv[..., :E], qkv[..., E:2 * E], qkv[..., 2 * E:])
            q = xpos_apply(q, downscale=False)
            k = xpos_apply(k, downscale=True)
            q = q.reshape(B, T, H, dk).transpose(0, 2, 1, 3)
            k = k.reshape(B, T, H, dk).transpose(0, 2, 1, 3)
            v = v.reshape(B, T, H, dv).transpose(0, 2, 1, 3)
            mask = decay_mask_fn(T, H)
            retention = jnp.einsum('bhid,bhjd->bhij', q, k) * dk ** (-0.5)
            retention = retention * mask[None]
            out = jnp.einsum('bhij,bhjv->bhiv', retention, v)
            curr_kv = jnp.einsum('hj,bhjk,bhjv->bhkv', mask[:, -1, :], k, v)
            retention_out = out.transpose(0, 2, 1, 3).reshape(B, T, V)
            g = retention_out.reshape(B * T, H, dv)
            mu = g.mean(axis=-1, keepdims=True)
            var = ((g - mu) ** 2).mean(axis=-1, keepdims=True)
            normed = ((g - mu) / jnp.sqrt(var + GN_EPS)).reshape(B, T, V)
            gated = jax.nn.silu(hidden_states @ w_g + b_g) * normed
            proj = gated @ w_p + b_p
            return (proj, curr_kv)
        return _reference_tuple_inner(hidden_states, w_qkv, b_qkv, w_g, b_g, w_p, b_p)[0]

    def _L0_ffn_ref(hidden_states, Wr, W1, b1, W2, b2):
        import jax, jax.numpy as jnp
        import numpy as np
        B, S, D, E, F = (2, 256, 128, 8, 512)
        b, s, d = hidden_states.shape
        e = Wr.shape[1]
        x = hidden_states.reshape(b * s, d)
        router_logits = x @ Wr
        router_probs = jax.nn.softmax(router_logits, axis=-1)
        expert_idx = jnp.argmax(router_probs, axis=-1)
        p_max = jnp.max(router_probs, axis=-1, keepdims=True)

        def expert_mlp(w1, bb1, w2, bb2):
            h = jax.nn.gelu(x @ w1 + bb1, approximate=False)
            return h @ w2 + bb2
        outs = jax.vmap(expert_mlp)(W1, b1, W2, b2)
        onehot = jax.nn.one_hot(expert_idx, e, dtype=x.dtype)
        next_states = jnp.einsum('te,etd->td', onehot, outs)
        out = p_max * next_states
        return out.reshape(b, s, d)

    def _L1_attn_ref(x, Wq, bq, Wk, bk, Wv, bv, Wo, bo, ln1_s, ln1_b, Wf1, bf1, Wf2, bf2, ln2_s, ln2_b):
        import jax, jax.numpy as jnp
        import numpy as np
        N, L, D, A, F, B = (4, 512, 128, 128, 512, 8)
        EPS_LN = 1e-06
        EPS_Z = 1e-06

        def _layernorm(x, scale, bias):
            m = jnp.mean(x, axis=-1, keepdims=True)
            v = jnp.mean(jnp.square(x - m), axis=-1, keepdims=True)
            return (x - m) * jax.lax.rsqrt(v + EPS_LN) * scale + bias

        def _block(x, p):
            Wq, bq, Wk, bk, Wv, bv, Wo, bo, ln1_s, ln1_b, Wf1, bf1, Wf2, bf2, ln2_s, ln2_b = p
            residual = x
            q = jnp.einsum('nld,da->nla', x, Wq) + bq
            k = jnp.einsum('nld,da->nla', x, Wk) + bk
            v = jnp.einsum('nld,da->nla', x, Wv) + bv
            Q = jax.nn.elu(q) + 1.0
            K = jax.nn.elu(k) + 1.0
            KV = jnp.einsum('nsh,nsh->nh', K, v)
            Ksum = jnp.sum(K, axis=1)
            Z = 1.0 / (Q * Ksum[:, None, :] + EPS_Z)
            V = Q * KV[:, None, :] * Z
            attn = jax.nn.gelu(jnp.einsum('nla,ad->nld', V, Wo) + bo)
            x = _layernorm(attn + residual, ln1_s, ln1_b)
            residual = x
            h = jax.nn.gelu(jnp.einsum('nld,df->nlf', x, Wf1) + bf1)
            ff = jax.nn.gelu(jnp.einsum('nlf,fd->nld', h, Wf2) + bf2)
            x = _layernorm(ff + residual, ln2_s, ln2_b)
            return (x, None)
        params = (Wq, bq, Wk, bk, Wv, bv, Wo, bo, ln1_s, ln1_b, Wf1, bf1, Wf2, bf2, ln2_s, ln2_b)
        out, _ = jax.lax.scan(_block, x, params)
        return out

    def _L1_ffn_ref(x, wqkv, q_scale, k_scale, wo, ln_g, ln_b, w1, b1, w2, b2):
        import jax, jax.numpy as jnp
        import numpy as np
        DIM = 128
        DEPTH = 2
        HEADS = 8
        DIM_HEAD = 64
        WINDOW = 64
        INNER = HEADS * DIM_HEAD
        HID = int(DIM * 4 * 2 / 3)
        B, N = (2, 1024)
        QK_SCALE = 8.0

        def shift_token(t):
            t1, t2 = jnp.split(t, 2, axis=-1)
            t2 = jnp.pad(t2, ((0, 0), (1, 0), (0, 0)))[:, :-1]
            return jnp.concatenate([t1, t2], axis=-1)

        def l2norm(t):
            return t / jnp.clip(jnp.linalg.norm(t, axis=-1, keepdims=True), 1e-12)

        def rotate_half(x):
            x1, x2 = jnp.split(x, 2, axis=-1)
            return jnp.concatenate([-x2, x1], axis=-1)

        def rotary_xpos(q, k):
            n = q.shape[-2]
            half_idx = jnp.arange(0, DIM_HEAD, 2, dtype=jnp.float32)
            inv_freq = 1.0 / 10000.0 ** (half_idx / DIM_HEAD)
            t = jnp.arange(n, dtype=jnp.float32)
            freqs = t[:, None] * inv_freq[None, :]
            freqs = jnp.concatenate([freqs, freqs], axis=-1)
            base = (half_idx + 0.4 * DIM_HEAD) / (1.4 * DIM_HEAD)
            power = (t - n // 2) / float(WINDOW // 2)
            scale = base[None, :] ** power[:, None]
            scale = jnp.concatenate([scale, scale], axis=-1)
            cos, sin = (jnp.cos(freqs), jnp.sin(freqs))
            q = q * cos * scale + rotate_half(q) * sin * scale
            k = k * cos / scale + rotate_half(k) * sin / scale
            return (q, k)

        def local_attention(q, k, v):
            b, h, n, d = q.shape
            w = n // WINDOW
            bq = q.reshape(b, h, w, WINDOW, d) * QK_SCALE
            bk = k.reshape(b, h, w, WINDOW, d)
            bv = v.reshape(b, h, w, WINDOW, d)

            def look_around(t):
                p = jnp.pad(t, ((0, 0), (0, 0), (1, 0), (0, 0), (0, 0)))
                return jnp.concatenate([p[:, :, :w], p[:, :, 1:]], axis=3)
            bk, bv = (look_around(bk), look_around(bv))
            bt = jnp.arange(n).reshape(w, WINDOW)
            btp = jnp.pad(bt, ((1, 0), (0, 0)), constant_values=-1)
            btk = jnp.concatenate([btp[:w], btp[1:]], axis=1)
            sim = jnp.einsum('bhwid,bhwjd->bhwij', bq, bk)
            i = bt[:, :, None]
            j = btk[:, None, :]
            mask = (i < j) | (i > j + WINDOW) | (j == -1)
            sim = jnp.where(mask, -jnp.finfo(sim.dtype).max, sim)
            attn = jax.nn.softmax(sim, axis=-1)
            out = jnp.einsum('bhwij,bhwjd->bhwid', attn, bv)
            return out.reshape(b, h, n, d)

        def _layer(x, wqkv, qs, ksc, wo, lg, lb, w1, b1, w2, b2):
            b, n, _ = x.shape
            h = shift_token(x)
            qkv = h @ wqkv
            q, k, v = jnp.split(qkv, 3, axis=-1)
            to_heads = lambda t: t.reshape(b, n, HEADS, DIM_HEAD).transpose(0, 2, 1, 3)
            q, k, v = (to_heads(q), to_heads(k), to_heads(v))
            q = l2norm(q) * qs
            k = l2norm(k) * ksc
            q, k = rotary_xpos(q, k)
            o = local_attention(q, k, v)
            o = o.transpose(0, 2, 1, 3).reshape(b, n, INNER)
            x = x + o @ wo
            h = shift_token(x)
            mu = h.mean(-1, keepdims=True)
            var = h.var(-1, keepdims=True)
            h = (h - mu) / jnp.sqrt(var + 1e-05) * lg + lb
            h = h @ w1 + b1
            a, g = jnp.split(h, 2, axis=-1)
            h = a * jax.nn.gelu(g, approximate=False)
            x = x + h @ w2 + b2
            return x
        for l in range(DEPTH):
            x = _layer(x, wqkv[l], q_scale[l], k_scale[l], wo[l], ln_g[l], ln_b[l], w1[l], b1[l], w2[l], b2[l])
        return x
    x = L0_attn_hidden_states
    x = _layernorm(x + _L0_attn_ref(x, L0_attn_w_qkv, L0_attn_b_qkv, L0_attn_w_g, L0_attn_b_g, L0_attn_w_p, L0_attn_b_p), axis=-1)
    x = _layernorm(x + _L0_ffn_ref(x, L0_ffn_Wr, L0_ffn_W1, L0_ffn_b1, L0_ffn_W2, L0_ffn_b2), axis=-1)
    x = _layernorm(x + _L1_attn_ref(x, L1_attn_Wq, L1_attn_bq, L1_attn_Wk, L1_attn_bk, L1_attn_Wv, L1_attn_bv, L1_attn_Wo, L1_attn_bo, L1_attn_ln1_s, L1_attn_ln1_b, L1_attn_Wf1, L1_attn_bf1, L1_attn_Wf2, L1_attn_bf2, L1_attn_ln2_s, L1_attn_ln2_b), axis=-1)
    x = _layernorm(x + _L1_ffn_ref(x, L1_ffn_wqkv, L1_ffn_q_scale, L1_ffn_k_scale, L1_ffn_wo, L1_ffn_ln_g, L1_ffn_ln_b, L1_ffn_w1, L1_ffn_b1, L1_ffn_w2, L1_ffn_b2), axis=-1)
    return x

_drawn_inputs = setup_inputs


def setup_inputs(seed=0):
    import zlib

    import numpy as np

    out = dict(_drawn_inputs(seed))
    spreads = {'L0_attn_b_qkv': (0.0, 0.1),
     'L0_attn_b_g': (0.0, 0.1),
     'L0_attn_b_p': (0.0, 0.1),
     'L0_ffn_b1': (0.0, 0.332),
     'L0_ffn_b2': (0.0, 0.1),
     'L1_attn_bq': (0.0, 2.0),
     'L1_attn_bk': (0.0, 2.0),
     'L1_attn_bv': (0.0, 0.428),
     'L1_attn_bo': (0.0, 0.1),
     'L1_attn_ln1_s': (1.0, 0.2),
     'L1_attn_ln1_b': (0.0, 0.1),
     'L1_attn_bf1': (0.0, 0.537),
     'L1_attn_bf2': (0.0, 0.1),
     'L1_attn_ln2_s': (1.0, 0.2),
     'L1_attn_ln2_b': (0.0, 0.1),
     'L1_ffn_q_scale': (1.0, 0.6),
     'L1_ffn_k_scale': (1.0, 0.6),
     'L1_ffn_ln_g': (1.0, 0.6),
     'L1_ffn_ln_b': (0.0, 0.8),
     'L1_ffn_b1': (0.0, 0.8),
     'L1_ffn_b2': (0.0, 0.626)}
    factors = {'L1_attn_Wq': 64.0,
     'L1_attn_Wk': 8.0,
     'L1_attn_Wv': 4.397,
     'L1_ffn_w1': 6.619,
     'L1_ffn_w2': 6.561}
    for name, (base, spread) in spreads.items():
        noise = np.random.default_rng([zlib.crc32(name.encode()), seed]).standard_normal(out[name].shape)
        drawn = base * np.exp(spread * noise) if base else spread * noise
        out[name] = jnp.asarray(drawn.astype(out[name].dtype))
    for name, factor in factors.items():
        out[name] = (out[name] * factor).astype(out[name].dtype)
    return out
```

```python
from contextlib import ExitStack

import numpy as np
import concourse.bass as bass
import concourse.mybir as mybir

F32 = mybir.dt.float32
ACT = mybir.ActivationFunctionType
ALU = mybir.AluOpType
AX = mybir.AxisListType

P = 128
B, T, D = 16, 512, 128
C = T // P
A_BLOCKS, A_FF = 8, 512
FT = A_FF // P
EPS_LN1, EPS_Z = 1e-6, 1e-6
TINY = 1e-37
LAG = 2
START = 4


class Shared:
    pass


def in_range(n, lag):
    return not isinstance(n, int) or 0 <= n - lag < B


def apart(eng, g):
    eng.sem_inc(g.passed, 1)


def phase_semaphore(nc, g, name):
    g.used.append(g.keep.enter_context(nc.semaphore(name)))
    return g.used[-1]


def run_phase(nc, g, build, *args):
    with ExitStack() as g.keep:
        g.used = []
        with ExitStack() as ctx:
            build(nc, ctx, g, *args)
        with nc.Block() as block:
            @block.gpsimd
            def _(pool):
                for sem in g.used:
                    pool.sem_clear(sem)


def layer_stats(dve, g, x, stats, mean_var, bn_done, count, mv_done):
    for c in range(C):
        last = dve.bn_stats(stats[:, c, :], x[:, c, :])
    last.then_inc(bn_done, 1)
    dve.wait_ge(bn_done, count)
    apart(dve, g)
    for c in range(C):
        last = dve.bn_aggr(mean_var[:, c, :], stats[:, c, :])
    last.then_inc(mv_done, 1)


def l1_attention(nc, ctx, g, w):
    def sb(name, shape):
        return ctx.enter_context(nc.sbuf_tensor("a1_" + name, shape, F32))

    def sem(name):
        return phase_semaphore(nc, g, "a1_" + name)

    xw, ident, bank = g.xw, g.ident, g.bank
    w_qkv = sb("w_qkv", [P, 3, D])
    w_o = sb("w_o", [P, D])
    w_f1 = sb("w_f1", [P, A_FF])
    w_f2 = sb("w_f2", [P, FT, D])
    VEC = ["bq", "bk", "bv", "bo", "ln1_s", "ln1_b", "bf2", "ln2_s", "ln2_b"]
    NROWS = len(VEC) * A_BLOCKS + FT * A_BLOCKS
    rows = sb("rows", [NROWS, P])
    cols = sb("cols", [P, NROWS])
    qv = sb("qv", [P, B, T])
    ex = sb("ex", [P, 2, 2, T])
    re = sb("re", [P, 2, 2, T])
    kk = sb("kk", [P, 2, T])
    junk = sb("junk", [P, T])
    zz = sb("zz", [P, 2, T])
    ksum = sb("ksum", [P, B])
    kvsum = sb("kvsum", [P, B])
    rks = sb("rks", [P, B])
    va = sb("va", [P, B])
    nva = sb("nva", [P, B])
    consts = sb("consts", [P, 2])
    eps_z, ln_eps_z = consts[:, 0:1], consts[:, 1:2]
    att = sb("att", [P, T])
    y1 = sb("y1", [P, T])
    xn1 = sb("xn1", [P, C, D])
    hid = sb("hid", [P, FT, T])
    ffo = sb("ffo", [P, T])
    y2 = sb("y2", [P, T])
    xn2 = sb("xn2", [P, C, D])
    st = sb("st", [P, 2, C, 6])
    mv = sb("mv", [P, 2, C, 2])
    ve = sb("ve", [P, 2, C])
    rstd = sb("rstd", [P, 2, C])
    mhalf = sb("mhalf", [P, C])

    def col(kind, blk):
        k = VEC.index(kind) * A_BLOCKS
        return cols[:, bass.ds(blk + k, 1)]

    def col_f1(blk, f):
        return cols[:, bass.ds(blk * FT + (len(VEC) * A_BLOCKS + f), 1)]

    rows_in = sem("rows_in")
    rows_T = sem("rows_T")
    cols_done = sem("cols_done")
    cst_done = sem("cst_done")
    x_done = sem("x_done")
    wa_in = sem("wa_in")
    wb_in = sem("wb_in")
    qk_mm = sem("qk_mm")
    v_mm = sem("v_mm")
    er_done = sem("er_done")
    k_done = sem("k_done")
    e_done = sem("e_done")
    q_done = sem("q_done")
    kv_done = sem("kv_done")
    coef = sem("coef")
    va_done = sem("va_done")
    ln_done = sem("ln_done")
    z_done = sem("z_done")
    v_done = sem("v_done")
    o_mm = sem("o_mm")
    att_done = sem("att_done")
    y1_done = sem("y1_done")
    y2_done = sem("y2_done")
    t1_mm = sem("t1_mm")
    t2_mm = sem("t2_mm")
    bn1_done, bn2_done = sem("bn1_done"), sem("bn2_done")
    mv1_done, mv2_done = sem("mv1_done"), sem("mv2_done")
    ve1_done, ve2_done = sem("ve1_done"), sem("ve2_done")
    rs1_done, rs2_done = sem("rs1_done"), sem("rs2_done")
    xn1_done = sem("xn1_done")
    xn2_done = sem("xn2_done")
    u1_mm = sem("u1_mm")
    u2_mm = sem("u2_mm")
    x1_done = sem("x1_done")
    h_mm = sem("h_mm")
    h_done = sem("h_done")
    f2_mm = sem("f2_mm")
    ff_done = sem("ff_done")

    def qbank(par):
        return bank[:, 0 + par, :]

    def kbank(par):
        return bank[:, 2 + par, :]

    def vbank(par):
        return bank[:, 4 + par, :]
    O, T1, U1, H, F, T2, U2 = 0, 1, 2, 3, 5, 6, 7

    def tiles(b):
        return bank[:, b, :].rearrange("p (c d) -> p c d", c=C)

    def loop_a(eng, step):
        step(0, 0)
        step(1, 1)
        with eng.Fori(1, B // 2) as pair:
            step(pair * 2, 0)
            step(pair * 2 + 1, 1)
        step(B, 0)

    DEEP = 3

    def loop_b(eng, step):
        for n in range(DEEP):
            step(n)
        with eng.Fori(DEEP, B) as n:
            step(n)
        for n in range(B, B + DEEP):
            step(n)

    block = ctx.enter_context(nc.Block())

    @block.sync
    def _(sp):
        names = VEC + ["bf1"]
        for i, name in enumerate(names):
            src = w[name] if name != "bf1" else w[name].rearrange("b (f p) -> (b f) p", p=P)
            n = src.shape[0]
            sp.dma_start(rows[i * A_BLOCKS:i * A_BLOCKS + n, :], src).then_inc(rows_in, 16)

        def load_a(b):
            for i, name in enumerate(["Wq", "Wk", "Wv"]):
                sp.dma_start(w_qkv[:, i, :], w[name][bass.ds(b, 1), :, :].rearrange("b p a -> (b p) a")).then_inc(wa_in, 16)

        def load_b(b):
            sp.dma_start(w_o[:, :], w["Wo"][bass.ds(b, 1), :, :].rearrange("b p a -> (b p) a")).then_inc(wb_in, 16)
            sp.dma_start(w_f1[:, :], w["Wf1"][bass.ds(b, 1), :, :].rearrange("b p a -> (b p) a")).then_inc(wb_in, 16)
            sp.dma_start(w_f2[:, :, :], w["Wf2"][bass.ds(b, 1), :, :].rearrange("b (k p) a -> p (b k) a", p=P)).then_inc(wb_in, 16)
        load_a(0)
        load_b(0)
        with sp.Fori(0, A_BLOCKS - 1) as b:
            sp.wait_ge(v_mm, b * B + B)
            load_a(b + 1)
            sp.wait_ge(f2_mm, b * B + B)
            load_b(b + 1)

    @block.tensor
    def _(pe):
        pe.wait_ge(rows_in, 16 * (len(VEC) + 1))
        pe.transpose(bank[:, 7, 0:NROWS], rows[:, :], ident[0:NROWS, 0:NROWS]).then_inc(rows_T, 1)
        pe.wait_ge(cols_done, 1)
        with pe.Fori(0, A_BLOCKS) as blk:
            base = blk * B

            def step_a(n, par):
                if not in_range(n, 0):
                    return
                at = n + base
                pe.wait_ge(x_done, at + 1)
                x = xw[:, n, :]
                pe.wait_ge(er_done, at + (1 + LAG - 2))
                pe.matmul(qbank(par), w_qkv[:, 0, :], x, start=True, stop=True)
                pe.matmul(kbank(par), w_qkv[:, 1, :], x, start=True, stop=True).then_inc(qk_mm, 1)
                pe.wait_ge(kv_done, at + (1 + LAG - 2))
                pe.matmul(vbank(par), w_qkv[:, 2, :], x, start=True, stop=True).then_inc(v_mm, 1)

            pe.wait_ge(wa_in, (blk + 1) * 48)
            pe.wait_ge(ff_done, base + LAG)
            loop_a(pe, step_a)

            def step_b(n):
                at = base + n
                if in_range(n, 1):
                    pe.wait_ge(y1_done, at + (LAG - 1 + 1))
                    pe.wait_ge(xn1_done, at + (LAG - 2 + 1))
                    for c in range(C):
                        mm = pe.transpose(tiles(T1)[:, c, :], y1[:, c * P:(c + 1) * P], ident[:, :])
                    mm.then_inc(t1_mm, 1)
                if in_range(n, 3):
                    pe.wait_ge(y2_done, at + (LAG - 3 + 1))
                    pe.wait_ge(xn2_done, at + (LAG - 4 + 1))
                    for c in range(C):
                        mm = pe.transpose(tiles(T2)[:, c, :], y2[:, c * P:(c + 1) * P], ident[:, :])
                    mm.then_inc(t2_mm, 1)
                if in_range(n, 2):
                    pe.wait_ge(x1_done, at + (LAG - 2 + 1))
                    for f in range(FT):
                        pe.wait_ge(h_done, (at - 2) * FT + (f - 2 + 1 + LAG * FT))
                        pe.matmul(bank[:, H + f % 2, :], w_f1[:, f * P:(f + 1) * P], xw[:, n - 2, :], start=True,
                                  stop=True).then_inc(h_mm, 1)
                if in_range(n, 0):
                    pe.wait_ge(att_done, at + (LAG - 1 + 1))
                    mm = pe.matmul(bank[:, O, :], w_o[:, :], qv[:, n, :], start=True, stop=True)
                    mm.then_inc(o_mm, 1)
                if in_range(n, 2):
                    pe.wait_ge(ff_done, at + (LAG - 3 + 1))
                    for f in range(2):
                        pe.wait_ge(h_done, (at - 2) * FT + (f + 1 + LAG * FT))
                        pe.matmul(bank[:, F, :], w_f2[:, f, :], hid[:, f, :], start=(f == 0), stop=False)
                if in_range(n, 1):
                    pe.wait_ge(xn1_done, at + (LAG - 1 + 1))
                    pe.wait_ge(x1_done, at + (LAG - 2 + 1))
                    for c in range(C):
                        mm = pe.transpose(bank[:, U1, c * P:(c + 1) * P], xn1[:, c, :], ident[:, :])
                    mm.then_inc(u1_mm, 1)
                if in_range(n, 3):
                    pe.wait_ge(xn2_done, at + (LAG - 3 + 1))
                    pe.wait_ge(x_done, at + (B - 4 + 1))
                    for c in range(C):
                        mm = pe.transpose(bank[:, U2, c * P:(c + 1) * P], xn2[:, c, :], ident[:, :])
                    mm.then_inc(u2_mm, 1)
                if in_range(n, 2):
                    for f in range(2, FT):
                        pe.wait_ge(h_done, (at - 2) * FT + (f + 1 + LAG * FT))
                        mm = pe.matmul(bank[:, F, :], w_f2[:, f, :], hid[:, f, :], start=False, stop=(f == FT - 1))
                    mm.then_inc(f2_mm, 1)

            pe.wait_ge(wb_in, (blk + 1) * 48)
            pe.wait_ge(er_done, base + (B + LAG))
            pe.wait_ge(z_done, base + (B + LAG))
            pe.wait_ge(v_done, base + (B + LAG))
            loop_b(pe, step_b)

    @block.scalar
    def _(act):
        act.wait_ge(cst_done, 1)
        act.sem_inc(x_done, B)
        for s in (er_done, z_done, att_done, x1_done, ff_done):
            act.sem_inc(s, LAG)
        act.sem_inc(h_done, LAG * FT)
        act.wait_ge(cols_done, 1)
        with act.Fori(0, A_BLOCKS) as blk:
            base = blk * B
            nc.scalar.preload_act_table_set("natural_log_exp_and_others")

            def step_a(n, par):
                at = base + n
                if in_range(n, 0):
                    act.wait_ge(qk_mm, at + 1)
                    act.wait_ge(q_done, at + (LAG - 2 + 1))
                    apart(act, g)
                    act.activation(ex[:, par, 1, :], kbank(par), ACT.Exp, bias=col("bk", blk))
                    act.activation(re[:, par, 1, :], kbank(par), ACT.Relu, bias=col("bk", blk))
                    act.activation(ex[:, par, 0, :], qbank(par), ACT.Exp, bias=col("bq", blk))
                    act.activation(re[:, par, 0, :], qbank(par), ACT.Relu, bias=col("bq", blk)).then_inc(er_done, 1)
                if in_range(n, 1):
                    q = 1 - par
                    act.wait_ge(v_done, at + (LAG - 3 + 1))
                    act.wait_ge(q_done, at + (LAG - 1 + 1))
                    apart(act, g)
                    act.activation(zz[:, q, :], qv[:, n - 1, :], ACT.Ln, bias=eps_z, scale=ksum[:, bass.ds(n - 1, 1)]).then_inc(ln_done, 1)
                    act.wait_ge(ln_done, at)
                    apart(act, g)
                    act.activation(zz[:, q, :], zz[:, q, :], ACT.Exp, bias=ln_eps_z, scale=-1.0).then_inc(z_done, 1)

            loop_a(act, step_a)
            nc.scalar.preload_act_table_set("gelu_apprx_tanh_and_others")

            def step_b(n):
                at = base + n
                if in_range(n, 2):
                    for f in range(FT):
                        act.wait_ge(h_mm, (at - 2) * FT + (f + 1))
                        act.wait_ge(f2_mm, at - 2)
                        apart(act, g)
                        act.activation(hid[:, f, :], bank[:, H + f % 2, :], ACT.Gelu_apprx_tanh, bias=col_f1(blk, f)).then_inc(h_done, 1)
                if in_range(n, 0):
                    act.wait_ge(o_mm, at + 1)
                    act.wait_ge(y1_done, at + (LAG - 1 + 1))
                    apart(act, g)
                    act.activation(att[:, :], bank[:, O, :], ACT.Gelu_apprx_tanh, bias=col("bo", blk)).then_inc(att_done, 1)
                if in_range(n, 1):
                    act.wait_ge(u1_mm, at)
                    apart(act, g)
                    act.activation(xw[:, n - 1, :], bank[:, U1, :], ACT.Identity, bias=col("ln1_b", blk), scale=col("ln1_s", blk)).then_inc(x1_done, 1)
                if in_range(n, 3):
                    act.wait_ge(u2_mm, at - 2)
                    apart(act, g)
                    act.activation(xw[:, n - 3, :], bank[:, U2, :], ACT.Identity, bias=col("ln2_b", blk), scale=col("ln2_s", blk)).then_inc(x_done, 1)
                if in_range(n, 2):
                    act.wait_ge(f2_mm, at - 1)
                    act.wait_ge(y2_done, at + (LAG - 3 + 1))
                    apart(act, g)
                    act.activation(ffo[:, :], bank[:, F, :], ACT.Gelu_apprx_tanh, bias=col("bf2", blk)).then_inc(ff_done, 1)

            loop_b(act, step_b)

    @block.vector
    def _(dve):
        dve.memset(eps_z, EPS_Z)
        dve.memset(ln_eps_z, float(np.log(EPS_Z)))
        dve.memset(mhalf[:, :], -0.5).then_inc(cst_done, 1)
        dve.wait_ge(rows_T, 1)
        dve.tensor_copy(cols[:, :], bank[:, 7, 0:NROWS]).then_inc(cols_done, 1)
        for s in (kv_done, q_done, v_done, xn1_done, xn2_done):
            dve.sem_inc(s, LAG)
        with dve.Fori(0, A_BLOCKS) as blk:
            base = blk * B

            def step_a(n, par):
                at = base + n
                if in_range(n, 0):
                    dve.wait_ge(er_done, at + (LAG + 1))
                    dve.scalar_tensor_tensor(out=kk[:, par, :], in0=ex[:, par, 1, :], scalar=1.0, in1=re[:, par, 1, :],
                                             op0=ALU.min, op1=ALU.add, accum_out=ksum[:, bass.ds(n, 1)]).then_inc(k_done, 1)
                    dve.tensor_scalar(ex[:, par, 0, :], ex[:, par, 0, :], 1.0, -1.0, ALU.min, ALU.add).then_inc(e_done, 1)
                    dve.wait_ge(k_done, at + 1)
                    dve.wait_ge(v_mm, at + 1)
                    dve.scalar_tensor_tensor(out=junk[:, :], in0=vbank(par), scalar=col("bv", blk), in1=kk[:, par, :],
                                             op0=ALU.add, op1=ALU.mult, accum_out=kvsum[:, bass.ds(n, 1)]).then_inc(kv_done, 1)
                    dve.tensor_scalar(rks[:, bass.ds(n, 1)], ksum[:, bass.ds(n, 1)], TINY, None, ALU.max).then_inc(coef, 1)
                    dve.wait_ge(e_done, at + 1)
                    dve.scalar_tensor_tensor(out=qv[:, n, :], in0=ex[:, par, 0, :], scalar=1.0, in1=re[:, par, 0, :],
                                             op0=ALU.add, op1=ALU.add).then_inc(q_done, 1)
                if in_range(n, 1):
                    dve.wait_ge(z_done, at + (LAG - 1 + 1))
                    dve.wait_ge(va_done, at)
                    dve.tensor_scalar(qv[:, n - 1, :], zz[:, 1 - par, :], nva[:, bass.ds(n - 1, 1)], va[:, bass.ds(n - 1, 1)],
                                      ALU.mult, ALU.add).then_inc(v_done, 1)
                if in_range(n, 0):
                    dve.wait_ge(coef, (at * 2) + 1)
                    apart(dve, g)
                    dve.reciprocal(rks[:, bass.ds(n, 1)], rks[:, bass.ds(n, 1)]).then_inc(coef, 1)
                    dve.wait_ge(coef, (at * 2) + 2)
                    dve.tensor_tensor(va[:, bass.ds(n, 1)], kvsum[:, bass.ds(n, 1)], rks[:, bass.ds(n, 1)], ALU.mult)
                    dve.scalar_tensor_tensor(out=nva[:, bass.ds(n, 1)], in0=kvsum[:, bass.ds(n, 1)], scalar=-1.0,
                                             in1=rks[:, bass.ds(n, 1)], op0=ALU.mult, op1=ALU.mult).then_inc(va_done, 1)

            loop_a(dve, step_a)

            def norm(src, dst, i, done):
                for c in range(C):
                    last = dve.tensor_scalar(dst[:, c, :], tiles(src)[:, c, :], mv[:, i, c, 0:1], rstd[:, i, c:c + 1],
                                             ALU.subtract, ALU.mult)
                last.then_inc(done, 1)

            def step_b(n):
                at = base + n
                first = in_range(n, 1)
                second = in_range(n, 3)
                if first:
                    dve.wait_ge(t1_mm, at)
                    layer_stats(dve, g, tiles(T1), st[:, 0], mv[:, 0], bn1_done, at, mv1_done)
                if second:
                    dve.wait_ge(t2_mm, at - 2)
                    layer_stats(dve, g, tiles(T2), st[:, 1], mv[:, 1], bn2_done, at - 2, mv2_done)
                if first:
                    dve.wait_ge(rs1_done, at)
                    dve.wait_ge(u1_mm, at - 1)
                    norm(T1, xn1, 0, xn1_done)
                if second:
                    dve.wait_ge(rs2_done, at - 2)
                    dve.wait_ge(u2_mm, at - 3)
                    norm(T2, xn2, 1, xn2_done)

            loop_b(dve, step_b)

    @block.gpsimd
    def _(pool):
        pool.sem_inc(y1_done, LAG)
        pool.sem_inc(y2_done, LAG)
        pool.wait_ge(cst_done, 1)
        with pool.Fori(0, A_BLOCKS) as blk:
            base = blk * B

            def rs(i, mv_s, ve_s, rs_s, count):
                pool.wait_ge(mv_s, count)
                apart(pool, g)
                pool.tensor_scalar(ve[:, i, :], mv[:, i, :, 1], EPS_LN1, None, ALU.add).then_inc(ve_s, 1)
                pool.wait_ge(ve_s, count)
                pool.tensor_tensor(rstd[:, i, :], ve[:, i, :], mhalf[:, :], ALU.pow).then_inc(rs_s, 1)

            def step_b(n):
                at = base + n
                if in_range(n, 1):
                    rs(0, mv1_done, ve1_done, rs1_done, at)
                if in_range(n, 3):
                    rs(1, mv2_done, ve2_done, rs2_done, at - 2)
                if in_range(n, 0):
                    pool.wait_ge(att_done, at + (LAG + 1))
                    pool.wait_ge(t1_mm, at)
                    pool.tensor_tensor(y1[:, :], att[:, :], xw[:, n, :], ALU.add).then_inc(y1_done, 1)
                if in_range(n, 2):
                    pool.wait_ge(ff_done, at + (LAG - 2 + 1))
                    pool.wait_ge(t2_mm, at - 2)
                    pool.tensor_tensor(y2[:, :], ffo[:, :], xw[:, n - 2, :], ALU.add).then_inc(y2_done, 1)

            loop_b(pool, step_b)


L_DEPTH, L_HEADS, L_DH, L_WIN = 2, 8, 64, 64
L_INNER = L_HEADS * L_DH
L_HID = int(D * 4 * 2 / 3)
HT = -(-L_HID // P)
EPS_NORM, EPS_LN = 1e-24, 1e-5
MASKED = -1e30
CHUNKS = B * C


def chunk_range(i, c, lag):
    return not isinstance(i, int) or 0 <= C * i + c - lag < CHUNKS


def chunk_of(i, c, lag):
    d = c - lag
    return i + d // C, d % C


def chunk_loop(eng, step, depth):
    for c in range(C):
        step(0, c)
    with eng.Fori(1, B) as i:
        for c in range(C):
            step(i, c)
    for c in range(depth):
        step(B, c)


def seq_loop(eng, step, depth):
    for n in range(depth):
        step(n)
    with eng.Fori(depth, B) as n:
        step(n)
    for n in range(B, B + depth):
        step(n)


def local_tables():
    f = np.float32
    half = np.arange(0, L_DH, 2, dtype=f)
    inv = (f(1.0) / f(10000.0) ** (half / f(L_DH))).astype(f)
    t = np.arange(T, dtype=f)
    fr = (t[:, None] * inv[None, :]).astype(f).astype(np.float64)
    fr = np.concatenate([fr, fr], -1)
    base = ((half + f(0.4 * L_DH)) / f(1.4 * L_DH)).astype(f).astype(np.float64)
    power = (t.astype(np.float64) - T // 2) / float(L_WIN // 2)
    s = base[None, :] ** power[:, None]
    s = np.concatenate([s, s], -1)
    sign = np.concatenate([-np.ones(L_DH // 2), np.ones(L_DH // 2)])
    tab = np.stack([8.0 * np.cos(fr) * s, 8.0 * np.sin(fr) * s * sign, np.cos(fr) / s, np.sin(fr) / s * sign], 1)
    tab = tab.reshape(C, P, 4, L_DH).transpose(1, 0, 2, 3).astype(f)
    i, j = np.arange(P)[:, None], np.arange(P + L_WIN)[None, :] - L_WIN
    band = np.where((i < j) | (i > j + L_WIN), f(MASKED), f(0)).astype(f)
    return np.ascontiguousarray(tab), band


def l1_local(nc, ctx, g, w):
    def sb(name, shape):
        return ctx.enter_context(nc.sbuf_tensor("l1_" + name, shape, F32))

    def sem(name):
        return phase_semaphore(nc, g, "l1_" + name)

    xw, ident, bank = g.xw, g.ident, g.bank
    w_qkv = sb("w_qkv", [P, 3, L_INNER])
    w_o = sb("w_o", [P, C, D])
    w_1 = sb("w_1", [P, 2 * L_HID])
    w_2 = sb("w_2", [P, HT, D])
    tab0 = sb("tab0", [P, C, 4, L_DH])
    tab = sb("tab", [P, C, 4, L_DH])
    band = sb("band", [P, P + L_WIN])
    qks = sb("qks", [P, 2, L_DH])
    NR = 6 + 3
    rows = sb("rows", [NR * L_DEPTH, P])
    cols = sb("cols", [P, L_DEPTH, NR])
    hs = sb("hs", [P, 2, P])
    sq = sb("sq", [P, 2, L_INNER])
    ra = sb("ra", [P, 2, L_INNER])
    rb = sb("rb", [P, 2, L_INNER])
    ss = sb("ss", [P, 16])
    rs = sb("rs", [P, 16])
    mhalf = sb("mhalf", [P, 16])
    qn = sb("qn", [P, 2, L_INNER])
    qT = sb("qT", [P, 4, P])
    kT = sb("kT", [P, 4, L_WIN + T])
    vt = sb("vt", [P, C, L_INNER])
    sm = sb("sm", [P, L_HEADS, P + L_WIN])
    mx = sb("mx", [P, L_HEADS])
    nmx = sb("nmx", [P, L_HEADS])
    psum = sb("psum", [P, 2, L_HEADS])
    rsum = sb("rsum", [P, L_HEADS])
    pb = sb("pb", [P, 2, L_HEADS, 2 * P])
    pt = sb("pt", [P, 4, 4, P])
    on = sb("on", [P, L_INNER])
    oT = sb("oT", [P, 4, P])
    y = sb("y", [P, T])
    st = sb("st", [P, C, 6])
    mv = sb("mv", [P, C, 2])
    ve = sb("ve", [P, C])
    rstd = sb("rstd", [P, C])
    xn = sb("xn", [P, C, D])
    hn = sb("hn", [P, T])
    gl = sb("gl", [P, HT, T])
    hm = sb("hm", [P, HT, T])

    cst_in = sem("cst_in")
    wa_in = sem("wa_in")
    wb_in = sem("wb_in")
    sc_in = sem("sc_in")
    rows_z = sem("rows_z")
    rows_in = sem("rows_in")
    rows_T = sem("rows_T")
    cols_done = sem("cols_done")
    tabs = sem("tabs")
    zero_done = sem("zero_done")
    hs_done = sem("hs_done")
    q_mm = sem("q_mm")
    k_mm = sem("k_mm")
    v_mm = sem("v_mm")
    sqq_done = sem("sqq_done")
    sq_done = sem("sq_done")
    ab_done = sem("ab_done")
    ss_done = sem("ss_done")
    sm_done = sem("sm_done")
    cl_done = sem("cl_done")
    rs_done = sem("rs_done")
    qn_done = sem("qn_done")
    tq_mm = sem("tq_mm")
    tq_ev = sem("tq_ev")
    tk_mm = sem("tk_mm")
    tk_ev = sem("tk_ev")
    v_ev = sem("v_ev")
    slo_mm = sem("slo_mm")
    shi_mm = sem("shi_mm")
    mlo_done = sem("mlo_done")
    mhi_done = sem("mhi_done")
    n_done = sem("n_done")
    nlo_done = sem("nlo_done")
    elo_done = sem("elo_done")
    ehi_done = sem("ehi_done")
    pt_mm = sem("pt_mm")
    pt_ev = sem("pt_ev")
    pv_mm = sem("pv_mm")
    rc_done = sem("rc_done")
    on_done = sem("on_done")
    ot_mm = sem("ot_mm")
    ot_ev = sem("ot_ev")
    wo_mm = sem("wo_mm")
    res_done = sem("res_done")
    y_done = sem("y_done")
    t_mm = sem("t_mm")
    bn_done = sem("bn_done")
    mv_done = sem("mv_done")
    ve_done = sem("ve_done")
    rstd_done = sem("rstd_done")
    xn_done = sem("xn_done")
    u_mm = sem("u_mm")
    hn_done = sem("hn_done")
    g_mm = sem("g_mm")
    a_mm = sem("a_mm")
    gl_done = sem("gl_done")
    hm_done = sem("hm_done")
    f2_mm = sem("f2_mm")
    x_done = sem("x_done")
    Q, K, O, MIX, S0, R0 = 0, 1, 2, 3, 4, 6

    def widths(k):
        return min(P, L_HID - k * P)

    block = ctx.enter_context(nc.Block())

    def heads_of(half, r):
        return [4 * half + r, 4 * half + 2 + r]

    @block.sync
    def _(sp):
        sp.dma_start(tab0[:, :, :, :], w["tab"]).then_inc(cst_in, 16)
        sp.dma_start(band[:, :], w["band"]).then_inc(cst_in, 16)
        sp.wait_ge(rows_z, 1)
        for l in range(L_DEPTH):
            r = l * NR
            for k in range(HT):
                sp.dma_start(rows[r + k:r + k + 1, 0:widths(k)], w["b1"][l:l + 1, k * P:k * P + widths(k)]).then_inc(rows_in, 16)
                sp.dma_start(rows[r + 3 + k:r + 4 + k, 0:widths(k)],
                             w["b1"][l:l + 1, L_HID + k * P:L_HID + k * P + widths(k)]).then_inc(rows_in, 16)
            for k, name in enumerate(["b2", "ln_g", "ln_b"]):
                sp.dma_start(rows[r + 6 + k:r + 7 + k, :], w[name][l:l + 1, :]).then_inc(rows_in, 16)

        def load(l):
            sp.dma_start(w_qkv[:, :, :], w["wqkv"][bass.ds(l, 1), :, :].rearrange("l p (t n) -> p (l t) n", t=3)).then_inc(wa_in, 16)
            sp.dma_start(w_o[:, :, :], w["wo"][bass.ds(l, 1), :, :].rearrange("l (k p) n -> p (l k) n", p=P)).then_inc(wa_in, 16)
            sp.dma_start(qks[:, 0, :], w["q_scale"][bass.ds(l, 1), :].partition_broadcast(P)).then_inc(sc_in, 16)
            sp.dma_start(qks[:, 1, :], w["k_scale"][bass.ds(l, 1), :].partition_broadcast(P)).then_inc(sc_in, 16)

        def load_ff(l):
            sp.dma_start(w_1[:, :], w["w1"][bass.ds(l, 1), :, :].rearrange("l p n -> (l p) n")).then_inc(wb_in, 16)
            sp.dma_start(w_2[:, 0:2, :], w["w2"][bass.ds(l, 1), 0:2 * P, :].rearrange("l (k p) n -> p (l k) n", p=P)).then_inc(wb_in, 16)
            sp.dma_start(w_2[0:widths(2), 2, :], w["w2"][bass.ds(l, 1), 2 * P:L_HID, :].rearrange("l p n -> (l p) n")).then_inc(wb_in, 16)
        load(0)
        load_ff(0)
        sp.wait_ge(res_done, CHUNKS + START)
        load(1)
        sp.wait_ge(f2_mm, B)
        load_ff(1)

    @block.tensor
    def _(pe):
        pe.wait_ge(rows_in, 16 * NR * L_DEPTH)
        pe.transpose(bank[:, 7, 0:NR * L_DEPTH], rows[:, :], ident[0:NR * L_DEPTH, 0:NR * L_DEPTH]).then_inc(rows_T, 1)
        pe.wait_ge(cols_done, 1)
        pe.wait_ge(zero_done, 1)
        with pe.Fori(0, L_DEPTH) as l:
            base = l * CHUNKS
            sbase = l * B

            def step_a(i, c):
                at = base + (i * C + c)

                def transposes(bk, src, blocks):
                    for j, b in blocks:
                        mm = pe.transpose(bank[:, bk, j * P:(j + 1) * P], src(b), ident[:, :])
                    return mm

                def scores(half):
                    cc = (c - 1) % C
                    lo = L_WIN if cc == 0 else 0
                    n = P + L_WIN - lo
                    for r in range(2):
                        for j, h in enumerate(heads_of(half, r)):
                            mm = pe.matmul(bank[:, S0 + r, j * 192:j * 192 + n], qT[64 * r:64 * r + 64, h // 2, :],
                                           kT[64 * r:64 * r + 64, h // 2, cc * P + lo:cc * P + lo + n], start=True, stop=True)
                    return mm

                def probs_T(gp):
                    cc = (c - 2) % C
                    blocks = [(2 * hh + o, (2 * gp + hh, o)) for hh in range(2) for o in ((1,) if cc == 0 else (0, 1))]
                    transposes(R0 + (1, 1, 0, 1)[gp], lambda b: pb[:, c % 2, b[0], b[1] * P:(b[1] + 1) * P], blocks).then_inc(pt_mm, 1)

                def values(gp):
                    cc = (c - 2) % C
                    pe.wait_ge(pt_ev, (at - 2) * 4 + (gp + 1 + 4 * START))
                    for hh in range(2):
                        h = 2 * gp + hh
                        o = bank[:, O, h * L_DH:(h + 1) * L_DH]
                        mm = pe.matmul(o, pt[:, gp, 2 * hh + 1, :], vt[:, cc, h * L_DH:(h + 1) * L_DH], start=True, stop=(cc == 0))
                        if cc:
                            mm = pe.matmul(o, pt[:, gp, 2 * hh, :], vt[:, cc - 1, h * L_DH:(h + 1) * L_DH], start=False, stop=True)
                    return mm

                one, two, three, now = (chunk_range(i, c, k) for k in (1, 2, 3, 0))
                if one:
                    pe.wait_ge(qn_done, at + START)
                    pe.wait_ge(v_ev, at + START)
                    transposes(MIX, lambda b: qn[:, 0, b * P:(b + 1) * P], [(b, b) for b in range(4)]).then_inc(tq_mm, 1)
                if now:
                    pe.wait_ge(hs_done, at + (1 + START))
                    pe.wait_ge(sq_done, at + START)
                    pe.wait_ge(ab_done, at + START)
                    pe.matmul(bank[:, Q, :], hs[:, c % 2, :], w_qkv[:, 0, :], start=True, stop=True).then_inc(q_mm, 1)
                if one:
                    pe.wait_ge(tq_ev, at + START)
                    transposes(MIX, lambda b: qn[:, 1, b * P:(b + 1) * P], [(b, b) for b in range(4)]).then_inc(tk_mm, 1)
                if now:
                    pe.matmul(bank[:, K, :], hs[:, c % 2, :], w_qkv[:, 1, :], start=True, stop=True).then_inc(k_mm, 1)
                    pe.wait_ge(tk_ev, at + START)
                    pe.matmul(bank[:, MIX, :], hs[:, c % 2, :], w_qkv[:, 2, :], start=True, stop=True).then_inc(v_mm, 1)
                if three:
                    pe.wait_ge(on_done, at + (START - 2))
                    pe.wait_ge(pt_ev, (at - 3) * 4 + (3 + 4 * START))
                    transposes(R0, lambda b: on[:, b * P:(b + 1) * P], [(b, b) for b in range(4)]).then_inc(ot_mm, 1)
                if two:
                    pe.wait_ge(ehi_done, at + (START - 1))
                    pe.wait_ge(pt_ev, (at - 3) * 4 + (4 + 4 * START))
                    probs_T(0)
                if one:
                    pe.wait_ge(tk_ev, at + START)
                    pe.wait_ge(mhi_done, at + (START - 1))
                    scores(0).then_inc(slo_mm, 1)
                if three:
                    pe.wait_ge(ot_ev, at + (START - 2))
                    for k in range(4):
                        mm = pe.matmul(bank[:, R0, 0:P], w_o[:, k, :], oT[:, k, :], start=(k == 0), stop=(k == 3))
                    mm.then_inc(wo_mm, 1)
                if two:
                    pe.wait_ge(pt_ev, (at - 2) * 4 + (1 + 4 * START))
                    probs_T(1)
                    pe.wait_ge(on_done, at + (START - 2))
                    values(0)
                    pe.wait_ge(res_done, at + (START - 2))
                    probs_T(2)
                    values(1)
                if one:
                    pe.wait_ge(mlo_done, at + START)
                    scores(1).then_inc(shi_mm, 1)
                if two:
                    probs_T(3)
                    values(2)
                    values(3).then_inc(pv_mm, 1)

            pe.wait_ge(wa_in, (l + 1) * 32)
            pe.wait_ge(x_done, sbase + START)
            chunk_loop(pe, step_a, 3)

            def step_b(n):
                at = sbase + n
                if in_range(n, 0):
                    pe.wait_ge(y_done, at + (1 + START))
                    pe.wait_ge(xn_done, at + START)
                    for c in range(C):
                        mm = pe.transpose(bank[:, 0, c * P:(c + 1) * P], y[:, c * P:(c + 1) * P], ident[:, :])
                    mm.then_inc(t_mm, 1)
                if in_range(n, 1):
                    pe.wait_ge(hn_done, at + START)
                    for k in range(HT):
                        m = widths(k)
                        b = 2 + 2 * (k % 2)
                        pe.wait_ge(hm_done, (at - 1) * HT + (k - 2 + 1 + HT * START))
                        pe.matmul(bank[0:m, b, :], w_1[:, L_HID + k * P:L_HID + k * P + m], hn[:, :],
                                  start=True, stop=True).then_inc(g_mm, 1)
                        pe.matmul(bank[0:m, b + 1, :], w_1[:, k * P:k * P + m], hn[:, :],
                                  start=True, stop=True).then_inc(a_mm, 1)
                if in_range(n, 0):
                    pe.wait_ge(xn_done, at + (1 + START))
                    pe.wait_ge(hn_done, at + START)
                    for c in range(C):
                        mm = pe.transpose(bank[:, 1, c * P:(c + 1) * P], xn[:, c, :], ident[:, :])
                    mm.then_inc(u_mm, 1)
                if in_range(n, 1):
                    pe.wait_ge(x_done, at + (START - 1))
                    for k in range(HT):
                        m = widths(k)
                        pe.wait_ge(hm_done, (at - 1) * HT + (k + 1 + HT * START))
                        mm = pe.matmul(bank[:, 6, :], w_2[0:m, k, :], hm[0:m, k, :], start=(k == 0), stop=(k == HT - 1))
                    mm.then_inc(f2_mm, 1)

            pe.wait_ge(wb_in, (l + 1) * 48)
            pe.wait_ge(res_done, base + (CHUNKS + START))
            pe.wait_ge(on_done, base + (CHUNKS + START))
            seq_loop(pe, step_b, 1)

    @block.scalar
    def _(act):
        for x in (sq_done, tq_ev, tk_ev, v_ev, elo_done, ehi_done, ot_ev, hn_done):
            act.sem_inc(x, START)
        act.sem_inc(pt_ev, 4 * START)
        act.sem_inc(gl_done, HT * START)
        act.wait_ge(cols_done, 1)
        with act.Fori(0, L_DEPTH) as l:
            base = l * CHUNKS
            sbase = l * B
            nc.scalar.preload_act_table_set("exp_and_others")

            def step_a(i, c):
                at = base + (i * C + c)
                one, two, three, now = (chunk_range(i, c, k) for k in (1, 2, 3, 0))

                def exps(half, wait, done):
                    cc = (c - 1) % C
                    lo = L_WIN if cc == 0 else 0
                    act.wait_ge(wait, at + START)
                    for h in range(4 * half, 4 * half + 4):
                        a = act.activation(pb[:, (c + 1) % 2, h, L_WIN + lo:], sm[:, h, lo:], ACT.Exp, bias=nmx[:, h:h + 1],
                                           accum_out=psum[:, (c + 1) % 2, h:h + 1])
                    a.then_inc(done, 1)

                def probs(gp):
                    cc = (c - 2) % C
                    act.wait_ge(pt_mm, (at - 2) * 4 + (gp + 1))
                    src = bank[:, R0 + (1, 1, 0, 1)[gp], :].rearrange("p (h o q) -> p h o q", h=2, o=2)
                    dst = pt[:, gp, :, :].rearrange("p (h o) q -> p h o q", h=2)
                    o = 1 if cc == 0 else 0
                    act.copy(dst[:, :, o:, :], src[:, :, o:, :]).then_inc(pt_ev, 1)

                if one:
                    act.wait_ge(tq_mm, at)
                    act.copy(qT[:, :, :], bank[:, MIX, :].rearrange("p (a b) -> p a b", a=4)).then_inc(tq_ev, 1)
                if now:
                    act.wait_ge(q_mm, at + 1)
                    act.wait_ge(ss_done, at + START)
                    act.activation(sq[:, 0, :], bank[:, Q, :], ACT.Square).then_inc(sqq_done, 1)
                if one:
                    cc = (c - 1) % C
                    act.wait_ge(tk_mm, at)
                    act.copy(kT[:, :, L_WIN + cc * P:L_WIN + (cc + 1) * P], bank[:, MIX, :].rearrange("p (a b) -> p a b", a=4)).then_inc(tk_ev, 1)
                if now:
                    act.wait_ge(k_mm, at + 1)
                    act.activation(sq[:, 1, :], bank[:, K, :], ACT.Square).then_inc(sq_done, 1)
                    act.wait_ge(v_mm, at + 1)
                    act.copy(vt[:, c, :], bank[:, MIX, :]).then_inc(v_ev, 1)
                if three:
                    act.wait_ge(ot_mm, at - 2)
                    act.copy(oT[:, :, :], bank[:, R0, :].rearrange("p (a b) -> p a b", a=4)).then_inc(ot_ev, 1)
                if two:
                    probs(0)
                    probs(1)
                if one:
                    exps(0, nlo_done, elo_done)
                if two:
                    probs(2)
                    probs(3)
                if one:
                    exps(1, n_done, ehi_done)

            chunk_loop(act, step_a, 3)
            nc.scalar.preload_act_table_set("gelu_and_others")

            def step_b(n):
                at = sbase + n
                if in_range(n, 1):
                    for k in range(HT):
                        m = widths(k)
                        act.wait_ge(g_mm, (at - 1) * HT + (k + 1))
                        act.wait_ge(hm_done, (at - 2) * HT + (k + 1 + HT * START))
                        apart(act, g)
                        act.activation(gl[0:m, k, :], bank[0:m, 2 + 2 * (k % 2), :], ACT.Gelu, bias=cols[0:m, bass.ds(l, 1), 3 + k]).then_inc(gl_done, 1)
                if in_range(n, 0):
                    act.wait_ge(u_mm, at + 1)
                    act.wait_ge(a_mm, at * HT)
                    apart(act, g)
                    act.activation(hn[:, :], bank[:, 1, :], ACT.Identity, bias=cols[:, bass.ds(l, 1), 8], scale=cols[:, bass.ds(l, 1), 7]).then_inc(hn_done, 1)

            seq_loop(act, step_b, 1)

    @block.vector
    def _(dve):
        dve.memset(mhalf[:, :], -0.5)
        dve.memset(rows[:, :], 0.0).then_inc(rows_z, 1)
        dve.memset(kT[:, :, 0:L_WIN], 0.0)
        dve.memset(y[:, :], 0.0)
        dve.memset(pb[:, :, :, :], 0.0).then_inc(zero_done, 1)
        dve.wait_ge(rows_T, 1)
        dve.tensor_copy(cols[:, :, :], bank[:, 7, 0:NR * L_DEPTH].rearrange("p (l r) -> p l r", l=L_DEPTH)).then_inc(cols_done, 1)
        for x in (ab_done, ss_done, qn_done, mlo_done, mhi_done, n_done, nlo_done, on_done, res_done, xn_done, x_done, hs_done, y_done):
            dve.sem_inc(x, START)
        dve.sem_inc(hm_done, HT * START)
        with dve.Fori(0, L_DEPTH) as l:
            base = l * CHUNKS
            sbase = l * B

            def step_a(i, c):
                at = base + (i * C + c)
                one, two, three, now = (chunk_range(i, c, k) for k in (1, 2, 3, 0))

                def rotate(bk, qk):
                    x = bank[:, bk, :].rearrange("p (h d) -> p h d", h=L_HEADS)
                    x4 = bank[:, bk, :].rearrange("p (h t d) -> p h t d", h=L_HEADS, t=2)
                    cs = tab[:, c, 2 * qk, :].unsqueeze(1).broadcast_to([P, L_HEADS, L_DH])
                    sn = tab[:, c, 2 * qk + 1, :].unsqueeze(1).broadcast_to([P, L_HEADS, L_DH])
                    dve.tensor_tensor(ra[:, qk, :].rearrange("p (h d) -> p h d", h=L_HEADS), x, cs, ALU.mult)
                    return dve.tensor_tensor(rb[:, qk, :].rearrange("p (h t d) -> p h t d", h=L_HEADS, t=2), x4[:, :, ::-1, :],
                                             sn.rearrange("p h (t d) -> p h t d", t=2), ALU.mult)

                def masked_max(half, mm, freed, m_done, neg_done):
                    cc = (c - 1) % C
                    lo = L_WIN if cc == 0 else 0
                    n = P + L_WIN - lo
                    dve.wait_ge(mm, at)
                    dve.wait_ge(freed, at + (START - 1))
                    apart(dve, g)
                    for r in range(2):
                        for j, h in enumerate(heads_of(half, r)):
                            x = dve.tensor_tensor_reduce(sm[:, h, lo:], bank[:, S0 + r, j * 192:j * 192 + n], band[:, lo:], 1.0, MASKED * 2,
                                                         ALU.add, ALU.max, mx[:, h:h + 1])
                    x.then_inc(m_done, 1)
                    dve.wait_ge(m_done, at + START)
                    dve.tensor_scalar(nmx[:, 4 * half:4 * half + 4], mx[:, 4 * half:4 * half + 4], -1.0, None, ALU.mult).then_inc(neg_done, 1)

                if now:
                    n0, t0, p = chunk_of(i, c, 0)[0], c * P, c % 2
                    dve.wait_ge(v_ev, at + (START - 1))
                    dve.tensor_copy(hs[0:64, p, :], xw[0:64, n0, t0:t0 + P])
                    if c == 0:
                        dve.memset(hs[64:P, p, 0:1], 0.0)
                        dve.tensor_copy(hs[64:P, p, 1:P], xw[64:P, n0, 0:P - 1]).then_inc(hs_done, 1)
                    else:
                        dve.tensor_copy(hs[64:P, p, :], xw[64:P, n0, t0 - 1:t0 + P - 1]).then_inc(hs_done, 1)
                    dve.wait_ge(sqq_done, at + 1)
                    dve.wait_ge(sm_done, at + START)
                    rotate(Q, 0)
                    dve.wait_ge(sq_done, at + (1 + START))
                    rotate(K, 1).then_inc(ab_done, 1)
                    dve.wait_ge(rs_done, at + START)
                    dve.tensor_reduce(ss[:, :], sq[:, :, :].rearrange("p t (h d) -> p (t h) d", d=L_DH), AX.X, ALU.add).then_inc(ss_done, 1)
                if one:
                    masked_max(0, slo_mm, elo_done, mlo_done, nlo_done)
                if three:
                    n3, c3 = chunk_of(i, c, 3)
                    dve.wait_ge(wo_mm, at - 2)
                    x = xw[:, n3, c3 * P:(c3 + 1) * P]
                    dve.tensor_tensor(x, bank[:, R0, 0:P], x, ALU.add).then_inc(res_done, 1)
                if one:
                    masked_max(1, shi_mm, ehi_done, mhi_done, n_done)
                if now:
                    dve.wait_ge(rs_done, at + (1 + START))
                    dve.wait_ge(sm_done, at + (1 + START))
                    dve.wait_ge(tk_mm, at)
                    dve.tensor_tensor(qn[:, :, :].rearrange("p t (h d) -> p (t h) d", d=L_DH), ra[:, :, :].rearrange("p t (h d) -> p (t h) d", d=L_DH),
                                      rs[:, :].unsqueeze(2).broadcast_to([P, 16, L_DH]), ALU.mult).then_inc(qn_done, 1)
                if two:
                    dve.wait_ge(ehi_done, at + (START - 1))
                    dve.reciprocal(rsum[:, :], psum[:, c % 2, :]).then_inc(rc_done, 1)
                    dve.wait_ge(rc_done, at - 1)
                    dve.wait_ge(pv_mm, at - 1)
                    dve.wait_ge(ot_mm, at - 2)
                    dve.tensor_tensor(on[:, :].rearrange("p (h d) -> p h d", d=L_DH), bank[:, O, :].rearrange("p (h d) -> p h d", d=L_DH),
                                      rsum[:, :].unsqueeze(2).broadcast_to([P, L_HEADS, L_DH]), ALU.mult).then_inc(on_done, 1)

            dve.wait_ge(tabs, l + 1)
            chunk_loop(dve, step_a, 3)

            def norm(n, at):
                dve.wait_ge(rstd_done, at + 1)
                dve.wait_ge(u_mm, at)
                for c in range(C):
                    last = dve.tensor_scalar(xn[:, c, :], bank[:, 0, c * P:(c + 1) * P], mv[:, c, 0:1], rstd[:, c:c + 1], ALU.subtract, ALU.mult)
                last.then_inc(xn_done, 1)

            def step_b(n):
                at = sbase + n
                if in_range(n, 0):
                    dve.wait_ge(t_mm, at)
                    dve.tensor_copy(y[0:64, :], xw[0:64, n, :])
                    dve.tensor_copy(y[64:P, 1:T], xw[64:P, n, 0:T - 1]).then_inc(y_done, 1)
                    dve.wait_ge(t_mm, at + 1)
                    layer_stats(dve, g, bank[:, 0, :].rearrange("p (c d) -> p c d", c=C), st, mv, bn_done, at + 1, mv_done)
                if in_range(n, 1):
                    for k in range(HT):
                        m = widths(k)
                        if k == 1 and in_range(n, 0):
                            norm(n, at)
                        dve.wait_ge(a_mm, (at - 1) * HT + (k + 1))
                        dve.wait_ge(gl_done, (at - 1) * HT + (k + 1 + HT * START))
                        dve.wait_ge(f2_mm, at - 1)
                        dve.scalar_tensor_tensor(out=hm[0:m, k, :], in0=bank[0:m, 3 + 2 * (k % 2), :], scalar=cols[0:m, bass.ds(l, 1), k],
                                                 in1=gl[0:m, k, :], op0=ALU.add, op1=ALU.mult).then_inc(hm_done, 1)
                    dve.wait_ge(f2_mm, at)
                    x = xw[:, n - 1, :]
                    dve.scalar_tensor_tensor(out=x, in0=bank[:, 6, :], scalar=cols[:, bass.ds(l, 1), 6], in1=x, op0=ALU.add, op1=ALU.add).then_inc(x_done, 1)
                elif in_range(n, 0):
                    norm(n, at)

            seq_loop(dve, step_b, 1)

    @block.gpsimd
    def _(pool):
        for x in (sm_done, rs_done):
            pool.sem_inc(x, START)
        pool.wait_ge(cst_in, 32)
        with pool.Fori(0, L_DEPTH) as l:
            base = l * CHUNKS
            sbase = l * B

            def step_a(i, c):
                at = base + (i * C + c)
                if chunk_range(i, c, 0):
                    pool.wait_ge(ab_done, at + (1 + START))
                    pool.wait_ge(qn_done, at + START)
                    pool.tensor_tensor(ra[:, :, :], ra[:, :, :], rb[:, :, :], ALU.add).then_inc(sm_done, 1)
                    pool.wait_ge(ss_done, at + (1 + START))
                    apart(pool, g)
                    pool.tensor_scalar(ss[:, :], ss[:, :], EPS_NORM, None, ALU.max).then_inc(cl_done, 1)
                    pool.wait_ge(cl_done, at + 1)
                    pool.tensor_tensor(rs[:, :], ss[:, :], mhalf[:, :], ALU.pow).then_inc(rs_done, 1)

            pool.wait_ge(sc_in, (l + 1) * 32)
            pool.wait_ge(qn_done, base + START)
            for qk in range(2):
                sc = qks[:, qk, :]
                swapped = sc.rearrange("p (t d) -> p t d", t=2)[:, ::-1, :].unsqueeze(1).broadcast_to([P, C, 2, L_DH // 2])
                pool.tensor_tensor(tab[:, :, 2 * qk, :], tab0[:, :, 2 * qk, :], sc.unsqueeze(1).broadcast_to([P, C, L_DH]), ALU.mult)
                last = pool.tensor_tensor(tab[:, :, 2 * qk + 1, :].rearrange("p c (t d) -> p c t d", t=2),
                                          tab0[:, :, 2 * qk + 1, :].rearrange("p c (t d) -> p c t d", t=2), swapped, ALU.mult)
            last.then_inc(tabs, 1)
            pool.wait_ge(x_done, sbase + START)
            chunk_loop(pool, step_a, 0)

            def step_b(n):
                at = sbase + n
                if in_range(n, 0):
                    pool.wait_ge(mv_done, at + 1)
                    apart(pool, g)
                    pool.tensor_scalar(ve[:, :], mv[:, :, 1], EPS_LN, None, ALU.add).then_inc(ve_done, 1)
                    pool.wait_ge(ve_done, at + 1)
                    pool.tensor_tensor(rstd[:, :], ve[:, :], mhalf[:, 0:C], ALU.pow).then_inc(rstd_done, 1)

            seq_loop(pool, step_b, 1)


R_HEADS = 8
R_DV = 2 * D // R_HEADS
R_DK = D // R_HEADS
V2 = 2 * D
EPS_GN = 1e-5


def retention_tables():
    f = np.float32
    half = D // 2
    sv = ((np.arange(0, D, 2, dtype=f) + f(0.4 * D)) / f(1.4 * D)).astype(f).astype(np.float64)
    pos = np.arange(T, dtype=f)
    scale = sv[None, :] ** (pos.astype(np.float64)[:, None] / 512.0)
    inv = (f(1.0) / f(10000.0) ** (np.arange(half, dtype=f) / f(half))).astype(f)
    ang = (pos[:, None] * inv[None, :]).astype(f).astype(np.float64)
    sin, cos = np.sin(ang), np.cos(ang)
    two = lambda a: np.repeat(a, 2, axis=-1)
    sign = np.tile([-1.0, 1.0], half)
    lin = np.linspace(np.log(1.0 / 32.0), np.log(1.0 / 512.0), R_HEADS).astype(f)
    gamma = (f(1.0) - np.exp(lin)).astype(f)
    ld = np.log(gamma).astype(f).astype(np.float64)
    t = np.arange(T, dtype=np.float64)
    norm = np.sqrt(np.cumsum(np.exp(ld[:, None] * t[None, :]), axis=1))
    fq = np.repeat(np.exp(ld[:, None] * t) / norm * R_DK ** -0.5, R_DK, axis=0).T
    fk = np.repeat(np.exp(-ld[:, None] * t), R_DK, axis=0).T
    tab = np.stack([two(cos * scale) * fq, two(sin * scale) * sign * fq, two(cos / scale) * fk, two(sin / scale) * sign * fk], 0)
    tab = tab.reshape(4, C, P, D).transpose(3, 1, 0, 2).astype(f)
    tri = (np.arange(P)[:, None] <= np.arange(P)[None, :]).astype(f)
    feat = np.arange(P)[:, None] // R_DK
    diag = (feat == np.arange(V2)[None, :] // R_DV).astype(f)
    heads = (feat == np.arange(R_HEADS)[None, :]).astype(f)
    return np.ascontiguousarray(tab), tri, diag, heads


def l0_retention(nc, ctx, g, w):
    def sb(name, shape):
        return ctx.enter_context(nc.sbuf_tensor("l0_" + name, shape, F32))

    def sem(name):
        return phase_semaphore(nc, g, "l0_" + name)

    x_all, xw, ident, bank = g.x, g.xw, g.ident, g.bank
    w_qkv = sb("w_qkv", [P, 4 * D])
    w_sw = sb("w_sw", [P, 2, D])
    w_vc = sb("w_vc", [P, V2])
    w_g = sb("w_g", [P, V2])
    w_p = sb("w_p", [P, 2, D])
    bv = sb("bv", [P, V2])
    bvc = sb("bvc", [P, V2])
    vmean = sb("vmean", [P, 2, R_HEADS])
    tab = sb("tab", [P, C, 4, P])
    tri = sb("tri", [P, P])
    diag = sb("diag", [P, V2])
    heads = sb("heads", [P, R_HEADS])
    NR = 7
    rows = sb("rows", [NR, P])
    cols = sb("cols", [P, NR])
    xt = sb("xt", [P, C, D])
    xs = sb("xs", [P, 2, P])
    r4 = sb("r4", [P, 4, P])
    qk = sb("qk", [P, 2, 2, P])
    q8 = sb("q8", [P, R_HEADS, P])
    sm = sb("sm", [P, R_HEADS, P])
    vt = sb("vt", [P, 2, V2])
    kt = sb("kt", [P, P])
    state = sb("state", [P, V2])
    sg = sb("sg", [P, C, 2, P])
    so = sb("so", [P, V2])
    ss = sb("ss", [P, R_HEADS])
    sv = sb("sv", [P, R_HEADS])
    rs = sb("rs", [P, R_HEADS])
    mhalf = sb("mhalf", [P, R_HEADS])
    on = sb("on", [P, V2])
    gated = sb("gated", [P, 2, P])

    w_in = sem("w_in")
    cst_in = sem("cst_in")
    rows_in = sem("rows_in")
    rows_T = sem("rows_T")
    cols_done = sem("cols_done")
    wc = sem("wc")
    mean_done = sem("mean_done")
    mh_done = sem("mh_done")
    x_in0 = sem("x_in0")
    x_in1 = sem("x_in1")
    x_in2 = sem("x_in2")
    x_in3 = sem("x_in3")
    xt_mm = sem("xt_mm")
    xs_done = sem("xs_done")
    xst_done = sem("xst_done")
    qk_mm = sem("qk_mm")
    r4_done = sem("r4_done")
    qk_done = sem("qk_done")
    q8_done = sem("q8_done")
    v_mm = sem("v_mm")
    v_done = sem("v_done")
    g_mm = sem("g_mm")
    sg_done = sem("sg_done")
    slo_mm = sem("slo_mm")
    shi_mm = sem("shi_mm")
    mlo_done = sem("mlo_done")
    mhi_done = sem("mhi_done")
    o_mm = sem("o_mm")
    kt_mm = sem("kt_mm")
    kt_done = sem("kt_done")
    kv_mm = sem("kv_mm")
    state_done = sem("state_done")
    sq_done = sem("sq_done")
    ss_done = sem("ss_done")
    sv_done = sem("sv_done")
    rs_done = sem("rs_done")
    on_done = sem("on_done")
    ont_mm = sem("ont_mm")
    gated_done = sem("gated_done")
    p_mm = sem("p_mm")
    p_done = sem("p_done")
    x_in = [x_in0, x_in1, x_in2, x_in3]
    X, QK, V, G, S, O, KV = 0, 1, 2, 3, 4, 6, 7
    block = ctx.enter_context(nc.Block())

    def lag_range(i, c):
        return [chunk_range(i, c, k) for k in range(3)]

    @block.sync
    def _(sp):
        for r, (a, b) in enumerate([(0, D), (D, 2 * D)]):
            sp.dma_start(rows[r:r + 1, :], w["b_qkv"][a:b].unsqueeze(0)).then_inc(rows_in, 16)
            sp.dma_start(rows[2 + r:3 + r, 0::2], w["b_qkv"][a + 1:b:2].unsqueeze(0), allow_slow_non_contiguous=True).then_inc(rows_in, 16)
            sp.dma_start(rows[2 + r:3 + r, 1::2], w["b_qkv"][a:b:2].unsqueeze(0), allow_slow_non_contiguous=True).then_inc(rows_in, 16)
            sp.dma_start(rows[4 + r:5 + r, :], w["b_g"][a:b].unsqueeze(0)).then_inc(rows_in, 16)
        sp.dma_start(rows[6:7, :], w["b_p"].unsqueeze(0)).then_inc(rows_in, 16)
        sp.dma_start(w_qkv[:, :], w["w_qkv"]).then_inc(w_in, 16)
        sp.dma_start(w_g[:, :], w["w_g"]).then_inc(w_in, 16)
        sp.dma_start(w_p[:, :, :], w["w_p"].rearrange("(k p) n -> p k n", p=P)).then_inc(w_in, 16)
        sp.dma_start(bv[:, :], w["b_qkv"][2 * D:4 * D].unsqueeze(0).partition_broadcast(P)).then_inc(w_in, 16)
        for dst, name in ((tab, "rtab"), (tri, "tri"), (diag, "diag"), (heads, "heads")):
            sp.dma_start(dst[:], w[name]).then_inc(cst_in, 16)

        def load(n, c):
            sp.dma_start(xt[:, c, :], w["x"][bass.ds(n, 1), c * P:(c + 1) * P, :].rearrange("b p d -> p (b d)")).then_inc(x_in[c], 16)
        for c in range(C):
            load(0, c)
        with sp.Fori(1, B) as i:
            for c in range(C):
                sp.wait_ge(xt_mm, i * C + (c - 3))
                load(i, c)

    @block.tensor
    def _(pe):
        pe.wait_ge(rows_in, 16 * 9)
        pe.transpose(bank[:, 7, 0:NR], rows[:, :], ident[0:NR, 0:NR]).then_inc(rows_T, 1)
        pe.wait_ge(cols_done, 1)
        pe.wait_ge(wc, 4)
        pe.wait_ge(w_in, 64)

        def step(i, c):
            at = i * C + c
            now, one, two = lag_range(i, c)
            par, was = c % 2, (c - 1) % 2
            c1 = (c - 1) % C
            if now:
                pe.wait_ge(x_in[c], i * 16 + 16)
                pe.wait_ge(p_done, at + (START - 2))
                pe.transpose(bank[:, X, 0:P], xt[:, c, :], ident[:, :]).then_inc(xt_mm, 1)
            if one:
                pe.wait_ge(q8_done, at + START)
                pe.wait_ge(mlo_done, at + (START - 1))
                pe.matmul(bank[:, S, :], qk[:, was, 1, :], q8[:, 0:4, :], start=True, stop=True).then_inc(slo_mm, 1)
                pe.wait_ge(mhi_done, at + (START - 1))
                pe.matmul(bank[:, S + 1, :], qk[:, was, 1, :], q8[:, 4:8, :], start=True, stop=True).then_inc(shi_mm, 1)
            if now:
                pe.wait_ge(xs_done, at + (1 + START))
                pe.wait_ge(r4_done, at + START)
                for j, lhs in enumerate([w_qkv[:, 0:D], w_sw[:, 0, :], w_qkv[:, D:2 * D], w_sw[:, 1, :]]):
                    mm = pe.matmul(bank[:, QK, j * P:(j + 1) * P], lhs, xs[:, par, :], start=True, stop=True)
                mm.then_inc(qk_mm, 1)
                pe.wait_ge(gated_done, at + (START - 2))
                pe.matmul(bank[:, V, 0:V2], xs[:, par, :], w_vc[:, :], start=True, stop=True).then_inc(v_mm, 1)
                pe.wait_ge(sg_done, at + START)
                for j in range(2):
                    mm = pe.matmul(bank[:, G, j * P:(j + 1) * P], w_g[:, j * P:(j + 1) * P], xs[:, par, :], start=True, stop=True)
                mm.then_inc(g_mm, 1)
            if one:
                pe.wait_ge(on_done, at + (START - 1))
                if c1:
                    pe.wait_ge(state_done, at + (START - 1))
                    pe.matmul(bank[:, O, 0:V2], qk[:, was, 0, :], state[:, :], start=True, stop=False, skip_group_check=True)
                for h in range(R_HEADS):
                    if h % 4 == 0:
                        pe.wait_ge((mlo_done, mhi_done)[h // 4], at + START)
                    mm = pe.matmul(bank[:, O, h * R_DV:(h + 1) * R_DV], sm[:, h, :], vt[:, was, h * R_DV:(h + 1) * R_DV],
                                   start=(c1 == 0), stop=True, skip_group_check=True)
                mm.then_inc(o_mm, 1)
                if now:
                    pe.wait_ge(xs_done, at + (START + 1))
                else:
                    pe.wait_ge(p_done, at + (START - 2))
                pe.transpose(bank[:, X, 0:P], qk[:, was, 1, :], ident[:, :]).then_inc(kt_mm, 1)
            if two:
                pe.wait_ge(on_done, at + (START - 1))
                pe.wait_ge(v_done, at + (START + 1) if now else at + (START if one else START - 1))
                for j in range(2):
                    mm = pe.transpose(bank[:, V, j * P:(j + 1) * P], on[:, j * P:(j + 1) * P], ident[:, :])
                mm.then_inc(ont_mm, 1)
            if one:
                pe.wait_ge(kt_done, at + START)
                pe.wait_ge(state_done, at + (START - 1))
                pe.matmul(bank[:, KV, 0:V2], kt[:, :], vt[:, was, :], start=(c1 == 0), stop=True, skip_group_check=True).then_inc(kv_mm, 1)
            if two:
                pe.wait_ge(gated_done, at + (START - 1))
                if one:
                    pe.wait_ge(kt_done, at + START)
                else:
                    pe.wait_ge(p_done, at + (START - 2))
                for j in range(2):
                    mm = pe.matmul(bank[:, X, 0:P], w_p[:, j, :], gated[:, j, :], start=(j == 0), stop=(j == 1))
                mm.then_inc(p_mm, 1)

        chunk_loop(pe, step, 2)

    @block.scalar
    def _(act):
        for x in (xs_done, sg_done, kt_done, p_done):
            act.sem_inc(x, START)
        nc.scalar.preload_act_table_set("silu_and_others")
        act.wait_ge(cols_done, 1)

        def step(i, c):
            at = i * C + c
            now, one, two = lag_range(i, c)
            par = c % 2
            if now:
                act.wait_ge(xt_mm, at + 1)
                act.wait_ge(xst_done, at + (START - 1))
                if not (isinstance(i, int) and at < 2):
                    act.wait_ge(g_mm, at - 1)
                act.copy(xs[:, par, :], bank[:, X, 0:P]).then_inc(xs_done, 1)
                act.wait_ge(g_mm, at + 1)
                act.wait_ge(gated_done, at + (START - 3))
                for j in range(2):
                    a = act.activation(sg[:, c, j, :], bank[:, G, j * P:(j + 1) * P], ACT.Silu, bias=cols[:, 4 + j:5 + j])
                a.then_inc(sg_done, 1)
            if one:
                act.wait_ge(kt_mm, at)
                act.wait_ge(kv_mm, at - 1)
                act.copy(kt[:, :], bank[:, X, 0:P]).then_inc(kt_done, 1)
                act.wait_ge(o_mm, at)
                act.wait_ge(ss_done, at + (START - 1))
                act.activation(so[:, :], bank[:, O, 0:V2], ACT.Square).then_inc(sq_done, 1)
            if two:
                n2, c2 = chunk_of(i, c, 2)
                act.wait_ge(p_mm, at - 1)
                apart(act, g)
                act.activation(xw[:, n2, c2 * P:(c2 + 1) * P], bank[:, X, 0:P], ACT.Identity, bias=cols[:, 6:7]).then_inc(p_done, 1)

        chunk_loop(act, step, 2)

    @block.vector
    def _(dve):
        for x in (xst_done, r4_done, qk_done, q8_done, v_done, mlo_done, mhi_done, state_done, ss_done, on_done, gated_done):
            dve.sem_inc(x, START)
        dve.memset(mhalf[:, :], -0.5).then_inc(mh_done, 1)
        dve.wait_ge(rows_T, 1)
        dve.tensor_copy(cols[:, :], bank[:, 7, 0:NR]).then_inc(cols_done, 1)
        dve.wait_ge(w_in, 64)
        for j in range(2):
            src = w_qkv[:, j * D:(j + 1) * D].rearrange("p (a t) -> p a t", t=2)
            dve.tensor_copy(w_sw[:, j, :].rearrange("p (a t) -> p a t", t=2), src[:, :, ::-1]).then_inc(wc, 1)
        for j, (src, dst) in enumerate([(w_qkv[:, 2 * D:4 * D], w_vc), (bv[:, :], bvc)]):
            grp = src.rearrange("p (h d) -> p h d", d=R_DV)
            dve.tensor_reduce(vmean[:, j, :], grp, AX.X, ALU.add).then_inc(mean_done, 1)
            dve.wait_ge(mean_done, 2 * j + 1)
            dve.tensor_scalar(vmean[:, j, :], vmean[:, j, :], 1.0 / R_DV, None, ALU.mult).then_inc(mean_done, 1)
            dve.wait_ge(mean_done, 2 * j + 2)
            dve.tensor_tensor(dst[:, :].rearrange("p (h d) -> p h d", d=R_DV), grp,
                              vmean[:, j, :].unsqueeze(2).broadcast_to([P, R_HEADS, R_DV]), ALU.subtract).then_inc(wc, 1)
        dve.wait_ge(wc, 4)
        dve.wait_ge(cst_in, 64)

        def step(i, c):
            at = i * C + c
            now, one, two = lag_range(i, c)
            par, was = c % 2, (c - 1) % 2
            c1 = (c - 1) % C
            if two:
                dve.wait_ge(rs_done, at - 1)
                dve.wait_ge(ont_mm, at - 2)
                dve.tensor_tensor(on[:, :].rearrange("p (h d) -> p h d", d=R_DV), bank[:, O, 0:V2].rearrange("p (h d) -> p h d", d=R_DV),
                                  rs[:, :].unsqueeze(2).broadcast_to([P, R_HEADS, R_DV]), ALU.mult).then_inc(on_done, 1)
            if one:
                for half, (mm, done) in enumerate([(slo_mm, mlo_done), (shi_mm, mhi_done)]):
                    dve.wait_ge(mm, at)
                    if half == 0:
                        dve.wait_ge(o_mm, at - 1)
                    dve.tensor_tensor(sm[:, 4 * half:4 * half + 4, :], bank[:, S + half, :].rearrange("p (h q) -> p h q", h=4),
                                      tri[:, :].unsqueeze(1).broadcast_to([P, 4, P]), ALU.mult).then_inc(done, 1)
            if now:
                dve.wait_ge(qk_mm, at + 1)
                for j in range(4):
                    x = dve.scalar_tensor_tensor(out=r4[:, j, :], in0=bank[:, QK, j * P:(j + 1) * P], scalar=cols[:, (0, 2, 1, 3)[j]:(0, 2, 1, 3)[j] + 1],
                                                 in1=tab[:, c, j, :], op0=ALU.add, op1=ALU.mult)
                x.then_inc(r4_done, 1)
                dve.wait_ge(v_mm, at + 1)
                dve.tensor_tensor(vt[:, par, :], bank[:, V, 0:V2], bvc[:, :], ALU.add).then_inc(v_done, 1)
                dve.wait_ge(r4_done, at + (1 + START))
                dve.tensor_tensor(qk[:, par, :, :], r4[:, 0::2, :], r4[:, 1::2, :], ALU.add).then_inc(qk_done, 1)
                dve.wait_ge(xs_done, at + (1 + START))
                dve.tensor_copy(x_all[:, i, c * P:(c + 1) * P], xs[:, par, :]).then_inc(xst_done, 1)
                dve.wait_ge(qk_done, at + (1 + START))
                if one:
                    dve.wait_ge(shi_mm, at)
                dve.tensor_tensor(q8[:, :, :], qk[:, par, 0, :].unsqueeze(1).broadcast_to([P, R_HEADS, P]),
                                  heads[:, :].unsqueeze(2).broadcast_to([P, R_HEADS, P]), ALU.mult).then_inc(q8_done, 1)
            if two:
                dve.wait_ge(ont_mm, at - 1)
                dve.wait_ge(sg_done, at + (START - 1))
                dve.wait_ge(p_mm, at - 2)
                dve.tensor_tensor(gated[:, :, :], bank[:, V, 0:V2].rearrange("p (j q) -> p j q", j=2), sg[:, (c - 2) % C, :, :], ALU.mult).then_inc(gated_done, 1)
            if one:
                dve.wait_ge(kv_mm, at)
                dve.wait_ge(o_mm, at)
                dve.tensor_tensor(state[:, :], bank[:, KV, 0:V2], diag[:, :], ALU.mult).then_inc(state_done, 1)
                dve.wait_ge(sq_done, at)
                dve.wait_ge(sv_done, at - 1)
                dve.tensor_reduce(ss[:, :], so[:, :].rearrange("p (h d) -> p h d", d=R_DV), AX.X, ALU.add).then_inc(ss_done, 1)

        chunk_loop(dve, step, 2)

    @block.gpsimd
    def _(pool):
        pool.wait_ge(mh_done, 1)

        def step(i, c):
            at = i * C + c
            if chunk_range(i, c, 1):
                pool.wait_ge(ss_done, at + START)
                pool.wait_ge(on_done, at + (START - 1))
                apart(pool, g)
                pool.tensor_scalar(sv[:, :], ss[:, :], 1.0 / R_DV, EPS_GN, ALU.mult, ALU.add).then_inc(sv_done, 1)
                pool.wait_ge(sv_done, at)
                pool.tensor_tensor(rs[:, :], sv[:, :], mhalf[:, :], ALU.pow).then_inc(rs_done, 1)

        chunk_loop(pool, step, 2)


EPS_OUT = 1e-5
E_COUNT, E_FF = 8, 512
EF = E_FF // P
TILES = B * C
SLOTS = -(-(B * T + E_COUNT * (P - 1)) // (4 * P)) * 4
MOE_TABLES = ("before", "desc", "full", "slot")


def moe_tables():
    row = lambda a: np.ascontiguousarray(np.broadcast_to(np.asarray(a, np.float32), (P, len(a))))
    before = (np.arange(P)[:, None] < np.arange(P)[None, :]).astype(np.float32)
    return {"before": before, "desc": row(E_COUNT - np.arange(E_COUNT)), "full": row(P * np.arange(TILES)), "slot": row(np.arange(SLOTS))}


def pair_loop(eng, step, depth):
    for c in range(2):
        step(0, c)
    with eng.Fori(1, B // 2) as i:
        for c in range(2):
            step(i, c)
    for c in range(depth):
        step(B // 2, c)


def outer_norm(nc, ctx, g, tag, out=None):
    def sb(name, shape):
        return ctx.enter_context(nc.sbuf_tensor(tag + name, shape, F32))

    def sem(name):
        return phase_semaphore(nc, g, tag + name)

    x_all, xw, ident, bank = g.x, g.xw, g.ident, g.bank
    y = sb("y", [P, 2, T])
    st = sb("st", [P, 2, C, 6])
    mv = sb("mv", [P, 2, C, 2])
    ve = sb("ve", [P, C])
    mhalf = sb("mhalf", [P, C])
    rstd = sb("rstd", [P, 2, C])
    xn = sb("xn", [P, 2, C, D])
    mh_done = sem("mh_done")
    y_done = sem("y_done")
    y_mm = sem("y_mm")
    bn_done = sem("bn_done")
    mv_done = sem("mv_done")
    ve_done = sem("ve_done")
    rstd_done = sem("rstd_done")
    xn_done = sem("xn_done")
    back_mm = sem("back_mm")
    x_done = sem("x_done")
    xw_done = sem("xw_done")
    out0 = sem("out0")
    out1 = sem("out1")
    out_done = [out0, out1]
    Y, BACK = (0, 1), (2, 3)
    block = ctx.enter_context(nc.Block())

    def there(i, c, lag):
        return not isinstance(i, int) or 0 <= 2 * i + c - lag < B

    @block.tensor
    def _(pe):
        def step(i, c):
            n = 2 * i + c
            p, q = c % 2, (c - 1) % 2
            if there(i, c, 0):
                pe.wait_ge(y_done, n + 1)
                pe.wait_ge(xn_done, n + (START - 1))
                for k in range(C):
                    mm = pe.transpose(bank[:, Y[p], k * P:(k + 1) * P], y[:, p, k * P:(k + 1) * P], ident[:, :])
                mm.then_inc(y_mm, 1)
            if there(i, c, 1) and out is None:
                pe.wait_ge(xn_done, n + START)
                pe.wait_ge(x_done, n + (START - 2))
                pe.wait_ge(xw_done, n + (START - 2))
                for k in range(C):
                    mm = pe.transpose(bank[:, BACK[q], k * P:(k + 1) * P], xn[:, q, k, :], ident[:, :])
                mm.then_inc(back_mm, 1)

        pair_loop(pe, step, 1)

    @block.gpsimd
    def _(pool):
        pool.wait_ge(mh_done, 1)

        def step(i, c):
            n = 2 * i + c
            p = c % 2
            if there(i, c, 0):
                if not (isinstance(i, int) and n < 2):
                    pool.wait_ge(y_mm, n - 1)
                pool.tensor_tensor(y[:, p, :], x_all[:, n, :], xw[:, n, :], ALU.add).then_inc(y_done, 1)
                pool.wait_ge(mv_done, n + 1)
                pool.wait_ge(xn_done, n + (START - 1))
                apart(pool, g)
                pool.tensor_scalar(ve[:, :], mv[:, p, :, 1], EPS_OUT, None, ALU.add).then_inc(ve_done, 1)
                pool.wait_ge(ve_done, n + 1)
                pool.tensor_tensor(rstd[:, p, :], ve[:, :], mhalf[:, :], ALU.pow).then_inc(rstd_done, 1)

        pair_loop(pool, step, 1)

    @block.vector
    def _(dve):
        dve.sem_inc(xn_done, START)
        dve.memset(mhalf[:, :], -0.5).then_inc(mh_done, 1)

        def step(i, c):
            n = 2 * i + c
            p, q = c % 2, (c - 1) % 2
            if there(i, c, 0):
                dve.wait_ge(y_mm, n + 1)
                if not (isinstance(i, int) and n < 2):
                    dve.wait_ge(ve_done, n - 1)
                apart(dve, g)
                layer_stats(dve, g, bank[:, Y[p], :].rearrange("p (c d) -> p c d", c=C), st[:, p], mv[:, p], bn_done, n + 1, mv_done)
            if there(i, c, 1):
                dve.wait_ge(rstd_done, n)
                if out is None:
                    if not (isinstance(i, int) and n < 3):
                        dve.wait_ge(back_mm, n - 2)
                elif not (isinstance(i, int) and n < 3):
                    k = (c - 1) % 2
                    dve.wait_ge(out_done[k], (2 * i + c - 1 - k) * 8)
                for k in range(C):
                    x = dve.tensor_scalar(xn[:, q, k, :], bank[:, Y[q], k * P:(k + 1) * P], mv[:, q, k, 0:1], rstd[:, q, k:k + 1], ALU.subtract, ALU.mult)
                x.then_inc(xn_done, 1)

        pair_loop(dve, step, 1)

    @block.scalar
    def _(act):
        act.sem_inc(x_done, START)
        act.sem_inc(xw_done, START)

        def step(i, c):
            if there(i, c, 1) and out is None:
                n = 2 * i + c
                q = (c - 1) % 2
                act.wait_ge(back_mm, n)
                apart(act, g)
                act.copy(x_all[:, n - 1, :], bank[:, BACK[q], :]).then_inc(x_done, 1)
                act.copy(xw[:, n - 1, :], bank[:, BACK[q], :]).then_inc(xw_done, 1)

        pair_loop(act, step, 1)

    @block.sync
    def _(sp):
        def step(i, c):
            if there(i, c, 1) and out is not None:
                n = 2 * i + c
                q = (c - 1) % 2
                sp.wait_ge(xn_done, n + START)
                sp.dma_start(out[bass.ds(n - 1, 1), :, :].rearrange("b (c p) d -> p (b c) d", p=P), xn[:, q, :, :]).then_inc(out_done[q], 16)

        pair_loop(sp, step, 1)
        if out is not None:
            for k in range(2):
                sp.wait_ge(out_done[k], 16 * B // 2)


def norm_and_route(nc, ctx, g, w):
    def sb(name, shape, dtype=F32):
        return ctx.enter_context(nc.sbuf_tensor("nr_" + name, shape, dtype))

    def sem(name):
        return phase_semaphore(nc, g, "nr_" + name)

    x_all, xw, ident, bank = g.x, g.xw, g.ident, g.bank
    y = sb("y", [P, 2, T])
    st = sb("st", [P, 2, C, 6])
    mv = sb("mv", [P, 2, C, 2])
    ve = sb("ve", [P, C])
    mhalf = sb("mhalf", [P, C])
    rstd = sb("rstd", [P, 2, C])
    xn = sb("xn", [P, 2, T])
    xT = sb("xT", [P, 2, T])
    ZW = SLOTS * D // 8
    zeros = sb("zeros", [P, ZW])
    wr = sb("wr", [P, E_COUNT])
    lg = sb("lg", [P, TILES, E_COUNT])
    ex = sb("ex", [P, TILES, E_COUNT])
    key = sb("key", [P, TILES, E_COUNT])
    scan = sb("scan", [P, 2, TILES, E_COUNT])
    place = sb("place", [P, TILES, E_COUNT])
    ones = sb("ones", [P, P])
    before = sb("before", [P, P])
    desc = sb("desc", [P, E_COUNT])
    full = sb("full", [P, TILES])
    slot = sb("slot", [P, SLOTS])
    over = sb("over", [P, E_COUNT, TILES])
    started = sb("started", [P, SLOTS, E_COUNT - 1])
    ends = sb("ends", [P, 2, E_COUNT])
    tiles = sb("tiles", [P, E_COUNT])
    starts = sb("starts", [P, E_COUNT])
    top = sb("top", [P, TILES])
    first = sb("first", [P, TILES])
    total = sb("total", [P, TILES])
    posf = sb("posf", [P, TILES])
    texp = sb("texp", [P, SLOTS])
    c_in = sem("c_in")
    mh_done = sem("mh_done")
    y_done = sem("y_done")
    y_mm = sem("y_mm")
    bn_done = sem("bn_done")
    mv_done = sem("mv_done")
    ve_done = sem("ve_done")
    rstd_done = sem("rstd_done")
    xn_done = sem("xn_done")
    back_mm = sem("back_mm")
    tok_done = sem("tok_done")
    xT_done = sem("xT_done")
    lg_mm = sem("lg_mm")
    lg_done = sem("lg_done")
    d_done = sem("d_done")
    ex_done = sem("ex_done")
    oh_done = sem("oh_done")
    cnt_mm = sem("cnt_mm")
    order = sem("order")
    zero_done = sem("zero_done")
    zero_out = sem("zero_out")
    Y, BACK, LG = (0, 1), (2, 3), (4, 5)
    bc = [P, TILES, E_COUNT]
    block = ctx.enter_context(nc.Block())

    def there(i, c, lag):
        return not isinstance(i, int) or 0 <= 2 * i + c - lag < B

    @block.sync
    def _(sp):
        for dst, src in ((wr, "Wr"), (before, "before"), (desc, "desc"), (full, "full"), (slot, "slot")):
            sp.dma_start(dst[:, :], w[src]).then_inc(c_in, 16)
        sp.wait_ge(zero_done, 1)
        flat = g.x_sorted.rearrange("(q p r) d -> q p (r d)", q=8, p=P)
        for q in range(8):
            sp.dma_start(flat[q:q + 1].rearrange("q p f -> p (q f)"), zeros[:, :]).then_inc(zero_out, 16)
        sp.wait_ge(zero_out, 8 * 16)

    @block.tensor
    def _(pe):
        pe.wait_ge(c_in, 5 * 16)

        def step(i, c):
            n = 2 * i + c
            p, q = c % 2, (c - 1) % 2
            if there(i, c, 0):
                pe.wait_ge(y_done, n + 1)
                pe.wait_ge(xn_done, n + (START - 1))
                for k in range(C):
                    mm = pe.transpose(bank[:, Y[p], k * P:(k + 1) * P], y[:, p, k * P:(k + 1) * P], ident[:, :])
                mm.then_inc(y_mm, 1)
            if there(i, c, 1):
                pe.wait_ge(xn_done, n + START)
                pe.wait_ge(xT_done, n + (START - 2))
                for k in range(C):
                    mm = pe.transpose(bank[:, BACK[q], k * P:(k + 1) * P], xn[:, q, k * P:(k + 1) * P], ident[:, :])
                mm.then_inc(back_mm, 1)
            if there(i, c, 2):
                pe.wait_ge(xT_done, n + (START - 1))
                pe.wait_ge(lg_done, n + (START - 3))
                for k in range(C):
                    mm = pe.matmul(bank[:, LG[p], k * E_COUNT:(k + 1) * E_COUNT], xT[:, p, k * P:(k + 1) * P], wr[:, :], start=True, stop=True)
                mm.then_inc(lg_mm, 1)

        pair_loop(pe, step, 2)
        pe.wait_ge(oh_done, 1)
        pe.matmul(bank[:, 6, :], before[:, :], key[:, :, :], start=True, stop=True)
        pe.matmul(bank[:, 7, :], ones[:, :], key[:, :, :], start=True, stop=True).then_inc(cnt_mm, 1)

    @block.gpsimd
    def _(pool):
        pool.memset(zeros[:, :], 0.0).then_inc(zero_done, 1)
        pool.wait_ge(mh_done, 1)

        def step(i, c):
            n = 2 * i + c
            p = c % 2
            if there(i, c, 0):
                if not (isinstance(i, int) and n < 2):
                    pool.wait_ge(y_mm, n - 1)
                pool.tensor_tensor(y[:, p, :], x_all[:, n, :], xw[:, n, :], ALU.add).then_inc(y_done, 1)
                pool.wait_ge(mv_done, n + 1)
                pool.wait_ge(xn_done, n + (START - 1))
                apart(pool, g)
                pool.tensor_scalar(ve[:, :], mv[:, p, :, 1], EPS_OUT, None, ALU.add).then_inc(ve_done, 1)
                pool.wait_ge(ve_done, n + 1)
                pool.tensor_tensor(rstd[:, p, :], ve[:, :], mhalf[:, :], ALU.pow).then_inc(rstd_done, 1)

        pair_loop(pool, step, 1)

    @block.scalar
    def _(act):
        for x in (tok_done, xT_done, lg_done):
            act.sem_inc(x, START)
        nc.scalar.preload_act_table_set("exp_and_others")

        def step(i, c):
            n = 2 * i + c
            p, q = c % 2, (c - 1) % 2
            if there(i, c, 1):
                act.wait_ge(back_mm, n)
                if not (isinstance(i, int) and n < 3):
                    act.wait_ge(lg_mm, n - 2)
                act.copy(xT[:, q, :], bank[:, BACK[q], :]).then_inc(xT_done, 1)
                apart(act, g)
                act.copy(xw[:, n - 1, :], xn[:, q, :]).then_inc(tok_done, 1)
            if there(i, c, 2):
                act.wait_ge(lg_mm, n - 1)
                apart(act, g)
                act.copy(lg[:, bass.ds((n - 2) * C, C), :], bank[:, LG[p], 0:C * E_COUNT].rearrange("p (c e) -> p c e", e=E_COUNT)).then_inc(lg_done, 1)

        pair_loop(act, step, 2)
        act.wait_ge(d_done, 1)
        act.activation(ex[:, :, :], lg[:, :, :], ACT.Exp).then_inc(ex_done, 1)

    @block.vector
    def _(dve):
        dve.sem_inc(xn_done, START)
        dve.memset(ones[:, :], 1.0)
        dve.memset(mhalf[:, :], -0.5).then_inc(mh_done, 1)

        def step(i, c):
            n = 2 * i + c
            p, q = c % 2, (c - 1) % 2
            if there(i, c, 0):
                dve.wait_ge(y_mm, n + 1)
                if not (isinstance(i, int) and n < 2):
                    dve.wait_ge(ve_done, n - 1)
                apart(dve, g)
                layer_stats(dve, g, bank[:, Y[p], :].rearrange("p (c d) -> p c d", c=C), st[:, p], mv[:, p], bn_done, n + 1, mv_done)
            if there(i, c, 1):
                dve.wait_ge(rstd_done, n)
                if not (isinstance(i, int) and n < 3):
                    dve.wait_ge(back_mm, n - 2)
                dve.wait_ge(tok_done, n + (START - 2))
                for k in range(C):
                    x = dve.tensor_scalar(xn[:, q, k * P:(k + 1) * P], bank[:, Y[q], k * P:(k + 1) * P], mv[:, q, k, 0:1], rstd[:, q, k:k + 1], ALU.subtract, ALU.mult)
                x.then_inc(xn_done, 1)

        pair_loop(dve, step, 1)
        dve.wait_ge(lg_done, B + START)
        dve.wait_ge(mh_done, 1)
        dve.tensor_reduce(top[:, :], lg[:, :, :], AX.X, ALU.max).then_inc(order, 1)
        dve.wait_ge(order, 1)
        dve.tensor_tensor(lg[:, :, :], lg[:, :, :], top[:, :].unsqueeze(2).broadcast_to(bc), ALU.subtract).then_inc(d_done, 1)
        dve.wait_ge(d_done, 1)
        dve.wait_ge(c_in, 5 * 16)
        dve.scalar_tensor_tensor(out=key[:, :, :], in0=lg[:, :, :], scalar=0.0, in1=desc[:, :].unsqueeze(1).broadcast_to(bc), op0=ALU.is_ge, op1=ALU.mult).then_inc(order, 1)
        dve.wait_ge(order, 2)
        dve.tensor_reduce(first[:, :], key[:, :, :], AX.X, ALU.max).then_inc(order, 1)
        dve.wait_ge(order, 3)
        dve.tensor_tensor(key[:, :, :], key[:, :, :], first[:, :].unsqueeze(2).broadcast_to(bc), ALU.is_equal).then_inc(oh_done, 1)
        dve.wait_ge(ex_done, 1)
        dve.tensor_reduce(total[:, :], ex[:, :, :], AX.X, ALU.add).then_inc(order, 1)
        dve.wait_ge(order, 4)
        dve.reciprocal(g.pmax[:, :], total[:, :]).then_inc(order, 1)
        dve.wait_ge(cnt_mm, 1)
        dve.tensor_copy(scan[:, 0, :, :], bank[:, 7, :].rearrange("p (k e) -> p k e", e=E_COUNT)).then_inc(order, 1)
        shift, a, at = 1, 0, 6
        while shift < TILES:
            dve.wait_ge(order, at)
            dve.tensor_copy(scan[:, 1 - a, 0:shift, :], scan[:, a, 0:shift, :])
            dve.tensor_tensor(scan[:, 1 - a, shift:, :], scan[:, a, shift:, :], scan[:, a, 0:TILES - shift, :], ALU.add).then_inc(order, 1)
            shift, a, at = 2 * shift, 1 - a, at + 1
        dve.wait_ge(order, at)
        dve.tensor_tensor(place[:, :, :], scan[:, a, :, :], bank[:, 7, :].rearrange("p (k e) -> p k e", e=E_COUNT), ALU.subtract).then_inc(order, 1)
        dve.tensor_tensor(over[:, :, :], scan[:, a, TILES - 1, :].unsqueeze(2).broadcast_to([P, E_COUNT, TILES]),
                          full[:, :].unsqueeze(1).broadcast_to([P, E_COUNT, TILES]), ALU.is_gt).then_inc(order, 1)
        dve.wait_ge(order, at + 2)
        dve.tensor_tensor(place[:, :, :], place[:, :, :], bank[:, 6, :].rearrange("p (k e) -> p k e", e=E_COUNT), ALU.add).then_inc(order, 1)
        dve.tensor_reduce(tiles[:, :], over[:, :, :], AX.X, ALU.add).then_inc(order, 1)
        dve.wait_ge(order, at + 4)
        dve.tensor_copy(ends[:, 0, :], tiles[:, :]).then_inc(order, 1)
        shift, a, at = 1, 0, at + 5
        while shift < E_COUNT:
            dve.wait_ge(order, at)
            dve.tensor_copy(ends[:, 1 - a, 0:shift], ends[:, a, 0:shift])
            dve.tensor_tensor(ends[:, 1 - a, shift:], ends[:, a, shift:], ends[:, a, 0:E_COUNT - shift], ALU.add).then_inc(order, 1)
            shift, a, at = 2 * shift, 1 - a, at + 1
        dve.wait_ge(order, at)
        dve.tensor_tensor(starts[:, :], ends[:, a, :], tiles[:, :], ALU.subtract).then_inc(order, 1)
        dve.wait_ge(order, at + 1)
        dve.scalar_tensor_tensor(out=place[:, :, :], in0=starts[:, :].unsqueeze(1).broadcast_to(bc), scalar=float(P), in1=place[:, :, :], op0=ALU.mult, op1=ALU.add).then_inc(order, 1)
        dve.tensor_tensor(started[:, :, :], starts[:, 1:].unsqueeze(1).broadcast_to([P, SLOTS, E_COUNT - 1]),
                          slot[:, :].unsqueeze(2).broadcast_to([P, SLOTS, E_COUNT - 1]), ALU.is_le).then_inc(order, 1)
        dve.wait_ge(order, at + 3)
        dve.tensor_tensor(place[:, :, :], place[:, :, :], key[:, :, :], ALU.mult).then_inc(order, 1)
        dve.tensor_reduce(texp[:, :], started[:, :, :], AX.X, ALU.add).then_inc(order, 1)
        dve.wait_ge(order, at + 5)
        dve.tensor_reduce(posf[:, :], place[:, :, :], AX.X, ALU.add).then_inc(order, 1)
        dve.tensor_copy(g.tile_expert[:, :], texp[:, :]).then_inc(order, 1)
        dve.wait_ge(order, at + 7)
        dve.tensor_copy(g.place[:, :], posf[:, :]).then_inc(order, 1)


def slot_loop(eng, step, depth):
    for c in range(4):
        step(0, c)
    with eng.Fori(1, SLOTS // 4 - 1) as i:
        for c in range(4):
            step(i, c)
    for c in range(4 + depth):
        step(SLOTS // 4 - 1 + c // 4, c % 4)


def l0_experts(nc, ctx, g, w):
    def sb(name, shape):
        return ctx.enter_context(nc.sbuf_tensor("ex_" + name, shape, F32))

    def sem(name):
        return phase_semaphore(nc, g, "ex_" + name)

    ident, bank = g.ident, g.bank
    tok = g.xw[:, :, :].rearrange("p n (c d) -> p (n c) d", d=D)
    w1 = sb("w1", [P, E_COUNT, E_FF])
    w2 = sb("w2", [P, E_COUNT, EF, D])
    b1 = sb("b1", [P, E_COUNT, E_FF])
    b2 = sb("b2", [P, E_COUNT, D])
    xin = sb("xin", [P, 4, D])
    xT = sb("xT", [P, 2, P])
    hb = sb("hb", [P, 2, E_FF])
    hg = sb("hg", [P, 2, E_FF])
    hT = sb("hT", [P, 2, EF, P])
    yo = sb("yo", [P, 4, D])
    w_in = sem("w_in")
    sorted = sem("sorted")
    x_in0 = sem("x_in0")
    x_in1 = sem("x_in1")
    x_in2 = sem("x_in2")
    x_in3 = sem("x_in3")
    y_out0 = sem("y_out0")
    y_out1 = sem("y_out1")
    y_out2 = sem("y_out2")
    y_out3 = sem("y_out3")
    x_mm = sem("x_mm")
    xT_done = sem("xT_done")
    h_mm = sem("h_mm")
    hb_done = sem("hb_done")
    hg_done = sem("hg_done")
    ht_mm = sem("ht_mm")
    hT_done = sem("hT_done")
    y_mm = sem("y_mm")
    y_done = sem("y_done")
    x_in = [x_in0, x_in1, x_in2, x_in3]
    y_out = [y_out0, y_out1, y_out2, y_out3]
    X, H, HT_, Y = 0, (1, 2), (3, 4), (5, 6)
    block = ctx.enter_context(nc.Block())

    def there(i, c, lag):
        return not isinstance(i, int) or 0 <= 4 * i + c - lag < SLOTS

    def expert_of(eng, t):
        return eng.value_load(g.tile_expert[0:1, bass.ds(t, 1)], min_val=0, max_val=E_COUNT - 1)

    @block.gpsimd
    def _(pool):
        for k in range(TILES):
            pool.indirect_dma_start(g.x_sorted, bass.IndirectOffsetOnAxis(g.place[:, k:k + 1], 0), tok[:, k, :], None).then_inc(sorted, 16)
        pool.wait_ge(sorted, 16 * TILES)

    @block.sync
    def _(sp):
        for e in range(E_COUNT):
            sp.dma_start(w1[:, e, :], w["W1"][e]).then_inc(w_in, 16)
        sp.dma_start(w2[:, :, :, :].rearrange("p e f d -> p (e f) d"), w["W2"].rearrange("e (f p) d -> p (e f) d", p=P)).then_inc(w_in, 16)
        sp.dma_start(b1[:, :, :].rearrange("p e f -> p (e f)"), w["b1"].rearrange("e f -> (e f)").unsqueeze(0).partition_broadcast(P)).then_inc(w_in, 16)
        sp.dma_start(b2[:, :, :].rearrange("p e f -> p (e f)"), w["b2"].rearrange("e f -> (e f)").unsqueeze(0).partition_broadcast(P)).then_inc(w_in, 16)
        for y in y_out:
            sp.sem_inc(y, 16)
        sp.wait_ge(sorted, 16 * TILES)

        def load(t, slot):
            sp.dma_start(xin[:, slot, :], g.x_sorted[bass.ds(t * P, P), :]).then_inc(x_in[slot], 16)
        for t in range(3):
            load(t, t)

        def step(i, c):
            m = 4 * i + c
            if not isinstance(i, int) or m + 3 < SLOTS:
                if not (isinstance(i, int) and m < 1):
                    sp.wait_ge(x_mm, m)
                load(m + 3, (c + 3) % 4)
            if there(i, c, 4):
                sp.wait_ge(y_done, m + (START - 3))
                sp.dma_start(g.y_sorted[bass.ds((m - 4) * P, P), :], yo[:, c, :]).then_inc(y_out[c], 16)

        slot_loop(sp, step, 4)
        for y in y_out:
            sp.wait_ge(y, 16 * (SLOTS // 4 + 1))

    @block.tensor
    def _(pe):
        pe.wait_ge(w_in, 16 * (E_COUNT + 3))

        def step(i, c):
            m = 4 * i + c
            p, q = c % 2, (c - 1) % 2
            if there(i, c, 0):
                pe.wait_ge(x_in[c], i * 16 + 16)
                pe.wait_ge(xT_done, m + START)
                pe.transpose(bank[:, X, 0:P], xin[:, c, :], ident[:, :]).then_inc(x_mm, 1)
            if there(i, c, 1):
                e = expert_of(pe, m - 1)
                pe.wait_ge(xT_done, m + START)
                pe.wait_ge(hb_done, m + (START - 2))
                pe.matmul(bank[:, H[q], :], xT[:, q, :], w1[:, bass.ds(e, 1), :].rearrange("p a f -> p (a f)"), start=True, stop=True).then_inc(h_mm, 1)
            if there(i, c, 2):
                pe.wait_ge(hg_done, m + (START - 1))
                pe.wait_ge(hT_done, m + (START - 3))
                for f in range(EF):
                    mm = pe.transpose(bank[:, HT_[p], f * P:(f + 1) * P], hg[:, p, f * P:(f + 1) * P], ident[:, :])
                mm.then_inc(ht_mm, 1)
            if there(i, c, 3):
                e = expert_of(pe, m - 3)
                pe.wait_ge(hT_done, m + (START - 2))
                pe.wait_ge(y_done, m + (START - 4))
                for f in range(EF):
                    mm = pe.matmul(bank[:, Y[q], 0:D], hT[:, q, f, :], w2[:, bass.ds(e, 1), f, :].rearrange("p a d -> p (a d)"), start=(f == 0), stop=(f == EF - 1))
                mm.then_inc(y_mm, 1)

        slot_loop(pe, step, 3)

    @block.vector
    def _(dve):
        for x in (xT_done, hb_done, y_done):
            dve.sem_inc(x, START)
        dve.wait_ge(w_in, 16 * (E_COUNT + 3))

        def step(i, c):
            m = 4 * i + c
            p, q = c % 2, (c - 1) % 2
            if there(i, c, 0):
                dve.wait_ge(x_mm, m + 1)
                if not (isinstance(i, int) and m < 2):
                    dve.wait_ge(h_mm, m - 1)
                dve.tensor_copy(xT[:, p, :], bank[:, X, 0:P]).then_inc(xT_done, 1)
            if there(i, c, 1):
                e = expert_of(dve, m - 1)
                dve.wait_ge(h_mm, m)
                dve.wait_ge(hg_done, m + (START - 2))
                dve.tensor_tensor(hb[:, q, :], bank[:, H[q], :], b1[:, bass.ds(e, 1), :].rearrange("p a f -> p (a f)"), ALU.add).then_inc(hb_done, 1)
            if there(i, c, 3):
                e = expert_of(dve, m - 3)
                dve.wait_ge(y_mm, m - 2)
                slot = (c - 3) % 4
                dve.wait_ge(y_out[slot], (i + (c - 3) // 4) * 16 + 16)
                dve.tensor_tensor(yo[:, slot, :], bank[:, Y[q], 0:D], b2[:, bass.ds(e, 1), :].rearrange("p a f -> p (a f)"), ALU.add).then_inc(y_done, 1)

        slot_loop(dve, step, 3)

    @block.scalar
    def _(act):
        act.sem_inc(hg_done, START)
        act.sem_inc(hT_done, START)
        nc.scalar.preload_act_table_set("gelu_and_others")

        def step(i, c):
            m = 4 * i + c
            p, q = c % 2, (c - 1) % 2
            if there(i, c, 2):
                act.wait_ge(ht_mm, m - 1)
                if not (isinstance(i, int) and m < 4):
                    act.wait_ge(y_mm, m - 3)
                act.copy(hT[:, p, :, :], bank[:, HT_[p], :].rearrange("p (f t) -> p f t", t=P)).then_inc(hT_done, 1)
            if there(i, c, 1):
                act.wait_ge(hb_done, m + START)
                if not (isinstance(i, int) and m < 3):
                    act.wait_ge(ht_mm, m - 2)
                act.activation(hg[:, q, :], hb[:, q, :], ACT.Gelu).then_inc(hg_done, 1)

        slot_loop(act, step, 2)


def gather_and_norm(nc, ctx, g):
    def sb(name, shape):
        return ctx.enter_context(nc.sbuf_tensor("gn_" + name, shape, F32))

    def sem(name):
        return phase_semaphore(nc, g, "gn_" + name)

    x_all, xw, ident, bank = g.x, g.xw, g.ident, g.bank
    back = g.x[:, :, :].rearrange("p n (c d) -> p (n c) d", d=D)
    y = sb("y", [P, 2, C, D])
    st = sb("st", [P, 2, C, 6])
    mv = sb("mv", [P, 2, C, 2])
    ve = sb("ve", [P, 2, C])
    mhalf = sb("mhalf", [P, C])
    rstd = sb("rstd", [P, 2, C])
    xn = sb("xn", [P, 2, C, D])
    mh_done = sem("mh_done")
    y_done = sem("y_done")
    bn_done = sem("bn_done")
    mv_done = sem("mv_done")
    ve_done = sem("ve_done")
    rstd_done = sem("rstd_done")
    xn_done = sem("xn_done")
    back_mm = sem("back_mm")
    x_done = sem("x_done")
    AHEAD = 8
    taken = [sem("taken%d" % k) for k in range(AHEAD)]
    BACK = (2, 3)
    block = ctx.enter_context(nc.Block())

    def there(i, c, lag):
        return not isinstance(i, int) or 0 <= 2 * i + c - lag < B

    @block.gpsimd
    def _(pool):
        pool.wait_ge(mh_done, 1)
        for n in range(B + 2):
            if n < B:
                for k in range(C * n, C * n + C):
                    if k >= AHEAD:
                        pool.wait_ge(taken[k % AHEAD], 16 * (k // AHEAD))
                    pool.indirect_dma_start(back[:, k, :], None, g.y_sorted, bass.IndirectOffsetOnAxis(g.place[:, k:k + 1], 0)).then_inc(taken[k % AHEAD], 16)
            if n >= 2:
                m = n - 2
                pool.wait_ge(mv_done, m + 1)
                if m:
                    pool.wait_ge(xn_done, m + (START - 1))
                pool.tensor_scalar(ve[:, m % 2, :], mv[:, m % 2, :, 1], EPS_OUT, None, ALU.add).then_inc(ve_done, 1)
                pool.wait_ge(ve_done, m + 1)
                pool.tensor_tensor(rstd[:, m % 2, :], ve[:, m % 2, :], mhalf[:, :], ALU.pow).then_inc(rstd_done, 1)

    @block.vector
    def _(dve):
        dve.sem_inc(xn_done, START)
        dve.memset(mhalf[:, :], -0.5).then_inc(mh_done, 1)

        def step(i, c):
            n = 2 * i + c
            p, q = c % 2, (c - 1) % 2
            if there(i, c, 0):
                dve.wait_ge(xn_done, n + (START - 1))
                for k in range(C):
                    dve.wait_ge(taken[p * C + k], i * 16 + 16)
                    t = n * C + k
                    x = dve.scalar_tensor_tensor(out=y[:, p, k:k + 1, :], in0=back[:, bass.ds(t, 1), :], scalar=g.pmax[:, bass.ds(t, 1)],
                                                 in1=xw[:, n, k * D:(k + 1) * D].unsqueeze(1), op0=ALU.mult, op1=ALU.add)
                x.then_inc(y_done, 1)
                dve.wait_ge(y_done, n + 1)
                if not (isinstance(i, int) and n < 2):
                    dve.wait_ge(ve_done, n - 1)
                apart(dve, g)
                layer_stats(dve, g, y[:, p], st[:, p], mv[:, p], bn_done, n + 1, mv_done)
            if there(i, c, 1):
                dve.wait_ge(rstd_done, n)
                if not (isinstance(i, int) and n < 3):
                    dve.wait_ge(back_mm, n - 2)
                for k in range(C):
                    x = dve.tensor_scalar(xn[:, q, k, :], y[:, q, k, :], mv[:, q, k, 0:1], rstd[:, q, k:k + 1], ALU.subtract, ALU.mult)
                x.then_inc(xn_done, 1)

        pair_loop(dve, step, 1)

    @block.tensor
    def _(pe):
        def step(i, c):
            n = 2 * i + c
            q = (c - 1) % 2
            if there(i, c, 1):
                pe.wait_ge(xn_done, n + START)
                pe.wait_ge(x_done, n + (START - 2))
                for k in range(C):
                    mm = pe.transpose(bank[:, BACK[q], k * P:(k + 1) * P], xn[:, q, k, :], ident[:, :])
                mm.then_inc(back_mm, 1)

        pair_loop(pe, step, 1)

    @block.scalar
    def _(act):
        act.sem_inc(x_done, START)

        def step(i, c):
            if there(i, c, 1):
                n = 2 * i + c
                q = (c - 1) % 2
                act.wait_ge(back_mm, n)
                apart(act, g)
                act.copy(x_all[:, n - 1, :], bank[:, BACK[q], :])
                act.copy(xw[:, n - 1, :], bank[:, BACK[q], :]).then_inc(x_done, 1)

        pair_loop(act, step, 1)


def program(nc, w, out):
    with ExitStack() as ctx:
        sb = lambda name, shape: ctx.enter_context(nc.sbuf_tensor(name, shape, F32))
        ident = sb("ident_sb", [P, P])
        ident_in = ctx.enter_context(nc.semaphore("ident_in"))
        g = Shared()
        g.ident = ident
        g.x = sb("x_all", [P, B, T])
        g.xw = sb("xw_all", [P, B, T])
        g.bank = ctx.enter_context(nc.psum_tensor("bank", [P, 8, T], F32))
        g.place = ctx.enter_context(nc.sbuf_tensor("place_all", [P, TILES], mybir.dt.int32))
        g.tile_expert = ctx.enter_context(nc.sbuf_tensor("tile_expert", [P, SLOTS], mybir.dt.int32))
        g.pmax = sb("pmax_all", [P, TILES])
        g.x_sorted = nc.dram_tensor("x_sorted", (SLOTS * P, D), F32, kind="Internal").ap()
        g.y_sorted = nc.dram_tensor("y_sorted", (SLOTS * P, D), F32, kind="Internal").ap()
        g.passed = ctx.enter_context(nc.semaphore("passed"))
        with nc.Block() as block:
            @block.sync
            def _(sp):
                sp.dma_start(ident[:, :], w["ident"]).then_inc(ident_in, 16)
                sp.wait_ge(ident_in, 16)

        def part(prefix, *tables):
            own = {k[len(prefix):]: v for k, v in w.items() if k.startswith(prefix)}
            own.update({k: w[k] for k in tables})
            return own

        l0 = part("L0_attn_", "rtab", "tri", "diag", "heads")
        l0["x"] = w["L0_attn_hidden_states"]
        run_phase(nc, g, l0_retention, l0)
        run_phase(nc, g, norm_and_route, part("L0_ffn_", *MOE_TABLES))
        run_phase(nc, g, l0_experts, part("L0_ffn_"))
        run_phase(nc, g, gather_and_norm)
        run_phase(nc, g, l1_attention, part("L1_attn_"))
        run_phase(nc, g, outer_norm, "n2_")
        run_phase(nc, g, l1_local, part("L1_ffn_", "tab", "band"))
        run_phase(nc, g, outer_norm, "n3_", out)


def kernel(**inputs):
    import concourse.bacc as bacc
    from concourse.bass_utils import run_bass_kernel_spmd

    nc = bacc.Bacc("TRN2", target_bir_lowering=False, num_devices=1)
    arrays = {name: np.ascontiguousarray(a) for name, a in inputs.items()}
    arrays["ident"] = np.eye(P, dtype=np.float32)
    arrays["tab"], arrays["band"] = local_tables()
    arrays["rtab"], arrays["tri"], arrays["diag"], arrays["heads"] = retention_tables()
    arrays.update(moe_tables())
    w = {name: nc.dram_tensor("in_" + name, a.shape, F32, kind="ExternalInput").ap() for name, a in arrays.items()}
    out = nc.dram_tensor("out_x", (B, T, D), F32, kind="ExternalOutput").ap()
    program(nc, w, out)
    r = run_bass_kernel_spmd(nc, [{"in_" + name: a for name, a in arrays.items()}], core_ids=[0])
    return r.results[0]["out_x"]
```

```python
from contextlib import ExitStack

import numpy as np
import concourse.bass as bass
import concourse.mybir as mybir

F32 = mybir.dt.float32
F32R = mybir.dt.float32r
ACT = mybir.ActivationFunctionType
ALU = mybir.AluOpType
AX = mybir.AxisListType

P = 128
B, T, D = 16, 512, 128
C = T // P
A_BLOCKS, A_FF = 8, 512
FT = A_FF // P
EPS_LN1, EPS_Z = 1e-6, 1e-6
TINY = 1e-37
START = 4


class Shared:
    pass


def in_range(n, lag):
    return not isinstance(n, int) or 0 <= n - lag < B


def apart(eng, g):
    eng.sem_inc(g.passed, 1)


def split_matmul(pe, out, lhs, rhs):
    pe.matmul(out, lhs[0], rhs[1], start=True, stop=False)
    pe.matmul(out, lhs[1], rhs[0], start=False, stop=False)
    return pe.matmul(out, lhs[0], rhs[0], start=False, stop=True)


def phase_semaphore(nc, g, name):
    g.used.append(g.keep.enter_context(nc.semaphore(name)))
    return g.used[-1]


def run_phase(nc, g, build, *args):
    with ExitStack() as g.keep:
        g.used = []
        with ExitStack() as ctx:
            build(nc, ctx, g, *args)
        with nc.Block() as block:
            @block.gpsimd
            def _(pool):
                for sem in g.used:
                    pool.sem_clear(sem)


def layer_stats(dve, g, x, stats, mean_var, bn_done, count, mv_done):
    for c in range(C):
        last = dve.bn_stats(stats[:, c, :], x[:, c, :])
    last.then_inc(bn_done, 1)
    dve.wait_ge(bn_done, count)
    apart(dve, g)
    for c in range(C):
        last = dve.bn_aggr(mean_var[:, c, :], stats[:, c, :])
    last.then_inc(mv_done, 1)


def l1_attention(nc, ctx, g, w):
    def sb(name, shape, dtype=F32):
        return ctx.enter_context(nc.sbuf_tensor("a1_" + name, shape, dtype))

    def sem(name):
        return phase_semaphore(nc, g, "a1_" + name)

    xw, ident, bank = g.xw, g.ident, g.bank
    w_qkv = sb("w_qkv", [P, 3, D])
    w_o = sb("w_o", [P, D])
    w_f1 = sb("w_f1", [P, A_FF])
    w_f1_hi, w_f1_lo = sb("w_f1_hi", [P, A_FF], F32R), sb("w_f1_lo", [P, A_FF], F32R)
    x1_hi, x1_lo = sb("x1_hi", [P, T], F32R), sb("x1_lo", [P, T], F32R)
    w_f2 = sb("w_f2", [P, FT, D])
    VEC = ["bq", "bk", "bv", "bo", "ln1_s", "ln1_b", "bf2", "ln2_s", "ln2_b"]
    NROWS = len(VEC) * A_BLOCKS + FT * A_BLOCKS
    rows = sb("rows", [NROWS, P])
    cols = sb("cols", [P, NROWS])
    qv = sb("qv", [P, B, T])
    ex = sb("ex", [P, 2, T])
    re = sb("re", [P, 2, T])
    kk = sb("kk", [P, T])
    junk = sb("junk", [P, T])
    zz = sb("zz", [P, T])
    ksum = sb("ksum", [P, B])
    kvsum = sb("kvsum", [P, B])
    rks = sb("rks", [P, B])
    va = sb("va", [P, B])
    nva = sb("nva", [P, B])
    consts = sb("consts", [P, 2])
    eps_z, ln_eps_z = consts[:, 0:1], consts[:, 1:2]
    att = sb("att", [P, T])
    y1 = sb("y1", [P, T])
    xn1 = sb("xn1", [P, C, D])
    hid = sb("hid", [P, FT, T])
    ffo = sb("ffo", [P, T])
    y2 = sb("y2", [P, T])
    xn2 = sb("xn2", [P, C, D])
    st = sb("st", [P, 2, C, 6])
    mv = sb("mv", [P, 2, C, 2])
    ve = sb("ve", [P, 2, C])
    rstd = sb("rstd", [P, 2, C])
    mhalf = sb("mhalf", [P, C])

    def col(kind, blk):
        k = VEC.index(kind) * A_BLOCKS
        return cols[:, bass.ds(blk + k, 1)]

    def col_f1(blk, f):
        return cols[:, bass.ds(blk * FT + (len(VEC) * A_BLOCKS + f), 1)]

    QKV, ACTS, Z, WO, LN1, FF, FF_OUT, LN2 = range(8)
    BEGIN = LN2 + 1
    HEAD = LN2

    rows_in, rows_T, cols_done, cst_done = sem("rows_in"), sem("rows_T"), sem("cols_done"), sem("cst_done")
    wa_in, wo_in, wf_in = sem("wa_in"), sem("wo_in"), sem("wf_in")
    x_done = sem("x_done")
    qk_mm, v_mm = sem("qk_mm"), sem("v_mm")
    er_done = sem("er_done")
    k_done = sem("k_done")
    e_done = sem("e_done")
    q_done = sem("q_done")
    kv_done = sem("kv_done")
    coef, rec = sem("coef"), sem("rec")
    va_done = sem("va_done")
    ln_done = sem("ln_done")
    z_done = sem("z_done")
    v_done = sem("v_done")
    o_mm, att_done = sem("o_mm"), sem("att_done")
    y1_done, y2_done = sem("y1_done"), sem("y2_done")
    t1_mm, t2_mm = sem("t1_mm"), sem("t2_mm")
    bn1_done, bn2_done = sem("bn1_done"), sem("bn2_done")
    mv1_done, mv2_done = sem("mv1_done"), sem("mv2_done")
    ve1_done, ve2_done = sem("ve1_done"), sem("ve2_done")
    rs1_done, rs2_done = sem("rs1_done"), sem("rs2_done")
    xn1_done, xn2_done = sem("xn1_done"), sem("xn2_done")
    u1_mm, u2_mm = sem("u1_mm"), sem("u2_mm")
    x1_done = sem("x1_done")
    x1_hi_done, x1_split = sem("x1_hi_done"), sem("x1_split")
    w_f1_in, w_hi_done, w_f1_split = sem("w_f1_in"), sem("w_hi_done"), sem("w_f1_split")
    h_mm, h_done = sem("h_mm"), sem("h_done")
    f2_mm, ff_done = sem("f2_mm"), sem("ff_done")

    QB, KB, VB, T1, T2, H, F = 0, 1, 2, 3, 4, 5, 7

    def tiles(b):
        return bank[:, b, :].rearrange("p (c d) -> p c d", c=C)

    def has(blk, n, lag):
        if isinstance(n, int) and isinstance(blk, int):
            return n >= lag if blk == 0 else n < lag
        return True

    def seq(n, lag):
        return n - lag + (B if isinstance(n, int) and n < lag else 0)

    def block_of(blk, n, lag):
        return blk - 1 if isinstance(n, int) and n < lag else blk

    def done(j):
        return j + (BEGIN + 1)

    def part_done(j, f):
        return j * FT + (BEGIN * FT + f + 1)

    def block_loop(eng, step):
        for n in range(HEAD):
            step(0, n)
        with eng.Fori(0, A_BLOCKS - 1) as b:
            with eng.Fori(HEAD, B) as n:
                step(b, n)
            for n in range(HEAD):
                step(b + 1, n)
        with eng.Fori(HEAD, B) as n:
            step(A_BLOCKS - 1, n)
        for n in range(HEAD):
            step(A_BLOCKS, n)

    block = ctx.enter_context(nc.Block())

    @block.sync
    def _(sp):
        names = VEC + ["bf1"]
        for i, name in enumerate(names):
            src = w[name] if name != "bf1" else w[name].rearrange("b (f p) -> (b f) p", p=P)
            n = src.shape[0]
            sp.dma_start(rows[i * A_BLOCKS:i * A_BLOCKS + n, :], src).then_inc(rows_in, 16)

        def load_a(b):
            for i, name in enumerate(["Wq", "Wk", "Wv"]):
                sp.dma_start(w_qkv[:, i, :], w[name][bass.ds(b, 1), :, :].rearrange("b p a -> (b p) a")).then_inc(wa_in, 16)

        def load_o(b):
            sp.dma_start(w_o[:, :], w["Wo"][bass.ds(b, 1), :, :].rearrange("b p a -> (b p) a")).then_inc(wo_in, 16)

        def load_f1(b):
            sp.dma_start(w_f1[:, :], w["Wf1"][bass.ds(b, 1), :, :].rearrange("b p a -> (b p) a")).then_inc(w_f1_in, 16)

        def load_f(b):
            sp.dma_start(w_f2[:, :, :], w["Wf2"][bass.ds(b, 1), :, :].rearrange("b (k p) a -> p (b k) a", p=P)).then_inc(wf_in, 16)
        load_a(0)
        load_o(0)
        load_f1(0)
        load_f(0)
        with sp.Fori(0, A_BLOCKS - 1) as b:
            sp.wait_ge(w_f1_split, b + 1)
            load_f1(b + 1)
            sp.wait_ge(v_mm, done(b * B + (B - 1)))
            load_a(b + 1)
            sp.wait_ge(o_mm, done(b * B + (B - 1)))
            load_o(b + 1)
            sp.wait_ge(f2_mm, done(b * B + (B - 1)))
            load_f(b + 1)

    @block.tensor
    def _(pe):
        for s in (qk_mm, v_mm, o_mm, t1_mm, t2_mm, u1_mm, u2_mm, f2_mm):
            pe.sem_inc(s, BEGIN)
        pe.sem_inc(h_mm, BEGIN * FT)
        pe.wait_ge(rows_in, 16 * (len(VEC) + 1))
        pe.transpose(bank[:, 7, 0:NROWS], rows[:, :], ident[0:NROWS, 0:NROWS]).then_inc(rows_T, 1)
        pe.wait_ge(cols_done, 1)

        def transposes(b, src, count):
            for c in range(C):
                mm = pe.transpose(tiles(b)[:, c, :], src[c], ident[:, :])
            mm.then_inc(count, 1)

        def step(blk, n):
            at = blk * B + n
            there = [has(blk, n, lag) for lag in range(LN2 + 1)]
            if there[LN1]:
                pe.wait_ge(y1_done, done(at - LN1))
                pe.wait_ge(x1_done, done(at - LN1 - 1))
                transposes(T1, [y1[:, c * P:(c + 1) * P] for c in range(C)], t1_mm)
            if there[LN2]:
                pe.wait_ge(y2_done, done(at - LN2))
                pe.wait_ge(x_done, at + (B - LN2))
                transposes(T2, [y2[:, c * P:(c + 1) * P] for c in range(C)], t2_mm)
            def first_products(tiles_of_hidden):
                for f in tiles_of_hidden:
                    pe.wait_ge(h_done, part_done(at - FF, f - 2))
                    cut = slice(f * P, (f + 1) * P)
                    split_matmul(pe, bank[:, H + f % 2, :], (w_f1_hi[:, cut], w_f1_lo[:, cut]), (x1_hi[:, :], x1_lo[:, :])).then_inc(h_mm, 1)

            if there[FF]:
                if isinstance(n, int) and n == FF:
                    pe.wait_ge(w_f1_split, blk + 1)
                    pe.wait_ge(wf_in, (blk + 1) * 16)
                pe.wait_ge(x1_split, done(at - FF))
                first_products(range(2))
            if there[WO]:
                if isinstance(n, int) and n == WO:
                    pe.wait_ge(wo_in, (blk + 1) * 16)
                pe.wait_ge(v_done, done(at - WO))
                if there[FF_OUT]:
                    pe.wait_ge(ff_done, done(at - FF_OUT))
                pe.matmul(bank[:, F, :], w_o[:, :], qv[:, seq(n, WO), :], start=True, stop=True).then_inc(o_mm, 1)
            if there[FF]:
                first_products(range(2, FT))
            def second_products(tiles_of_hidden):
                for f in tiles_of_hidden:
                    pe.wait_ge(h_done, part_done(at - FF, f))
                    mm = pe.matmul(bank[:, F, :], w_f2[:, f, :], hid[:, f, :], start=(f == 0), stop=(f == FT - 1))
                return mm

            if there[FF]:
                if there[WO]:
                    pe.wait_ge(att_done, done(at - WO))
                elif there[FF_OUT]:
                    pe.wait_ge(ff_done, done(at - FF_OUT))
                second_products(range(2))
            if there[LN1]:
                pe.wait_ge(xn1_done, done(at - LN1))
                transposes(T1, [xn1[:, c, :] for c in range(C)], u1_mm)
            if there[FF]:
                second_products(range(2, FT)).then_inc(f2_mm, 1)
            if there[LN2]:
                pe.wait_ge(xn2_done, done(at - LN2))
                transposes(T2, [xn2[:, c, :] for c in range(C)], u2_mm)
            if there[QKV]:
                if isinstance(n, int) and n == QKV:
                    pe.wait_ge(wa_in, (blk + 1) * 48)
                x = xw[:, seq(n, QKV), :]
                pe.wait_ge(x_done, at + 1)
                pe.wait_ge(er_done, done(at - ACTS))
                pe.matmul(bank[:, QB, :], w_qkv[:, 0, :], x, start=True, stop=True)
                pe.matmul(bank[:, KB, :], w_qkv[:, 1, :], x, start=True, stop=True).then_inc(qk_mm, 1)
                pe.wait_ge(kv_done, done(at - ACTS))
                pe.matmul(bank[:, VB, :], w_qkv[:, 2, :], x, start=True, stop=True).then_inc(v_mm, 1)

        block_loop(pe, step)

    @block.scalar
    def _(act):
        act.wait_ge(cst_done, 1)
        act.sem_inc(x_done, B)
        for s in (er_done, ln_done, z_done, att_done, ff_done):
            act.sem_inc(s, BEGIN)
        act.sem_inc(h_done, BEGIN * FT)
        act.wait_ge(cols_done, 1)

        def step(blk, n):
            at = blk * B + n
            there = [has(blk, n, lag) for lag in range(LN2 + 1)]
            in_block = [block_of(blk, n, lag) for lag in range(LN2 + 1)]
            if there[FF_OUT] or there[WO] or there[FF]:
                nc.scalar.preload_act_table_set("gelu_apprx_tanh_and_others")
            if there[FF_OUT]:
                act.wait_ge(f2_mm, done(at - FF_OUT))
                act.wait_ge(y2_done, done(at - FF_OUT - 1))
                apart(act, g)
                act.activation(ffo[:, :], bank[:, F, :], ACT.Gelu_apprx_tanh, bias=col("bf2", in_block[FF_OUT])).then_inc(ff_done, 1)

            def hidden(tiles_of_hidden):
                for f in tiles_of_hidden:
                    act.wait_ge(h_mm, part_done(at - FF, f))
                    act.wait_ge(f2_mm, done(at - FF - 1))
                    apart(act, g)
                    act.activation(hid[:, f, :], bank[:, H + f % 2, :], ACT.Gelu_apprx_tanh, bias=col_f1(in_block[FF], f)).then_inc(h_done, 1)

            if there[FF]:
                hidden(range(2))
            if there[WO]:
                act.wait_ge(o_mm, done(at - WO))
                act.wait_ge(y1_done, done(at - WO - 1))
                apart(act, g)
                act.activation(att[:, :], bank[:, F, :], ACT.Gelu_apprx_tanh, bias=col("bo", in_block[WO])).then_inc(att_done, 1)
            if there[FF]:
                hidden(range(2, FT))
            if there[ACTS] or there[Z]:
                nc.scalar.preload_act_table_set("natural_log_exp_and_others")
            if there[ACTS]:
                b = in_block[ACTS]
                act.wait_ge(qk_mm, done(at - ACTS))
                act.wait_ge(q_done, done(at - ACTS - 1))
                apart(act, g)
                act.activation(ex[:, 1, :], bank[:, KB, :], ACT.Exp, bias=col("bk", b))
                act.activation(re[:, 1, :], bank[:, KB, :], ACT.Relu, bias=col("bk", b))
                act.activation(ex[:, 0, :], bank[:, QB, :], ACT.Exp, bias=col("bq", b))
                act.activation(re[:, 0, :], bank[:, QB, :], ACT.Relu, bias=col("bq", b)).then_inc(er_done, 1)
            if there[Z]:
                k = seq(n, Z)
                act.wait_ge(v_done, done(at - Z - 1))
                act.wait_ge(q_done, done(at - Z))
                apart(act, g)
                act.activation(zz[:, :], qv[:, k, :], ACT.Ln, bias=eps_z, scale=ksum[:, bass.ds(k, 1)]).then_inc(ln_done, 1)
                act.wait_ge(ln_done, done(at - Z))
                apart(act, g)
                act.activation(zz[:, :], zz[:, :], ACT.Exp, bias=ln_eps_z, scale=-1.0).then_inc(z_done, 1)
            if there[LN2]:
                b = in_block[LN2]
                act.wait_ge(u2_mm, done(at - LN2))
                apart(act, g)
                act.activation(xw[:, seq(n, LN2), :], bank[:, T2, :], ACT.Identity, bias=col("ln2_b", b), scale=col("ln2_s", b)).then_inc(x_done, 1)

        block_loop(act, step)

    @block.vector
    def _(dve):
        dve.memset(eps_z, EPS_Z)
        dve.memset(ln_eps_z, float(np.log(EPS_Z)))
        dve.memset(mhalf[:, :], -0.5).then_inc(cst_done, 1)
        dve.wait_ge(rows_T, 1)
        dve.tensor_copy(cols[:, :], bank[:, 7, 0:NROWS]).then_inc(cols_done, 1)
        for s in (x1_done, x1_hi_done, x1_split, k_done, e_done, kv_done, q_done, coef, rec, va_done, v_done, bn1_done, bn2_done, mv1_done, mv2_done, xn1_done, xn2_done):
            dve.sem_inc(s, BEGIN)

        def norm(src, dst, i, count):
            for c in range(C):
                last = dve.tensor_scalar(dst[:, c, :], tiles(src)[:, c, :], mv[:, i, c, 0:1], rstd[:, i, c:c + 1], ALU.subtract, ALU.mult)
            last.then_inc(count, 1)

        def step(blk, n):
            at = blk * B + n
            there = [has(blk, n, lag) for lag in range(LN2 + 1)]
            if there[LN1]:
                dve.wait_ge(t1_mm, done(at - LN1))
                layer_stats(dve, g, tiles(T1), st[:, 0], mv[:, 0], bn1_done, done(at - LN1), mv1_done)
            if there[LN2]:
                dve.wait_ge(t2_mm, done(at - LN2))
                layer_stats(dve, g, tiles(T2), st[:, 1], mv[:, 1], bn2_done, done(at - LN2), mv2_done)
            if there[LN1]:
                dve.wait_ge(rs1_done, done(at - LN1))
                dve.wait_ge(u1_mm, done(at - LN1 - 1))
                norm(T1, xn1, 0, xn1_done)
            if there[LN2]:
                dve.wait_ge(rs2_done, done(at - LN2))
                dve.wait_ge(u2_mm, done(at - LN2 - 1))
                norm(T2, xn2, 1, xn2_done)
            if there[LN1]:
                j, k, b = at - LN1, seq(n, LN1), block_of(blk, n, LN1)
                dve.wait_ge(u1_mm, done(j))
                dve.tensor_scalar(xw[:, k, :], bank[:, T1, :], col("ln1_s", b), col("ln1_b", b), ALU.mult, ALU.add).then_inc(x1_done, 1)
                dve.wait_ge(x1_done, done(j))
                dve.wait_ge(h_mm, part_done(j - 1, FT - 1))
                apart(dve, g)
                dve.tensor_copy(x1_hi[:, :], xw[:, k, :]).then_inc(x1_hi_done, 1)
                dve.wait_ge(x1_hi_done, done(j))
                dve.tensor_tensor(x1_lo[:, :], xw[:, k, :], x1_hi[:, :].bitcast(F32), ALU.subtract).then_inc(x1_split, 1)
            if isinstance(n, int) and n == FF - 1 and there[QKV]:
                dve.wait_ge(w_f1_in, (blk + 1) * 16)
                dve.tensor_copy(w_f1_hi[:, :], w_f1[:, :]).then_inc(w_hi_done, 1)
                dve.wait_ge(w_hi_done, blk + 1)
                dve.tensor_tensor(w_f1_lo[:, :], w_f1[:, :], w_f1_hi[:, :].bitcast(F32), ALU.subtract).then_inc(w_f1_split, 1)
            if there[ACTS]:
                j, k, b = at - ACTS, seq(n, ACTS), block_of(blk, n, ACTS)
                one = bass.ds(k, 1)
                dve.wait_ge(er_done, done(j))
                dve.wait_ge(kv_done, done(j - 1))
                dve.scalar_tensor_tensor(out=kk[:, :], in0=ex[:, 1, :], scalar=1.0, in1=re[:, 1, :],
                                         op0=ALU.min, op1=ALU.add, accum_out=ksum[:, one]).then_inc(k_done, 1)
                dve.tensor_scalar(ex[:, 0, :], ex[:, 0, :], 1.0, -1.0, ALU.min, ALU.add).then_inc(e_done, 1)
                dve.wait_ge(k_done, done(j))
                dve.wait_ge(v_mm, done(j))
                dve.scalar_tensor_tensor(out=junk[:, :], in0=bank[:, VB, :], scalar=col("bv", b), in1=kk[:, :],
                                         op0=ALU.add, op1=ALU.mult, accum_out=kvsum[:, one]).then_inc(kv_done, 1)
                dve.tensor_scalar(rks[:, one], ksum[:, one], TINY, None, ALU.max).then_inc(coef, 1)
                dve.wait_ge(e_done, done(j))
                dve.scalar_tensor_tensor(out=qv[:, k, :], in0=ex[:, 0, :], scalar=1.0, in1=re[:, 0, :],
                                         op0=ALU.add, op1=ALU.add).then_inc(q_done, 1)
            if there[Z]:
                old = bass.ds(seq(n, Z), 1)
                dve.wait_ge(z_done, done(at - Z))
                dve.wait_ge(va_done, done(at - Z))
                dve.tensor_scalar(qv[:, seq(n, Z), :], zz[:, :], nva[:, old], va[:, old], ALU.mult, ALU.add).then_inc(v_done, 1)
            if there[ACTS]:
                dve.wait_ge(coef, done(j))
                apart(dve, g)
                dve.reciprocal(rks[:, one], rks[:, one]).then_inc(rec, 1)
                dve.wait_ge(rec, done(j))
                dve.tensor_tensor(va[:, one], kvsum[:, one], rks[:, one], ALU.mult)
                dve.scalar_tensor_tensor(out=nva[:, one], in0=kvsum[:, one], scalar=-1.0,
                                         in1=rks[:, one], op0=ALU.mult, op1=ALU.mult).then_inc(va_done, 1)

        block_loop(dve, step)

    @block.gpsimd
    def _(pool):
        for s in (y1_done, y2_done, ve1_done, ve2_done, rs1_done, rs2_done):
            pool.sem_inc(s, BEGIN)
        pool.wait_ge(cst_done, 1)

        def rs(i, mv_s, ve_s, rs_s, count):
            pool.wait_ge(mv_s, count)
            apart(pool, g)
            pool.tensor_scalar(ve[:, i, :], mv[:, i, :, 1], EPS_LN1, None, ALU.add).then_inc(ve_s, 1)
            pool.wait_ge(ve_s, count)
            pool.tensor_tensor(rstd[:, i, :], ve[:, i, :], mhalf[:, :], ALU.pow).then_inc(rs_s, 1)

        def step(blk, n):
            at = blk * B + n
            if has(blk, n, LN1):
                rs(0, mv1_done, ve1_done, rs1_done, done(at - LN1))
            if has(blk, n, LN2):
                rs(1, mv2_done, ve2_done, rs2_done, done(at - LN2))
            if has(blk, n, FF_OUT):
                pool.wait_ge(ff_done, done(at - FF_OUT))
                pool.wait_ge(t2_mm, done(at - FF_OUT - 1))
                pool.tensor_tensor(y2[:, :], ffo[:, :], xw[:, seq(n, FF_OUT), :], ALU.add).then_inc(y2_done, 1)
            if has(blk, n, WO):
                pool.wait_ge(att_done, done(at - WO))
                pool.wait_ge(t1_mm, done(at - WO - 1))
                pool.tensor_tensor(y1[:, :], att[:, :], xw[:, seq(n, WO), :], ALU.add).then_inc(y1_done, 1)

        block_loop(pool, step)


L_DEPTH, L_HEADS, L_DH, L_WIN = 2, 8, 64, 64
L_INNER = L_HEADS * L_DH
L_HID = int(D * 4 * 2 / 3)
HT = -(-L_HID // P)
EPS_NORM, EPS_LN = 1e-24, 1e-5
MASKED = -1e30
CHUNKS = B * C


def chunk_range(i, c, lag):
    return not isinstance(i, int) or 0 <= C * i + c - lag < CHUNKS


def chunk_of(i, c, lag):
    d = c - lag
    return i + d // C, d % C


def chunk_loop(eng, step, depth):
    for c in range(C):
        step(0, c)
    with eng.Fori(1, B) as i:
        for c in range(C):
            step(i, c)
    for c in range(depth):
        step(B, c)


def seq_loop(eng, step, depth):
    for n in range(depth):
        step(n)
    with eng.Fori(depth, B - 1) as n:
        step(n)
    for n in range(B - 1, B + depth):
        step(n)


def local_tables():
    f = np.float32
    half = np.arange(0, L_DH, 2, dtype=f)
    inv = (f(1.0) / f(10000.0) ** (half / f(L_DH))).astype(f)
    t = np.arange(T, dtype=f)
    fr = (t[:, None] * inv[None, :]).astype(f).astype(np.float64)
    fr = np.concatenate([fr, fr], -1)
    base = ((half + f(0.4 * L_DH)) / f(1.4 * L_DH)).astype(f).astype(np.float64)
    power = (t.astype(np.float64) - T // 2) / float(L_WIN // 2)
    s = base[None, :] ** power[:, None]
    s = np.concatenate([s, s], -1)
    sign = np.concatenate([-np.ones(L_DH // 2), np.ones(L_DH // 2)])
    tab = np.stack([8.0 * np.cos(fr) * s, 8.0 * np.sin(fr) * s * sign, np.cos(fr) / s, np.sin(fr) / s * sign], 1)
    tab = tab.reshape(C, P, 4, L_DH).transpose(1, 0, 2, 3).astype(f)
    i, j = np.arange(P)[:, None], np.arange(P + L_WIN)[None, :] - L_WIN
    band = np.where((i < j) | (i > j + L_WIN), f(MASKED), f(0)).astype(f)
    return np.ascontiguousarray(tab), band


def l1_local(nc, ctx, g, w):
    def sb(name, shape, dtype=F32):
        return ctx.enter_context(nc.sbuf_tensor("l1_" + name, shape, dtype))

    def sem(name):
        return phase_semaphore(nc, g, "l1_" + name)

    xw, ident, bank = g.xw, g.ident, g.bank
    w_qkv = sb("w_qkv", [P, 3, L_INNER])
    w_qkv_hi, w_qkv_lo = sb("w_qkv_hi", [P, 3, L_INNER], F32R), sb("w_qkv_lo", [P, 3, L_INNER], F32R)
    w_1_hi, w_1_lo = sb("w_1_hi", [P, 2 * L_HID], F32R), sb("w_1_lo", [P, 2 * L_HID], F32R)
    w_o = sb("w_o", [P, C, D])
    w_1 = sb("w_1", [P, 2 * L_HID])
    w_2 = sb("w_2", [P, HT, D])
    tab0 = sb("tab0", [P, C, 4, L_DH])
    tab = sb("tab", [P, C, 4, L_DH])
    band = sb("band", [P, P + L_WIN])
    qks = sb("qks", [P, 2, L_DH])
    NR = 6 + 3
    rows = sb("rows", [NR * L_DEPTH, P])
    cols = sb("cols", [P, L_DEPTH, NR])
    hs_hi, hs_lo = sb("hs_hi", [P, 2, P], F32R), sb("hs_lo", [P, 2, P], F32R)
    sq = sb("sq", [P, 2, L_INNER])
    ra = sb("ra", [P, 2, L_INNER])
    rb = sb("rb", [P, 2, L_INNER])
    ss = sb("ss", [P, 16])
    rs = sb("rs", [P, 16])
    mhalf = sb("mhalf", [P, 16])
    qn = sb("qn", [P, 2, L_INNER])
    qT = sb("qT", [P, 4, P])
    kT = sb("kT", [P, 4, L_WIN + T])
    vt = sb("vt", [P, C, L_INNER])
    sm = sb("sm", [P, L_HEADS, P + L_WIN])
    mx = sb("mx", [P, L_HEADS])
    nmx = sb("nmx", [P, L_HEADS])
    psum = sb("psum", [P, 2, L_HEADS])
    rsum = sb("rsum", [P, L_HEADS])
    pb = sb("pb", [P, 2, L_HEADS, 2 * P])
    pt = sb("pt", [P, 4, 4, P])
    on = sb("on", [P, L_INNER])
    oT = sb("oT", [P, 4, P])
    y = sb("y", [P, T])
    st = sb("st", [P, C, 6])
    mv = sb("mv", [P, C, 2])
    ve = sb("ve", [P, C])
    rstd = sb("rstd", [P, C])
    xn = sb("xn", [P, C, D])
    hn = sb("hn", [P, T])
    hn_hi, hn_lo = sb("hn_hi", [P, T], F32R), sb("hn_lo", [P, T], F32R)
    gl = sb("gl", [P, HT, T])
    hm = sb("hm", [P, HT, T])

    split_hi = sem("split_hi")
    wa_split = sem("wa_split")
    wb_split = sem("wb_split")
    hs_hi_done = sem("hs_hi_done")
    hn_split = sem("hn_split")
    cst_in = sem("cst_in")
    wa_in = sem("wa_in")
    wb_in = sem("wb_in")
    sc_in = sem("sc_in")
    rows_z = sem("rows_z")
    rows_in = sem("rows_in")
    rows_T = sem("rows_T")
    cols_done = sem("cols_done")
    tabs = sem("tabs")
    zero_done = sem("zero_done")
    hs_done = sem("hs_done")
    q_mm = sem("q_mm")
    k_mm = sem("k_mm")
    v_mm = sem("v_mm")
    sqq_done = sem("sqq_done")
    sq_done = sem("sq_done")
    ab_done = sem("ab_done")
    ss_done = sem("ss_done")
    sm_done = sem("sm_done")
    cl_done = sem("cl_done")
    rs_done = sem("rs_done")
    qnq_done = sem("qnq_done")
    qn_done = sem("qn_done")
    tq_mm = sem("tq_mm")
    tq_ev = sem("tq_ev")
    tk_mm = sem("tk_mm")
    tk_ev = sem("tk_ev")
    v_ev = sem("v_ev")
    slo_mm = sem("slo_mm")
    shi_mm = sem("shi_mm")
    mlo_done = sem("mlo_done")
    mhi_done = sem("mhi_done")
    n_done = sem("n_done")
    nlo_done = sem("nlo_done")
    elo_done = sem("elo_done")
    ehi_done = sem("ehi_done")
    pt_mm = sem("pt_mm")
    pt_ev = sem("pt_ev")
    pv_mm = sem("pv_mm")
    rc_done = sem("rc_done")
    on_done = sem("on_done")
    ot_mm = sem("ot_mm")
    ot_ev = sem("ot_ev")
    wo_mm = sem("wo_mm")
    res_done = sem("res_done")
    y_done = sem("y_done")
    t_mm = sem("t_mm")
    bn_done = sem("bn_done")
    mv_done = sem("mv_done")
    ve_done = sem("ve_done")
    rstd_done = sem("rstd_done")
    xn_done = sem("xn_done")
    u_mm = sem("u_mm")
    hn_done = sem("hn_done")
    g_mm = sem("g_mm")
    a_mm = sem("a_mm")
    gl_done = sem("gl_done")
    hm_done = sem("hm_done")
    f2_mm = sem("f2_mm")
    x_done = sem("x_done")
    Q, K, O, MIX, S0, R0 = 0, 1, 2, 3, 4, 6

    def widths(k):
        return min(P, L_HID - k * P)

    block = ctx.enter_context(nc.Block())

    def heads_of(half, r):
        return [4 * half + r, 4 * half + 2 + r]

    @block.sync
    def _(sp):
        sp.dma_start(tab0[:, :, :, :], w["tab"]).then_inc(cst_in, 16)
        sp.dma_start(band[:, :], w["band"]).then_inc(cst_in, 16)
        sp.wait_ge(rows_z, 1)
        for l in range(L_DEPTH):
            r = l * NR
            for k in range(HT):
                sp.dma_start(rows[r + k:r + k + 1, 0:widths(k)], w["b1"][l:l + 1, k * P:k * P + widths(k)]).then_inc(rows_in, 16)
                sp.dma_start(rows[r + 3 + k:r + 4 + k, 0:widths(k)],
                             w["b1"][l:l + 1, L_HID + k * P:L_HID + k * P + widths(k)]).then_inc(rows_in, 16)
            for k, name in enumerate(["b2", "ln_g", "ln_b"]):
                sp.dma_start(rows[r + 6 + k:r + 7 + k, :], w[name][l:l + 1, :]).then_inc(rows_in, 16)

        def load(l):
            sp.dma_start(w_qkv[:, :, :], w["wqkv"][bass.ds(l, 1), :, :].rearrange("l p (t n) -> p (l t) n", t=3)).then_inc(wa_in, 16)
            sp.dma_start(w_o[:, :, :], w["wo"][bass.ds(l, 1), :, :].rearrange("l (k p) n -> p (l k) n", p=P)).then_inc(wa_in, 16)
            sp.dma_start(qks[:, 0, :], w["q_scale"][bass.ds(l, 1), :].partition_broadcast(P)).then_inc(sc_in, 16)
            sp.dma_start(qks[:, 1, :], w["k_scale"][bass.ds(l, 1), :].partition_broadcast(P)).then_inc(sc_in, 16)

        def load_ff(l):
            sp.dma_start(w_1[:, :], w["w1"][bass.ds(l, 1), :, :].rearrange("l p n -> (l p) n")).then_inc(wb_in, 16)
            sp.dma_start(w_2[:, 0:2, :], w["w2"][bass.ds(l, 1), 0:2 * P, :].rearrange("l (k p) n -> p (l k) n", p=P)).then_inc(wb_in, 16)
            sp.dma_start(w_2[0:widths(2), 2, :], w["w2"][bass.ds(l, 1), 2 * P:L_HID, :].rearrange("l p n -> (l p) n")).then_inc(wb_in, 16)
        load(0)
        load_ff(0)
        sp.wait_ge(res_done, CHUNKS + START)
        load(1)
        sp.wait_ge(f2_mm, B + 1)
        load_ff(1)

    @block.tensor
    def _(pe):
        for x in (q_mm, k_mm, v_mm, tq_mm, tk_mm, slo_mm, shi_mm, pt_mm, pv_mm, ot_mm, wo_mm, t_mm, u_mm, g_mm, a_mm, f2_mm):
            pe.sem_inc(x, 1)
        pe.wait_ge(rows_in, 16 * NR * L_DEPTH)
        pe.transpose(bank[:, 7, 0:NR * L_DEPTH], rows[:, :], ident[0:NR * L_DEPTH, 0:NR * L_DEPTH]).then_inc(rows_T, 1)
        pe.wait_ge(cols_done, 1)
        pe.wait_ge(zero_done, 1)
        with pe.Fori(0, L_DEPTH) as l:
            base = l * CHUNKS
            sbase = l * B

            def step_a(i, c):
                at = base + (i * C + c)

                def transposes(bk, src, blocks):
                    for j, b in blocks:
                        mm = pe.transpose(bank[:, bk, j * P:(j + 1) * P], src(b), ident[:, :])
                    return mm

                def scores(half):
                    cc = (c - 1) % C
                    lo = L_WIN if cc == 0 else 0
                    n = P + L_WIN - lo
                    for r in range(2):
                        for j, h in enumerate(heads_of(half, r)):
                            mm = pe.matmul(bank[:, S0 + r, j * 192:j * 192 + n], qT[64 * r:64 * r + 64, h // 2, :],
                                           kT[64 * r:64 * r + 64, h // 2, cc * P + lo:cc * P + lo + n], start=True, stop=True)
                    return mm

                def probs_T(gp):
                    cc = (c - 2) % C
                    blocks = [(2 * hh + o, (2 * gp + hh, o)) for hh in range(2) for o in ((1,) if cc == 0 else (0, 1))]
                    transposes(R0 + (1, 1, 0, 1)[gp], lambda b: pb[:, c % 2, b[0], b[1] * P:(b[1] + 1) * P], blocks).then_inc(pt_mm, 1)

                def values(gp):
                    cc = (c - 2) % C
                    pe.wait_ge(pt_ev, (at - 2) * 4 + (gp + 1 + 4 * START))
                    for hh in range(2):
                        h = 2 * gp + hh
                        o = bank[:, O, h * L_DH:(h + 1) * L_DH]
                        mm = pe.matmul(o, pt[:, gp, 2 * hh + 1, :], vt[:, cc, h * L_DH:(h + 1) * L_DH], start=True, stop=(cc == 0))
                        if cc:
                            mm = pe.matmul(o, pt[:, gp, 2 * hh, :], vt[:, cc - 1, h * L_DH:(h + 1) * L_DH], start=False, stop=True)
                    return mm

                one, two, three, now = (chunk_range(i, c, k) for k in (1, 2, 3, 0))
                if one:
                    pe.wait_ge(qnq_done, at + START)
                    pe.wait_ge(v_ev, at + START)
                    transposes(MIX, lambda b: qn[:, 0, b * P:(b + 1) * P], [(b, b) for b in range(4)]).then_inc(tq_mm, 1)
                if now:
                    pe.wait_ge(hs_done, at + (1 + START))
                    pe.wait_ge(sq_done, at + START)
                    pe.wait_ge(ab_done, at + START)
                    split_matmul(pe, bank[:, Q, :], (hs_hi[:, c % 2, :], hs_lo[:, c % 2, :]), (w_qkv_hi[:, 0, :], w_qkv_lo[:, 0, :])).then_inc(q_mm, 1)
                if one:
                    pe.wait_ge(qn_done, at + START)
                    pe.wait_ge(tq_ev, at + START)
                    transposes(MIX, lambda b: qn[:, 1, b * P:(b + 1) * P], [(b, b) for b in range(4)]).then_inc(tk_mm, 1)
                if now:
                    split_matmul(pe, bank[:, K, :], (hs_hi[:, c % 2, :], hs_lo[:, c % 2, :]), (w_qkv_hi[:, 1, :], w_qkv_lo[:, 1, :])).then_inc(k_mm, 1)
                if three:
                    pe.wait_ge(on_done, at + (START - 2))
                    pe.wait_ge(pt_ev, (at - 3) * 4 + (3 + 4 * START))
                    transposes(R0, lambda b: on[:, b * P:(b + 1) * P], [(b, b) for b in range(4)]).then_inc(ot_mm, 1)
                if two:
                    pe.wait_ge(elo_done, at + (START - 1))
                    pe.wait_ge(pt_ev, (at - 3) * 4 + (4 + 4 * START))
                    probs_T(0)
                if now:
                    pe.wait_ge(tk_ev, at + START)
                    split_matmul(pe, bank[:, MIX, :], (hs_hi[:, c % 2, :], hs_lo[:, c % 2, :]), (w_qkv_hi[:, 2, :], w_qkv_lo[:, 2, :])).then_inc(v_mm, 1)
                if three:
                    pe.wait_ge(ot_ev, at + (START - 2))
                    for k in range(4):
                        mm = pe.matmul(bank[:, R0, 0:P], w_o[:, k, :], oT[:, k, :], start=(k == 0), stop=(k == 3))
                    mm.then_inc(wo_mm, 1)
                if one:
                    pe.wait_ge(tk_ev, at + START)
                    pe.wait_ge(mhi_done, at + (START - 1))
                    scores(0).then_inc(slo_mm, 1)
                if two:
                    pe.wait_ge(pt_ev, (at - 2) * 4 + (1 + 4 * START))
                    probs_T(1)
                    pe.wait_ge(on_done, at + (START - 2))
                    values(0)
                    pe.wait_ge(res_done, at + (START - 2))
                    pe.wait_ge(ehi_done, at + (START - 1))
                    probs_T(2)
                    values(1)
                if one:
                    pe.wait_ge(mlo_done, at + START)
                    scores(1).then_inc(shi_mm, 1)
                if two:
                    probs_T(3)
                    values(2)
                    values(3).then_inc(pv_mm, 1)

            pe.wait_ge(wa_in, (l + 1) * 32)
            pe.wait_ge(wa_split, l + 1)
            pe.wait_ge(x_done, sbase + START)
            chunk_loop(pe, step_a, 3)

            def step_b(n):
                at = sbase + n
                if in_range(n, 0):
                    pe.wait_ge(y_done, at + (1 + START))
                    pe.wait_ge(xn_done, at + START)
                    for c in range(C):
                        mm = pe.transpose(bank[:, 0, c * P:(c + 1) * P], y[:, c * P:(c + 1) * P], ident[:, :])
                    mm.then_inc(t_mm, 1)
                if in_range(n, 1):
                    pe.wait_ge(hn_split, at + START)
                    for k in range(HT):
                        m = widths(k)
                        b = 2 + 2 * (k % 2)
                        pe.wait_ge(hm_done, (at - 1) * HT + (k - 2 + 1 + HT * START))
                        for bk, lo, mm in ((b, L_HID + k * P, g_mm), (b + 1, k * P, a_mm)):
                            split_matmul(pe, bank[0:m, bk, :], (w_1_hi[:, lo:lo + m], w_1_lo[:, lo:lo + m]), (hn_hi[:, :], hn_lo[:, :])).then_inc(mm, 1)
                if in_range(n, 0):
                    pe.wait_ge(xn_done, at + (1 + START))
                    pe.wait_ge(hn_done, at + START)
                    for c in range(C):
                        mm = pe.transpose(bank[:, 1, c * P:(c + 1) * P], xn[:, c, :], ident[:, :])
                    mm.then_inc(u_mm, 1)
                if in_range(n, 1):
                    pe.wait_ge(x_done, at + (START - 1))
                    for k in range(HT):
                        m = widths(k)
                        pe.wait_ge(hm_done, (at - 1) * HT + (k + 1 + HT * START))
                        mm = pe.matmul(bank[:, 6, :], w_2[0:m, k, :], hm[0:m, k, :], start=(k == 0), stop=(k == HT - 1))
                    mm.then_inc(f2_mm, 1)

            pe.wait_ge(wb_in, (l + 1) * 48)
            pe.wait_ge(wb_split, l + 1)
            pe.wait_ge(res_done, base + (CHUNKS + START))
            pe.wait_ge(on_done, base + (CHUNKS + START))
            seq_loop(pe, step_b, 1)

    @block.scalar
    def _(act):
        for x in (sq_done, tq_ev, tk_ev, v_ev, elo_done, ehi_done, ot_ev, hn_done):
            act.sem_inc(x, START)
        act.sem_inc(pt_ev, 4 * START)
        act.sem_inc(gl_done, HT * START)
        act.wait_ge(cols_done, 1)
        with act.Fori(0, L_DEPTH) as l:
            base = l * CHUNKS
            sbase = l * B
            nc.scalar.preload_act_table_set("exp_and_others")

            def step_a(i, c):
                at = base + (i * C + c)
                one, two, three, now = (chunk_range(i, c, k) for k in (1, 2, 3, 0))

                def exps(half, lag, wait, done):
                    cc = (c - lag) % C
                    lo = L_WIN if cc == 0 else 0
                    act.wait_ge(wait, at + (START + 1 - lag))
                    for h in range(4 * half, 4 * half + 4):
                        a = act.activation(pb[:, (c + lag) % 2, h, L_WIN + lo:], sm[:, h, lo:], ACT.Exp, bias=nmx[:, h:h + 1],
                                           accum_out=psum[:, (c + lag) % 2, h:h + 1])
                    a.then_inc(done, 1)

                def probs(gp):
                    cc = (c - 2) % C
                    act.wait_ge(pt_mm, (at - 2) * 4 + (gp + 2))
                    src = bank[:, R0 + (1, 1, 0, 1)[gp], :].rearrange("p (h o q) -> p h o q", h=2, o=2)
                    dst = pt[:, gp, :, :].rearrange("p (h o) q -> p h o q", h=2)
                    o = 1 if cc == 0 else 0
                    act.copy(dst[:, :, o:, :], src[:, :, o:, :]).then_inc(pt_ev, 1)

                if one:
                    act.wait_ge(tq_mm, at + 1)
                    act.copy(qT[:, :, :], bank[:, MIX, :].rearrange("p (a b) -> p a b", a=4)).then_inc(tq_ev, 1)
                if now:
                    act.wait_ge(q_mm, at + 2)
                    act.wait_ge(ss_done, at + START)
                    act.activation(sq[:, 0, :], bank[:, Q, :], ACT.Square).then_inc(sqq_done, 1)
                if one:
                    cc = (c - 1) % C
                    act.wait_ge(tk_mm, at + 1)
                    act.copy(kT[:, :, L_WIN + cc * P:L_WIN + (cc + 1) * P], bank[:, MIX, :].rearrange("p (a b) -> p a b", a=4)).then_inc(tk_ev, 1)
                if now:
                    act.wait_ge(k_mm, at + 2)
                    act.activation(sq[:, 1, :], bank[:, K, :], ACT.Square).then_inc(sq_done, 1)
                if three:
                    act.wait_ge(ot_mm, at - 1)
                    act.copy(oT[:, :, :], bank[:, R0, :].rearrange("p (a b) -> p a b", a=4)).then_inc(ot_ev, 1)
                if two:
                    probs(0)
                if now:
                    act.wait_ge(v_mm, at + 2)
                    act.copy(vt[:, c, :], bank[:, MIX, :]).then_inc(v_ev, 1)
                if two:
                    exps(1, 2, n_done, ehi_done)
                    probs(1)
                    probs(2)
                if one:
                    exps(0, 1, nlo_done, elo_done)
                if two:
                    probs(3)

            chunk_loop(act, step_a, 3)
            nc.scalar.preload_act_table_set("gelu_and_others")

            def step_b(n):
                at = sbase + n
                if in_range(n, 1):
                    for k in range(HT):
                        m = widths(k)
                        act.wait_ge(g_mm, (at - 1) * HT + (k + 2))
                        act.wait_ge(hm_done, (at - 2) * HT + (k + 1 + HT * START))
                        apart(act, g)
                        act.activation(gl[0:m, k, :], bank[0:m, 2 + 2 * (k % 2), :], ACT.Gelu, bias=cols[0:m, bass.ds(l, 1), 3 + k]).then_inc(gl_done, 1)
                if in_range(n, 0):
                    act.wait_ge(u_mm, at + 2)
                    act.wait_ge(a_mm, at * HT + 1)
                    apart(act, g)
                    act.wait_ge(hn_split, at + START)
                    apart(act, g)
                    act.activation(hn_hi[:, :], bank[:, 1, :], ACT.Identity, bias=cols[:, bass.ds(l, 1), 8], scale=cols[:, bass.ds(l, 1), 7])
                    act.activation(hn[:, :], bank[:, 1, :], ACT.Identity, bias=cols[:, bass.ds(l, 1), 8], scale=cols[:, bass.ds(l, 1), 7]).then_inc(hn_done, 1)

            seq_loop(act, step_b, 1)

    @block.vector
    def _(dve):
        dve.memset(mhalf[:, :], -0.5)
        dve.memset(rows[:, :], 0.0).then_inc(rows_z, 1)
        dve.memset(kT[:, :, 0:L_WIN], 0.0)
        dve.memset(y[:, :], 0.0)
        dve.memset(pb[:, :, :, :], 0.0).then_inc(zero_done, 1)
        dve.wait_ge(rows_T, 1)
        dve.tensor_copy(cols[:, :, :], bank[:, 7, 0:NR * L_DEPTH].rearrange("p (l r) -> p l r", l=L_DEPTH)).then_inc(cols_done, 1)
        for x in (sm_done, hs_hi_done, hn_split, ab_done, ss_done, qnq_done, qn_done, mlo_done, mhi_done, n_done, nlo_done, on_done, res_done, xn_done, x_done, hs_done, y_done):
            dve.sem_inc(x, START)
        dve.sem_inc(hm_done, HT * START)
        with dve.Fori(0, L_DEPTH) as l:
            base = l * CHUNKS
            sbase = l * B

            def step_a(i, c):
                at = base + (i * C + c)
                one, two, three, now = (chunk_range(i, c, k) for k in (1, 2, 3, 0))

                def rotate(bk, qk):
                    x = bank[:, bk, :].rearrange("p (h d) -> p h d", h=L_HEADS)
                    x4 = bank[:, bk, :].rearrange("p (h t d) -> p h t d", h=L_HEADS, t=2)
                    cs = tab[:, c, 2 * qk, :].unsqueeze(1).broadcast_to([P, L_HEADS, L_DH])
                    sn = tab[:, c, 2 * qk + 1, :].unsqueeze(1).broadcast_to([P, L_HEADS, L_DH])
                    dve.tensor_tensor(ra[:, qk, :].rearrange("p (h d) -> p h d", h=L_HEADS), x, cs, ALU.mult)
                    return dve.tensor_tensor(rb[:, qk, :].rearrange("p (h t d) -> p h t d", h=L_HEADS, t=2), x4[:, :, ::-1, :],
                                             sn.rearrange("p h (t d) -> p h t d", t=2), ALU.mult)

                def masked_max(half, mm, freed, m_done, neg_done):
                    cc = (c - 1) % C
                    lo = L_WIN if cc == 0 else 0
                    n = P + L_WIN - lo
                    dve.wait_ge(mm, at + 1)
                    dve.wait_ge(freed, at + (START - 1))
                    apart(dve, g)
                    for r in range(2):
                        for j, h in enumerate(heads_of(half, r)):
                            x = dve.tensor_tensor_reduce(sm[:, h, lo:], bank[:, S0 + r, j * 192:j * 192 + n], band[:, lo:], 1.0, MASKED * 2,
                                                         ALU.add, ALU.max, mx[:, h:h + 1])
                    x.then_inc(m_done, 1)
                    dve.wait_ge(m_done, at + START)
                    dve.tensor_scalar(nmx[:, 4 * half:4 * half + 4], mx[:, 4 * half:4 * half + 4], -1.0, None, ALU.mult).then_inc(neg_done, 1)

                def shift_in(c, count):
                    t0, p = c * P, c % 2
                    dve.wait_ge(v_ev, count)
                    low, high = xw[0:64, i, t0:t0 + P], xw[64:P, i, max(t0 - 1, 0):t0 + P - 1]
                    first = 1 if c == 0 else 0
                    dve.tensor_copy(hs_hi[0:64, p, :], low)
                    dve.tensor_copy(hs_hi[64:P, p, first:P], high).then_inc(hs_hi_done, 1)
                    if c == 0:
                        dve.memset(hs_hi[64:P, p, 0:1].bitcast(F32), 0.0)
                        dve.memset(hs_lo[64:P, p, 0:1].bitcast(F32), 0.0)
                    dve.wait_ge(hs_hi_done, count + 2)
                    dve.tensor_tensor(hs_lo[0:64, p, :], low, hs_hi[0:64, p, :].bitcast(F32), ALU.subtract)
                    dve.tensor_tensor(hs_lo[64:P, p, first:P], high, hs_hi[64:P, p, first:P].bitcast(F32), ALU.subtract).then_inc(hs_done, 1)

                def scaled(qk):
                    return dve.tensor_tensor(qn[:, qk, :].rearrange("p (h d) -> p h d", d=L_DH), ra[:, qk, :].rearrange("p (h d) -> p h d", d=L_DH),
                                             rs[:, qk * L_HEADS:(qk + 1) * L_HEADS].unsqueeze(2).broadcast_to([P, L_HEADS, L_DH]), ALU.mult)

                if now:
                    if c == 0:
                        shift_in(0, at + (START - 1))
                    dve.wait_ge(sqq_done, at + 1)
                    dve.wait_ge(sm_done, at + START)
                    dve.wait_ge(qn_done, at + START)
                    rotate(Q, 0)
                    dve.wait_ge(sq_done, at + (1 + START))
                    dve.wait_ge(rs_done, at + START)
                    dve.tensor_reduce(ss[:, :], sq[:, :, :].rearrange("p t (h d) -> p (t h) d", d=L_DH), AX.X, ALU.add).then_inc(ss_done, 1)
                    rotate(K, 1).then_inc(ab_done, 1)
                if three:
                    n3, c3 = chunk_of(i, c, 3)
                    dve.wait_ge(wo_mm, at - 1)
                    x = xw[:, n3, c3 * P:(c3 + 1) * P]
                    dve.tensor_tensor(x, bank[:, R0, 0:P], x, ALU.add).then_inc(res_done, 1)
                if one:
                    masked_max(0, slo_mm, elo_done, mlo_done, nlo_done)
                if now:
                    dve.wait_ge(ab_done, at + (1 + START))
                    dve.tensor_tensor(ra[:, :, :], ra[:, :, :], rb[:, :, :], ALU.add).then_inc(sm_done, 1)
                if now and c < C - 1:
                    shift_in(c + 1, at + START)
                if now:
                    dve.wait_ge(rs_done, at + (1 + START))
                    dve.wait_ge(sm_done, at + (1 + START))
                    dve.wait_ge(tk_mm, at + 1)
                    scaled(0).then_inc(qnq_done, 1)
                    scaled(1).then_inc(qn_done, 1)
                if one:
                    masked_max(1, shi_mm, ehi_done, mhi_done, n_done)
                if two:
                    dve.wait_ge(ehi_done, at + (START - 1))
                    dve.reciprocal(rsum[:, :], psum[:, c % 2, :]).then_inc(rc_done, 1)
                    dve.wait_ge(rc_done, at - 1)
                    dve.wait_ge(pv_mm, at)
                    dve.wait_ge(ot_mm, at - 1)
                    dve.tensor_tensor(on[:, :].rearrange("p (h d) -> p h d", d=L_DH), bank[:, O, :].rearrange("p (h d) -> p h d", d=L_DH),
                                      rsum[:, :].unsqueeze(2).broadcast_to([P, L_HEADS, L_DH]), ALU.mult).then_inc(on_done, 1)

            def split(src, hi, lo, finished, turn):
                dve.tensor_copy(hi, src).then_inc(split_hi, 1)
                dve.wait_ge(split_hi, 2 * l + turn)
                dve.tensor_tensor(lo, src, hi.bitcast(F32), ALU.subtract).then_inc(finished, 1)

            dve.wait_ge(wa_in, (l + 1) * 32)
            split(w_qkv[:, :, :], w_qkv_hi[:, :, :], w_qkv_lo[:, :, :], wa_split, 1)
            dve.wait_ge(tabs, l + 1)
            chunk_loop(dve, step_a, 3)
            dve.wait_ge(wb_in, (l + 1) * 48)
            split(w_1[:, :], w_1_hi[:, :], w_1_lo[:, :], wb_split, 2)

            def norm(n, at):
                dve.wait_ge(rstd_done, at + 1)
                dve.wait_ge(u_mm, at + 1)
                for c in range(C):
                    last = dve.tensor_scalar(xn[:, c, :], bank[:, 0, c * P:(c + 1) * P], mv[:, c, 0:1], rstd[:, c:c + 1], ALU.subtract, ALU.mult)
                last.then_inc(xn_done, 1)

            def step_b(n):
                at = sbase + n
                def residual(n, at):
                    dve.wait_ge(f2_mm, at)
                    x = xw[:, n - 2, :]
                    dve.scalar_tensor_tensor(out=x, in0=bank[:, 6, :], scalar=cols[:, bass.ds(l, 1), 6], in1=x, op0=ALU.add, op1=ALU.add).then_inc(x_done, 1)

                def rest_of_hn(at):
                    dve.wait_ge(hn_done, at + (1 + START))
                    dve.tensor_tensor(hn_lo[:, :], hn[:, :], hn_hi[:, :].bitcast(F32), ALU.subtract).then_inc(hn_split, 1)

                def shift_in(n, count):
                    dve.wait_ge(t_mm, count + 1)
                    dve.tensor_copy(y[0:64, :], xw[0:64, n, :])
                    dve.tensor_copy(y[64:P, 1:T], xw[64:P, n, 0:T - 1]).then_inc(y_done, 1)

                if isinstance(n, int) and n == 0:
                    shift_in(0, at)
                if in_range(n, 0):
                    dve.wait_ge(t_mm, at + 2)
                    layer_stats(dve, g, bank[:, 0, :].rearrange("p (c d) -> p c d", c=C), st, mv, bn_done, at + 1, mv_done)
                if in_range(n, 1):
                    for k in range(HT):
                        m = widths(k)
                        if k == 1 and in_range(n, 0):
                            norm(n, at)
                        if k == 1 and in_range(n, 2):
                            residual(n, at)
                        dve.wait_ge(a_mm, (at - 1) * HT + (k + 2))
                        dve.wait_ge(gl_done, (at - 1) * HT + (k + 1 + HT * START))
                        dve.wait_ge(f2_mm, at)
                        dve.scalar_tensor_tensor(out=hm[0:m, k, :], in0=bank[0:m, 3 + 2 * (k % 2), :], scalar=cols[0:m, bass.ds(l, 1), k],
                                                 in1=gl[0:m, k, :], op0=ALU.add, op1=ALU.mult).then_inc(hm_done, 1)
                    if not isinstance(n, int) or n + 1 < B:
                        shift_in(n + 1, at + 1)
                    if in_range(n, 0):
                        rest_of_hn(at)
                elif in_range(n, 0):
                    norm(n, at)
                    shift_in(n + 1, at + 1)
                    rest_of_hn(at)
                elif in_range(n, 2):
                    residual(n, at)

            seq_loop(dve, step_b, 2)

    @block.gpsimd
    def _(pool):
        pool.sem_inc(rs_done, START)
        pool.wait_ge(cst_in, 32)
        with pool.Fori(0, L_DEPTH) as l:
            base = l * CHUNKS
            sbase = l * B

            def step_a(i, c):
                at = base + (i * C + c)
                if chunk_range(i, c, 0):
                    pool.wait_ge(ss_done, at + (1 + START))
                    pool.wait_ge(qn_done, at + START)
                    apart(pool, g)
                    pool.tensor_scalar(ss[:, :], ss[:, :], EPS_NORM, None, ALU.max).then_inc(cl_done, 1)
                    pool.wait_ge(cl_done, at + 1)
                    pool.tensor_tensor(rs[:, :], ss[:, :], mhalf[:, :], ALU.pow).then_inc(rs_done, 1)

            pool.wait_ge(sc_in, (l + 1) * 32)
            pool.wait_ge(qn_done, base + START)
            for qk in range(2):
                sc = qks[:, qk, :]
                swapped = sc.rearrange("p (t d) -> p t d", t=2)[:, ::-1, :].unsqueeze(1).broadcast_to([P, C, 2, L_DH // 2])
                pool.tensor_tensor(tab[:, :, 2 * qk, :], tab0[:, :, 2 * qk, :], sc.unsqueeze(1).broadcast_to([P, C, L_DH]), ALU.mult)
                last = pool.tensor_tensor(tab[:, :, 2 * qk + 1, :].rearrange("p c (t d) -> p c t d", t=2),
                                          tab0[:, :, 2 * qk + 1, :].rearrange("p c (t d) -> p c t d", t=2), swapped, ALU.mult)
            last.then_inc(tabs, 1)
            pool.wait_ge(x_done, sbase + START)
            chunk_loop(pool, step_a, 0)

            def step_b(n):
                at = sbase + n
                if in_range(n, 0):
                    pool.wait_ge(mv_done, at + 1)
                    apart(pool, g)
                    pool.tensor_scalar(ve[:, :], mv[:, :, 1], EPS_LN, None, ALU.add).then_inc(ve_done, 1)
                    pool.wait_ge(ve_done, at + 1)
                    pool.tensor_tensor(rstd[:, :], ve[:, :], mhalf[:, 0:C], ALU.pow).then_inc(rstd_done, 1)

            seq_loop(pool, step_b, 1)


R_HEADS = 8
R_DV = 2 * D // R_HEADS
R_DK = D // R_HEADS
V2 = 2 * D
EPS_GN = 1e-5


def retention_tables():
    f = np.float32
    half = D // 2
    sv = ((np.arange(0, D, 2, dtype=f) + f(0.4 * D)) / f(1.4 * D)).astype(f).astype(np.float64)
    pos = np.arange(T, dtype=f)
    scale = sv[None, :] ** (pos.astype(np.float64)[:, None] / 512.0)
    inv = (f(1.0) / f(10000.0) ** (np.arange(half, dtype=f) / f(half))).astype(f)
    ang = (pos[:, None] * inv[None, :]).astype(f).astype(np.float64)
    sin, cos = np.sin(ang), np.cos(ang)
    two = lambda a: np.repeat(a, 2, axis=-1)
    sign = np.tile([-1.0, 1.0], half)
    lin = np.linspace(np.log(1.0 / 32.0), np.log(1.0 / 512.0), R_HEADS).astype(f)
    gamma = (f(1.0) - np.exp(lin)).astype(f)
    ld = np.log(gamma).astype(f).astype(np.float64)
    t = np.arange(T, dtype=np.float64)
    norm = np.sqrt(np.cumsum(np.exp(ld[:, None] * t[None, :]), axis=1))
    fq = np.repeat(np.exp(ld[:, None] * t) / norm * R_DK ** -0.5, R_DK, axis=0).T
    fk = np.repeat(np.exp(-ld[:, None] * t), R_DK, axis=0).T
    tab = np.stack([two(cos * scale) * fq, two(sin * scale) * sign * fq, two(cos / scale) * fk, two(sin / scale) * sign * fk], 0)
    tab = tab.reshape(4, C, P, D).transpose(3, 1, 0, 2).astype(f)
    tri = (np.arange(P)[:, None] <= np.arange(P)[None, :]).astype(f)
    feat = np.arange(P)[:, None] // R_DK
    diag = (feat == np.arange(V2)[None, :] // R_DV).astype(f)
    heads = (feat == np.arange(R_HEADS)[None, :]).astype(f)
    return np.ascontiguousarray(tab), tri, diag, heads


def l0_retention(nc, ctx, g, w):
    def sb(name, shape):
        return ctx.enter_context(nc.sbuf_tensor("l0_" + name, shape, F32))

    def sem(name):
        return phase_semaphore(nc, g, "l0_" + name)

    x_all, xw, ident, bank = g.x, g.xw, g.ident, g.bank
    w_qkv = sb("w_qkv", [P, 4 * D])
    w_sw = sb("w_sw", [P, 2, D])
    w_vc = sb("w_vc", [P, V2])
    w_g = sb("w_g", [P, V2])
    w_p = sb("w_p", [P, 2, D])
    bv = sb("bv", [P, V2])
    bvc = sb("bvc", [P, V2])
    vmean = sb("vmean", [P, 2, R_HEADS])
    tab = sb("tab", [P, C, 4, P])
    tri = sb("tri", [P, P])
    diag = sb("diag", [P, V2])
    heads = sb("heads", [P, R_HEADS])
    NR = 7
    rows = sb("rows", [NR, P])
    cols = sb("cols", [P, NR])
    xt = sb("xt", [P, C, D])
    xs = sb("xs", [P, 2, P])
    r4 = sb("r4", [P, 4, P])
    qk = sb("qk", [P, 2, 2, P])
    q8 = sb("q8", [P, R_HEADS, P])
    sm = sb("sm", [P, R_HEADS, P])
    vt = sb("vt", [P, 2, V2])
    kt = sb("kt", [P, P])
    state = sb("state", [P, V2])
    sg = sb("sg", [P, C, 2, P])
    so = sb("so", [P, V2])
    ss = sb("ss", [P, R_HEADS])
    sv = sb("sv", [P, R_HEADS])
    rs = sb("rs", [P, R_HEADS])
    mhalf = sb("mhalf", [P, R_HEADS])
    on = sb("on", [P, V2])
    gated = sb("gated", [P, 2, P])

    w_in = sem("w_in")
    cst_in = sem("cst_in")
    rows_in = sem("rows_in")
    rows_T = sem("rows_T")
    cols_done = sem("cols_done")
    wc = sem("wc")
    mean_done = sem("mean_done")
    mh_done = sem("mh_done")
    x_in0 = sem("x_in0")
    x_in1 = sem("x_in1")
    x_in2 = sem("x_in2")
    x_in3 = sem("x_in3")
    xt_mm = sem("xt_mm")
    xs_done = sem("xs_done")
    xst_done = sem("xst_done")
    qk_mm = sem("qk_mm")
    r4_done = sem("r4_done")
    qk_done = sem("qk_done")
    q8_done = sem("q8_done")
    v_mm = sem("v_mm")
    v_done = sem("v_done")
    g_mm = sem("g_mm")
    sg_done = sem("sg_done")
    slo_mm = sem("slo_mm")
    shi_mm = sem("shi_mm")
    mlo_done = sem("mlo_done")
    mhi_done = sem("mhi_done")
    o_mm = sem("o_mm")
    kt_mm = sem("kt_mm")
    kt_done = sem("kt_done")
    kv_mm = sem("kv_mm")
    state_done = sem("state_done")
    sq_done = sem("sq_done")
    ss_done = sem("ss_done")
    sv_done = sem("sv_done")
    rs_done = sem("rs_done")
    on_done = sem("on_done")
    ont_mm = sem("ont_mm")
    gated_done = sem("gated_done")
    p_mm = sem("p_mm")
    p_done = sem("p_done")
    x_in = [x_in0, x_in1, x_in2, x_in3]
    X, QK, V, G, S, O, KV = 0, 1, 2, 3, 4, 6, 7
    block = ctx.enter_context(nc.Block())

    def lag_range(i, c):
        return [chunk_range(i, c, k) for k in range(4)]

    @block.sync
    def _(sp):
        for r, (a, b) in enumerate([(0, D), (D, 2 * D)]):
            sp.dma_start(rows[r:r + 1, :], w["b_qkv"][a:b].unsqueeze(0)).then_inc(rows_in, 16)
            sp.dma_start(rows[2 + r:3 + r, 0::2], w["b_qkv"][a + 1:b:2].unsqueeze(0), allow_slow_non_contiguous=True).then_inc(rows_in, 16)
            sp.dma_start(rows[2 + r:3 + r, 1::2], w["b_qkv"][a:b:2].unsqueeze(0), allow_slow_non_contiguous=True).then_inc(rows_in, 16)
            sp.dma_start(rows[4 + r:5 + r, :], w["b_g"][a:b].unsqueeze(0)).then_inc(rows_in, 16)
        sp.dma_start(rows[6:7, :], w["b_p"].unsqueeze(0)).then_inc(rows_in, 16)
        sp.dma_start(w_qkv[:, :], w["w_qkv"]).then_inc(w_in, 16)
        sp.dma_start(w_g[:, :], w["w_g"]).then_inc(w_in, 16)
        sp.dma_start(w_p[:, :, :], w["w_p"].rearrange("(k p) n -> p k n", p=P)).then_inc(w_in, 16)
        sp.dma_start(bv[:, :], w["b_qkv"][2 * D:4 * D].unsqueeze(0).partition_broadcast(P)).then_inc(w_in, 16)
        for dst, name in ((tab, "rtab"), (tri, "tri"), (diag, "diag"), (heads, "heads")):
            sp.dma_start(dst[:], w[name]).then_inc(cst_in, 16)

        def load(n, c):
            sp.dma_start(xt[:, c, :], w["x"][bass.ds(n, 1), c * P:(c + 1) * P, :].rearrange("b p d -> p (b d)")).then_inc(x_in[c], 16)
        for c in range(C):
            load(0, c)
        with sp.Fori(1, B) as i:
            for c in range(C):
                sp.wait_ge(xt_mm, i * C + (c - 3))
                load(i, c)

    @block.tensor
    def _(pe):
        pe.wait_ge(rows_in, 16 * 9)
        pe.transpose(bank[:, 7, 0:NR], rows[:, :], ident[0:NR, 0:NR]).then_inc(rows_T, 1)
        pe.wait_ge(cols_done, 1)
        pe.wait_ge(wc, 4)
        pe.wait_ge(w_in, 64)

        def step(i, c):
            at = i * C + c
            now, one, two, three = lag_range(i, c)
            par, was = c % 2, (c - 1) % 2
            c1 = (c - 1) % C
            if one:
                pe.wait_ge(q8_done, at + START)
                pe.wait_ge(mlo_done, at + (START - 1))
                pe.matmul(bank[:, S, :], qk[:, was, 1, :], q8[:, 0:4, :], start=True, stop=True).then_inc(slo_mm, 1)
            if now:
                pe.wait_ge(x_in[c], i * 16 + 16)
                pe.wait_ge(kt_done, at + (START - 1))
                pe.transpose(bank[:, X, 0:P], xt[:, c, :], ident[:, :]).then_inc(xt_mm, 1)
            if three:
                pe.wait_ge(gated_done, at + (START - 2))
                if one:
                    pe.wait_ge(sg_done, at + START)
                pe.wait_ge(p_done, at + (START - 3))
                for j in range(2):
                    mm = pe.matmul(bank[:, G, 2 * P:3 * P], w_p[:, j, :], gated[:, j, :], start=(j == 0), stop=(j == 1))
                mm.then_inc(p_mm, 1)
            if one:
                pe.wait_ge(mhi_done, at + (START - 1))
                pe.matmul(bank[:, S + 1, :], qk[:, was, 1, :], q8[:, 4:8, :], start=True, stop=True).then_inc(shi_mm, 1)
            if now:
                pe.wait_ge(xs_done, at + (1 + START))
                pe.wait_ge(r4_done, at + START)
                for j, lhs in enumerate([w_qkv[:, 0:D], w_sw[:, 0, :], w_qkv[:, D:2 * D], w_sw[:, 1, :]]):
                    mm = pe.matmul(bank[:, QK, j * P:(j + 1) * P], lhs, xs[:, par, :], start=True, stop=True)
                mm.then_inc(qk_mm, 1)
            if one:
                if now:
                    pe.wait_ge(xs_done, at + (START + 1))
                else:
                    pe.wait_ge(kt_done, at + (START - 1))
                pe.transpose(bank[:, X, 0:P], qk[:, was, 1, :], ident[:, :]).then_inc(kt_mm, 1)
            if now:
                pe.wait_ge(gated_done, at + (START - 2))
                pe.matmul(bank[:, V, 0:V2], xs[:, par, :], w_vc[:, :], start=True, stop=True).then_inc(v_mm, 1)
                pe.wait_ge(sg_done, at + START)
                pe.wait_ge(p_done, at + (START - 2))
                for j in range(2):
                    mm = pe.matmul(bank[:, G, j * P:(j + 1) * P], w_g[:, j * P:(j + 1) * P], xs[:, par, :], start=True, stop=True)
                mm.then_inc(g_mm, 1)
            if one:
                pe.wait_ge(on_done, at + (START - 1))
                if c1:
                    pe.wait_ge(state_done, at + (START - 1))
                    pe.matmul(bank[:, O, 0:V2], qk[:, was, 0, :], state[:, :], start=True, stop=False, skip_group_check=True)
                for h in range(R_HEADS):
                    if h % 4 == 0:
                        pe.wait_ge((mlo_done, mhi_done)[h // 4], at + START)
                    mm = pe.matmul(bank[:, O, h * R_DV:(h + 1) * R_DV], sm[:, h, :], vt[:, was, h * R_DV:(h + 1) * R_DV],
                                   start=(c1 == 0), stop=True, skip_group_check=True)
                mm.then_inc(o_mm, 1)
            if two:
                pe.wait_ge(on_done, at + (START - 1))
                pe.wait_ge(v_done, at + (START + 1) if now else at + (START if one else START - 1))
                for j in range(2):
                    mm = pe.transpose(bank[:, V, j * P:(j + 1) * P], on[:, j * P:(j + 1) * P], ident[:, :])
                mm.then_inc(ont_mm, 1)
            if one:
                pe.wait_ge(kt_done, at + START)
                pe.wait_ge(state_done, at + (START - 1))
                pe.matmul(bank[:, KV, 0:V2], kt[:, :], vt[:, was, :], start=(c1 == 0), stop=True, skip_group_check=True).then_inc(kv_mm, 1)
        chunk_loop(pe, step, 3)

    @block.scalar
    def _(act):
        for x in (xs_done, sg_done, kt_done, p_done):
            act.sem_inc(x, START)
        nc.scalar.preload_act_table_set("silu_and_others")
        act.wait_ge(cols_done, 1)

        def step(i, c):
            at = i * C + c
            now, one, two, three = lag_range(i, c)
            par = c % 2
            if now:
                act.wait_ge(xt_mm, at + 1)
                act.wait_ge(xst_done, at + (START - 1))
                if not (isinstance(i, int) and at < 2):
                    act.wait_ge(g_mm, at - 1)
                act.copy(xs[:, par, :], bank[:, X, 0:P]).then_inc(xs_done, 1)
            if three:
                n3, c3 = chunk_of(i, c, 3)
                act.wait_ge(p_mm, at - 2)
                apart(act, g)
                act.activation(xw[:, n3, c3 * P:(c3 + 1) * P], bank[:, G, 2 * P:3 * P], ACT.Identity, bias=cols[:, 6:7]).then_inc(p_done, 1)
            if one:
                act.wait_ge(kt_mm, at)
                act.wait_ge(kv_mm, at - 1)
                act.copy(kt[:, :], bank[:, X, 0:P]).then_inc(kt_done, 1)
            if now:
                act.wait_ge(g_mm, at + 1)
                act.wait_ge(gated_done, at + (START - 3))
                for j in range(2):
                    a = act.activation(sg[:, c, j, :], bank[:, G, j * P:(j + 1) * P], ACT.Silu, bias=cols[:, 4 + j:5 + j])
                a.then_inc(sg_done, 1)
            if one:
                act.wait_ge(o_mm, at)
                act.wait_ge(ss_done, at + (START - 1))
                act.activation(so[:, :], bank[:, O, 0:V2], ACT.Square).then_inc(sq_done, 1)

        chunk_loop(act, step, 3)

    @block.vector
    def _(dve):
        for x in (xst_done, r4_done, qk_done, q8_done, v_done, mlo_done, mhi_done, state_done, ss_done, on_done, gated_done):
            dve.sem_inc(x, START)
        dve.memset(mhalf[:, :], -0.5).then_inc(mh_done, 1)
        dve.wait_ge(rows_T, 1)
        dve.tensor_copy(cols[:, :], bank[:, 7, 0:NR]).then_inc(cols_done, 1)
        dve.wait_ge(w_in, 64)
        for j in range(2):
            src = w_qkv[:, j * D:(j + 1) * D].rearrange("p (a t) -> p a t", t=2)
            dve.tensor_copy(w_sw[:, j, :].rearrange("p (a t) -> p a t", t=2), src[:, :, ::-1]).then_inc(wc, 1)
        for j, (src, dst) in enumerate([(w_qkv[:, 2 * D:4 * D], w_vc), (bv[:, :], bvc)]):
            grp = src.rearrange("p (h d) -> p h d", d=R_DV)
            dve.tensor_reduce(vmean[:, j, :], grp, AX.X, ALU.add).then_inc(mean_done, 1)
            dve.wait_ge(mean_done, 2 * j + 1)
            dve.tensor_scalar(vmean[:, j, :], vmean[:, j, :], 1.0 / R_DV, None, ALU.mult).then_inc(mean_done, 1)
            dve.wait_ge(mean_done, 2 * j + 2)
            dve.tensor_tensor(dst[:, :].rearrange("p (h d) -> p h d", d=R_DV), grp,
                              vmean[:, j, :].unsqueeze(2).broadcast_to([P, R_HEADS, R_DV]), ALU.subtract).then_inc(wc, 1)
        dve.wait_ge(wc, 4)
        dve.wait_ge(cst_in, 64)

        def step(i, c):
            at = i * C + c
            now, one, two, three = lag_range(i, c)
            par, was = c % 2, (c - 1) % 2
            c1 = (c - 1) % C
            if one:
                for half, (mm, done) in enumerate([(slo_mm, mlo_done), (shi_mm, mhi_done)]):
                    dve.wait_ge(mm, at)
                    if half == 0:
                        dve.wait_ge(o_mm, at - 1)
                    dve.tensor_tensor(sm[:, 4 * half:4 * half + 4, :], bank[:, S + half, :].rearrange("p (h q) -> p h q", h=4),
                                      tri[:, :].unsqueeze(1).broadcast_to([P, 4, P]), ALU.mult).then_inc(done, 1)
            if two:
                dve.wait_ge(rs_done, at - 1)
                dve.wait_ge(ont_mm, at - 2)
                dve.tensor_tensor(on[:, :].rearrange("p (h d) -> p h d", d=R_DV), bank[:, O, 0:V2].rearrange("p (h d) -> p h d", d=R_DV),
                                  rs[:, :].unsqueeze(2).broadcast_to([P, R_HEADS, R_DV]), ALU.mult).then_inc(on_done, 1)
            if now:
                dve.wait_ge(qk_mm, at + 1)
                for j in range(4):
                    x = dve.scalar_tensor_tensor(out=r4[:, j, :], in0=bank[:, QK, j * P:(j + 1) * P], scalar=cols[:, (0, 2, 1, 3)[j]:(0, 2, 1, 3)[j] + 1],
                                                 in1=tab[:, c, j, :], op0=ALU.add, op1=ALU.mult)
                x.then_inc(r4_done, 1)
                dve.wait_ge(v_mm, at + 1)
                dve.tensor_tensor(vt[:, par, :], bank[:, V, 0:V2], bvc[:, :], ALU.add).then_inc(v_done, 1)
                dve.wait_ge(r4_done, at + (1 + START))
                dve.tensor_tensor(qk[:, par, :, :], r4[:, 0::2, :], r4[:, 1::2, :], ALU.add).then_inc(qk_done, 1)
                dve.wait_ge(xs_done, at + (1 + START))
                dve.tensor_copy(x_all[:, i, c * P:(c + 1) * P], xs[:, par, :]).then_inc(xst_done, 1)
                dve.wait_ge(qk_done, at + (1 + START))
                if one:
                    dve.wait_ge(shi_mm, at)
                dve.tensor_tensor(q8[:, :, :], qk[:, par, 0, :].unsqueeze(1).broadcast_to([P, R_HEADS, P]),
                                  heads[:, :].unsqueeze(2).broadcast_to([P, R_HEADS, P]), ALU.mult).then_inc(q8_done, 1)
            if two:
                dve.wait_ge(ont_mm, at - 1)
                dve.wait_ge(sg_done, at + (START - 1))
                dve.wait_ge(p_mm, at - 2)
                dve.tensor_tensor(gated[:, :, :], bank[:, V, 0:V2].rearrange("p (j q) -> p j q", j=2), sg[:, (c - 2) % C, :, :], ALU.mult).then_inc(gated_done, 1)
            if one:
                dve.wait_ge(kv_mm, at)
                dve.wait_ge(o_mm, at)
                dve.tensor_tensor(state[:, :], bank[:, KV, 0:V2], diag[:, :], ALU.mult).then_inc(state_done, 1)
                dve.wait_ge(sq_done, at)
                dve.wait_ge(sv_done, at - 1)
                dve.tensor_reduce(ss[:, :], so[:, :].rearrange("p (h d) -> p h d", d=R_DV), AX.X, ALU.add).then_inc(ss_done, 1)

        chunk_loop(dve, step, 2)

    @block.gpsimd
    def _(pool):
        pool.wait_ge(mh_done, 1)

        def step(i, c):
            at = i * C + c
            if chunk_range(i, c, 1):
                pool.wait_ge(ss_done, at + START)
                pool.wait_ge(on_done, at + (START - 1))
                apart(pool, g)
                pool.tensor_scalar(sv[:, :], ss[:, :], 1.0 / R_DV, EPS_GN, ALU.mult, ALU.add).then_inc(sv_done, 1)
                pool.wait_ge(sv_done, at)
                pool.tensor_tensor(rs[:, :], sv[:, :], mhalf[:, :], ALU.pow).then_inc(rs_done, 1)

        chunk_loop(pool, step, 2)


EPS_OUT = 1e-5
E_COUNT, E_FF = 8, 512
EF = E_FF // P
TILES = B * C
SLOTS = -(-(B * T + E_COUNT * (P - 1)) // (4 * P)) * 4
MOE_TABLES = ("before", "desc", "full", "slot")


def moe_tables():
    row = lambda a: np.ascontiguousarray(np.broadcast_to(np.asarray(a, np.float32), (P, len(a))))
    before = (np.arange(P)[:, None] < np.arange(P)[None, :]).astype(np.float32)
    return {"before": before, "desc": row(E_COUNT - np.arange(E_COUNT)), "full": row(P * np.arange(TILES)), "slot": row(np.arange(SLOTS))}


def pair_loop(eng, step, depth):
    for c in range(2):
        step(0, c)
    with eng.Fori(1, B // 2) as i:
        for c in range(2):
            step(i, c)
    for c in range(depth):
        step(B // 2, c)


def outer_norm(nc, ctx, g, tag, out=None):
    def sb(name, shape):
        return ctx.enter_context(nc.sbuf_tensor(tag + name, shape, F32))

    def sem(name):
        return phase_semaphore(nc, g, tag + name)

    x_all, xw, ident, bank = g.x, g.xw, g.ident, g.bank
    y = sb("y", [P, 2, T])
    st = sb("st", [P, 2, C, 6])
    mv = sb("mv", [P, 2, C, 2])
    ve = sb("ve", [P, C])
    mhalf = sb("mhalf", [P, C])
    rstd = sb("rstd", [P, 2, C])
    xn = sb("xn", [P, 2, C, D])
    mh_done = sem("mh_done")
    y_done = sem("y_done")
    y_mm = sem("y_mm")
    bn_done = sem("bn_done")
    mv_done = sem("mv_done")
    ve_done = sem("ve_done")
    rstd_done = sem("rstd_done")
    xn_done = sem("xn_done")
    back_mm = sem("back_mm")
    x_done = sem("x_done")
    xw_done = sem("xw_done")
    out0 = sem("out0")
    out1 = sem("out1")
    out_done = [out0, out1]
    Y, BACK = (0, 1), (2, 3)
    block = ctx.enter_context(nc.Block())

    def there(i, c, lag):
        return not isinstance(i, int) or 0 <= 2 * i + c - lag < B

    @block.tensor
    def _(pe):
        def step(i, c):
            n = 2 * i + c
            p, q = c % 2, (c - 1) % 2
            if there(i, c, 0):
                pe.wait_ge(y_done, n + 1)
                pe.wait_ge(xn_done, n + (START - 1))
                for k in range(C):
                    mm = pe.transpose(bank[:, Y[p], k * P:(k + 1) * P], y[:, p, k * P:(k + 1) * P], ident[:, :])
                mm.then_inc(y_mm, 1)
            if there(i, c, 1) and out is None:
                pe.wait_ge(xn_done, n + START)
                pe.wait_ge(x_done, n + (START - 2))
                pe.wait_ge(xw_done, n + (START - 2))
                for k in range(C):
                    mm = pe.transpose(bank[:, BACK[q], k * P:(k + 1) * P], xn[:, q, k, :], ident[:, :])
                mm.then_inc(back_mm, 1)

        pair_loop(pe, step, 1)

    @block.gpsimd
    def _(pool):
        pool.wait_ge(mh_done, 1)

        def step(i, c):
            n = 2 * i + c
            p = c % 2
            if there(i, c, 0):
                if not (isinstance(i, int) and n < 2):
                    pool.wait_ge(y_mm, n - 1)
                pool.tensor_tensor(y[:, p, :], x_all[:, n, :], xw[:, n, :], ALU.add).then_inc(y_done, 1)
                pool.wait_ge(mv_done, n + 1)
                pool.wait_ge(xn_done, n + (START - 1))
                apart(pool, g)
                pool.tensor_scalar(ve[:, :], mv[:, p, :, 1], EPS_OUT, None, ALU.add).then_inc(ve_done, 1)
                pool.wait_ge(ve_done, n + 1)
                pool.tensor_tensor(rstd[:, p, :], ve[:, :], mhalf[:, :], ALU.pow).then_inc(rstd_done, 1)

        pair_loop(pool, step, 1)

    @block.vector
    def _(dve):
        dve.sem_inc(xn_done, START)
        dve.memset(mhalf[:, :], -0.5).then_inc(mh_done, 1)

        def step(i, c):
            n = 2 * i + c
            p, q = c % 2, (c - 1) % 2
            if there(i, c, 0):
                dve.wait_ge(y_mm, n + 1)
                if not (isinstance(i, int) and n < 2):
                    dve.wait_ge(ve_done, n - 1)
                apart(dve, g)
                layer_stats(dve, g, bank[:, Y[p], :].rearrange("p (c d) -> p c d", c=C), st[:, p], mv[:, p], bn_done, n + 1, mv_done)
            if there(i, c, 1):
                dve.wait_ge(rstd_done, n)
                if out is None:
                    if not (isinstance(i, int) and n < 3):
                        dve.wait_ge(back_mm, n - 2)
                elif not (isinstance(i, int) and n < 3):
                    k = (c - 1) % 2
                    dve.wait_ge(out_done[k], (2 * i + c - 1 - k) * 8)
                for k in range(C):
                    x = dve.tensor_scalar(xn[:, q, k, :], bank[:, Y[q], k * P:(k + 1) * P], mv[:, q, k, 0:1], rstd[:, q, k:k + 1], ALU.subtract, ALU.mult)
                x.then_inc(xn_done, 1)

        pair_loop(dve, step, 1)

    @block.scalar
    def _(act):
        act.sem_inc(x_done, START)
        act.sem_inc(xw_done, START)

        def step(i, c):
            if there(i, c, 1) and out is None:
                n = 2 * i + c
                q = (c - 1) % 2
                act.wait_ge(back_mm, n)
                apart(act, g)
                act.copy(x_all[:, n - 1, :], bank[:, BACK[q], :]).then_inc(x_done, 1)
                act.copy(xw[:, n - 1, :], bank[:, BACK[q], :]).then_inc(xw_done, 1)

        pair_loop(act, step, 1)

    @block.sync
    def _(sp):
        def step(i, c):
            if there(i, c, 1) and out is not None:
                n = 2 * i + c
                q = (c - 1) % 2
                sp.wait_ge(xn_done, n + START)
                sp.dma_start(out[bass.ds(n - 1, 1), :, :].rearrange("b (c p) d -> p (b c) d", p=P), xn[:, q, :, :]).then_inc(out_done[q], 16)

        pair_loop(sp, step, 1)
        if out is not None:
            for k in range(2):
                sp.wait_ge(out_done[k], 16 * B // 2)


def norm_and_route(nc, ctx, g, w):
    def sb(name, shape, dtype=F32):
        return ctx.enter_context(nc.sbuf_tensor("nr_" + name, shape, dtype))

    def sem(name):
        return phase_semaphore(nc, g, "nr_" + name)

    x_all, xw, ident, bank = g.x, g.xw, g.ident, g.bank
    y = sb("y", [P, 2, T])
    st = sb("st", [P, 2, C, 6])
    mv = sb("mv", [P, 2, C, 2])
    ve = sb("ve", [P, C])
    mhalf = sb("mhalf", [P, C])
    rstd = sb("rstd", [P, 2, C])
    xn = sb("xn", [P, 2, T])
    xT = sb("xT", [P, 2, T])
    ZW = SLOTS * D // 8
    zeros = sb("zeros", [P, ZW])
    wr = sb("wr", [P, E_COUNT])
    lg = sb("lg", [P, TILES, E_COUNT])
    ex = sb("ex", [P, TILES, E_COUNT])
    key = sb("key", [P, TILES, E_COUNT])
    scan = sb("scan", [P, 2, TILES, E_COUNT])
    place = sb("place", [P, TILES, E_COUNT])
    ones = sb("ones", [P, P])
    before = sb("before", [P, P])
    desc = sb("desc", [P, E_COUNT])
    full = sb("full", [P, TILES])
    slot = sb("slot", [P, SLOTS])
    over = sb("over", [P, E_COUNT, TILES])
    started = sb("started", [P, SLOTS, E_COUNT - 1])
    ends = sb("ends", [P, 2, E_COUNT])
    tiles = sb("tiles", [P, E_COUNT])
    starts = sb("starts", [P, E_COUNT])
    top = sb("top", [P, TILES])
    first = sb("first", [P, TILES])
    total = sb("total", [P, TILES])
    posf = sb("posf", [P, TILES])
    texp = sb("texp", [P, SLOTS])
    c_in = sem("c_in")
    mh_done = sem("mh_done")
    y_done = sem("y_done")
    y_mm = sem("y_mm")
    bn_done = sem("bn_done")
    mv_done = sem("mv_done")
    ve_done = sem("ve_done")
    rstd_done = sem("rstd_done")
    xn_done = sem("xn_done")
    back_mm = sem("back_mm")
    tok_done = sem("tok_done")
    xT_done = sem("xT_done")
    lg_mm = sem("lg_mm")
    lg_done = sem("lg_done")
    d_done = sem("d_done")
    ex_done = sem("ex_done")
    oh_done = sem("oh_done")
    cnt_mm = sem("cnt_mm")
    order = sem("order")
    zero_done = sem("zero_done")
    zero_out = sem("zero_out")
    Y, BACK, LG = (0, 1), (2, 3), (4, 5)
    bc = [P, TILES, E_COUNT]
    block = ctx.enter_context(nc.Block())

    def there(i, c, lag):
        return not isinstance(i, int) or 0 <= 2 * i + c - lag < B

    @block.sync
    def _(sp):
        for dst, src in ((wr, "Wr"), (before, "before"), (desc, "desc"), (full, "full"), (slot, "slot")):
            sp.dma_start(dst[:, :], w[src]).then_inc(c_in, 16)
        sp.wait_ge(zero_done, 1)
        flat = g.x_sorted.rearrange("(q p r) d -> q p (r d)", q=8, p=P)
        for q in range(8):
            sp.dma_start(flat[q:q + 1].rearrange("q p f -> p (q f)"), zeros[:, :]).then_inc(zero_out, 16)
        sp.wait_ge(zero_out, 8 * 16)

    @block.tensor
    def _(pe):
        pe.wait_ge(c_in, 5 * 16)

        def step(i, c):
            n = 2 * i + c
            p, q = c % 2, (c - 1) % 2
            if there(i, c, 0):
                pe.wait_ge(y_done, n + 1)
                pe.wait_ge(xn_done, n + (START - 1))
                for k in range(C):
                    mm = pe.transpose(bank[:, Y[p], k * P:(k + 1) * P], y[:, p, k * P:(k + 1) * P], ident[:, :])
                mm.then_inc(y_mm, 1)
            if there(i, c, 1):
                pe.wait_ge(xn_done, n + START)
                pe.wait_ge(xT_done, n + (START - 2))
                for k in range(C):
                    mm = pe.transpose(bank[:, BACK[q], k * P:(k + 1) * P], xn[:, q, k * P:(k + 1) * P], ident[:, :])
                mm.then_inc(back_mm, 1)
            if there(i, c, 2):
                pe.wait_ge(xT_done, n + (START - 1))
                pe.wait_ge(lg_done, n + (START - 3))
                for k in range(C):
                    mm = pe.matmul(bank[:, LG[p], k * E_COUNT:(k + 1) * E_COUNT], xT[:, p, k * P:(k + 1) * P], wr[:, :], start=True, stop=True)
                mm.then_inc(lg_mm, 1)

        pair_loop(pe, step, 2)
        pe.wait_ge(oh_done, 1)
        pe.matmul(bank[:, 6, :], before[:, :], key[:, :, :], start=True, stop=True)
        pe.matmul(bank[:, 7, :], ones[:, :], key[:, :, :], start=True, stop=True).then_inc(cnt_mm, 1)

    @block.gpsimd
    def _(pool):
        pool.memset(zeros[:, :], 0.0).then_inc(zero_done, 1)
        pool.wait_ge(mh_done, 1)

        def step(i, c):
            n = 2 * i + c
            p = c % 2
            if there(i, c, 0):
                if not (isinstance(i, int) and n < 2):
                    pool.wait_ge(y_mm, n - 1)
                pool.tensor_tensor(y[:, p, :], x_all[:, n, :], xw[:, n, :], ALU.add).then_inc(y_done, 1)
                pool.wait_ge(mv_done, n + 1)
                pool.wait_ge(xn_done, n + (START - 1))
                apart(pool, g)
                pool.tensor_scalar(ve[:, :], mv[:, p, :, 1], EPS_OUT, None, ALU.add).then_inc(ve_done, 1)
                pool.wait_ge(ve_done, n + 1)
                pool.tensor_tensor(rstd[:, p, :], ve[:, :], mhalf[:, :], ALU.pow).then_inc(rstd_done, 1)

        pair_loop(pool, step, 1)

    @block.scalar
    def _(act):
        for x in (tok_done, xT_done, lg_done):
            act.sem_inc(x, START)
        nc.scalar.preload_act_table_set("exp_and_others")

        def step(i, c):
            n = 2 * i + c
            p, q = c % 2, (c - 1) % 2
            if there(i, c, 1):
                act.wait_ge(back_mm, n)
                if not (isinstance(i, int) and n < 3):
                    act.wait_ge(lg_mm, n - 2)
                act.copy(xT[:, q, :], bank[:, BACK[q], :]).then_inc(xT_done, 1)
                apart(act, g)
                act.copy(xw[:, n - 1, :], xn[:, q, :]).then_inc(tok_done, 1)
            if there(i, c, 2):
                act.wait_ge(lg_mm, n - 1)
                apart(act, g)
                act.copy(lg[:, bass.ds((n - 2) * C, C), :], bank[:, LG[p], 0:C * E_COUNT].rearrange("p (c e) -> p c e", e=E_COUNT)).then_inc(lg_done, 1)

        pair_loop(act, step, 2)
        act.wait_ge(d_done, 1)
        act.activation(ex[:, :, :], lg[:, :, :], ACT.Exp).then_inc(ex_done, 1)

    @block.vector
    def _(dve):
        dve.sem_inc(xn_done, START)
        dve.memset(ones[:, :], 1.0)
        dve.memset(mhalf[:, :], -0.5).then_inc(mh_done, 1)

        def step(i, c):
            n = 2 * i + c
            p, q = c % 2, (c - 1) % 2
            if there(i, c, 0):
                dve.wait_ge(y_mm, n + 1)
                if not (isinstance(i, int) and n < 2):
                    dve.wait_ge(ve_done, n - 1)
                apart(dve, g)
                layer_stats(dve, g, bank[:, Y[p], :].rearrange("p (c d) -> p c d", c=C), st[:, p], mv[:, p], bn_done, n + 1, mv_done)
            if there(i, c, 1):
                dve.wait_ge(rstd_done, n)
                if not (isinstance(i, int) and n < 3):
                    dve.wait_ge(back_mm, n - 2)
                dve.wait_ge(tok_done, n + (START - 2))
                for k in range(C):
                    x = dve.tensor_scalar(xn[:, q, k * P:(k + 1) * P], bank[:, Y[q], k * P:(k + 1) * P], mv[:, q, k, 0:1], rstd[:, q, k:k + 1], ALU.subtract, ALU.mult)
                x.then_inc(xn_done, 1)

        pair_loop(dve, step, 1)
        dve.wait_ge(lg_done, B + START)
        dve.wait_ge(mh_done, 1)
        dve.tensor_reduce(top[:, :], lg[:, :, :], AX.X, ALU.max).then_inc(order, 1)
        dve.wait_ge(order, 1)
        dve.tensor_tensor(lg[:, :, :], lg[:, :, :], top[:, :].unsqueeze(2).broadcast_to(bc), ALU.subtract).then_inc(d_done, 1)
        dve.wait_ge(d_done, 1)
        dve.wait_ge(c_in, 5 * 16)
        dve.scalar_tensor_tensor(out=key[:, :, :], in0=lg[:, :, :], scalar=0.0, in1=desc[:, :].unsqueeze(1).broadcast_to(bc), op0=ALU.is_ge, op1=ALU.mult).then_inc(order, 1)
        dve.wait_ge(order, 2)
        dve.tensor_reduce(first[:, :], key[:, :, :], AX.X, ALU.max).then_inc(order, 1)
        dve.wait_ge(order, 3)
        dve.tensor_tensor(key[:, :, :], key[:, :, :], first[:, :].unsqueeze(2).broadcast_to(bc), ALU.is_equal).then_inc(oh_done, 1)
        dve.wait_ge(ex_done, 1)
        dve.tensor_reduce(total[:, :], ex[:, :, :], AX.X, ALU.add).then_inc(order, 1)
        dve.wait_ge(order, 4)
        dve.reciprocal(g.pmax[:, :], total[:, :]).then_inc(order, 1)
        dve.wait_ge(cnt_mm, 1)
        dve.tensor_copy(scan[:, 0, :, :], bank[:, 7, :].rearrange("p (k e) -> p k e", e=E_COUNT)).then_inc(order, 1)
        shift, a, at = 1, 0, 6
        while shift < TILES:
            dve.wait_ge(order, at)
            dve.tensor_copy(scan[:, 1 - a, 0:shift, :], scan[:, a, 0:shift, :])
            dve.tensor_tensor(scan[:, 1 - a, shift:, :], scan[:, a, shift:, :], scan[:, a, 0:TILES - shift, :], ALU.add).then_inc(order, 1)
            shift, a, at = 2 * shift, 1 - a, at + 1
        dve.wait_ge(order, at)
        dve.tensor_tensor(place[:, :, :], scan[:, a, :, :], bank[:, 7, :].rearrange("p (k e) -> p k e", e=E_COUNT), ALU.subtract).then_inc(order, 1)
        dve.tensor_tensor(over[:, :, :], scan[:, a, TILES - 1, :].unsqueeze(2).broadcast_to([P, E_COUNT, TILES]),
                          full[:, :].unsqueeze(1).broadcast_to([P, E_COUNT, TILES]), ALU.is_gt).then_inc(order, 1)
        dve.wait_ge(order, at + 2)
        dve.tensor_tensor(place[:, :, :], place[:, :, :], bank[:, 6, :].rearrange("p (k e) -> p k e", e=E_COUNT), ALU.add).then_inc(order, 1)
        dve.tensor_reduce(tiles[:, :], over[:, :, :], AX.X, ALU.add).then_inc(order, 1)
        dve.wait_ge(order, at + 4)
        dve.tensor_copy(ends[:, 0, :], tiles[:, :]).then_inc(order, 1)
        shift, a, at = 1, 0, at + 5
        while shift < E_COUNT:
            dve.wait_ge(order, at)
            dve.tensor_copy(ends[:, 1 - a, 0:shift], ends[:, a, 0:shift])
            dve.tensor_tensor(ends[:, 1 - a, shift:], ends[:, a, shift:], ends[:, a, 0:E_COUNT - shift], ALU.add).then_inc(order, 1)
            shift, a, at = 2 * shift, 1 - a, at + 1
        dve.wait_ge(order, at)
        dve.tensor_tensor(starts[:, :], ends[:, a, :], tiles[:, :], ALU.subtract).then_inc(order, 1)
        dve.wait_ge(order, at + 1)
        dve.scalar_tensor_tensor(out=place[:, :, :], in0=starts[:, :].unsqueeze(1).broadcast_to(bc), scalar=float(P), in1=place[:, :, :], op0=ALU.mult, op1=ALU.add).then_inc(order, 1)
        dve.tensor_tensor(started[:, :, :], starts[:, 1:].unsqueeze(1).broadcast_to([P, SLOTS, E_COUNT - 1]),
                          slot[:, :].unsqueeze(2).broadcast_to([P, SLOTS, E_COUNT - 1]), ALU.is_le).then_inc(order, 1)
        dve.wait_ge(order, at + 3)
        dve.tensor_tensor(place[:, :, :], place[:, :, :], key[:, :, :], ALU.mult).then_inc(order, 1)
        dve.tensor_reduce(texp[:, :], started[:, :, :], AX.X, ALU.add).then_inc(order, 1)
        dve.wait_ge(order, at + 5)
        dve.tensor_reduce(posf[:, :], place[:, :, :], AX.X, ALU.add).then_inc(order, 1)
        dve.tensor_copy(g.tile_expert[:, :], texp[:, :]).then_inc(order, 1)
        dve.wait_ge(order, at + 7)
        dve.tensor_copy(g.place[:, :], posf[:, :]).then_inc(order, 1)


def slot_loop(eng, step, depth):
    for c in range(4):
        step(0, c)
    with eng.Fori(1, SLOTS // 4 - 1) as i:
        for c in range(4):
            step(i, c)
    for c in range(4 + depth):
        step(SLOTS // 4 - 1 + c // 4, c % 4)


def l0_experts(nc, ctx, g, w):
    def sb(name, shape):
        return ctx.enter_context(nc.sbuf_tensor("ex_" + name, shape, F32))

    def sem(name):
        return phase_semaphore(nc, g, "ex_" + name)

    ident, bank = g.ident, g.bank
    tok = g.xw[:, :, :].rearrange("p n (c d) -> p (n c) d", d=D)
    w1 = sb("w1", [P, E_COUNT, E_FF])
    w2 = sb("w2", [P, E_COUNT, EF, D])
    b1 = sb("b1", [P, E_COUNT, E_FF])
    b2 = sb("b2", [P, E_COUNT, D])
    xin = sb("xin", [P, 4, D])
    xT = sb("xT", [P, 2, P])
    hb = sb("hb", [P, 2, E_FF])
    hg = sb("hg", [P, 2, E_FF])
    hT = sb("hT", [P, 2, EF, P])
    yo = sb("yo", [P, 4, D])
    w_in = sem("w_in")
    x_in0 = sem("x_in0")
    x_in1 = sem("x_in1")
    x_in2 = sem("x_in2")
    x_in3 = sem("x_in3")
    y_out0 = sem("y_out0")
    y_out1 = sem("y_out1")
    y_out2 = sem("y_out2")
    y_out3 = sem("y_out3")
    x_mm = sem("x_mm")
    xT_done = sem("xT_done")
    h_mm = sem("h_mm")
    hb_done = sem("hb_done")
    hg_done = sem("hg_done")
    ht_mm = sem("ht_mm")
    hT_done = sem("hT_done")
    y_mm = sem("y_mm")
    y_done = sem("y_done")
    x_in = [x_in0, x_in1, x_in2, x_in3]
    y_out = [y_out0, y_out1, y_out2, y_out3]
    X, H, HT_, Y = 0, (1, 2), (3, 4), (5, 6)
    block = ctx.enter_context(nc.Block())

    def there(i, c, lag):
        return not isinstance(i, int) or 0 <= 4 * i + c - lag < SLOTS

    def expert_of(eng, t):
        return eng.value_load(g.tile_expert[0:1, bass.ds(t, 1)], min_val=0, max_val=E_COUNT - 1)

    @block.gpsimd
    def _(pool):
        for k in range(TILES):
            pool.indirect_dma_start(g.x_sorted, bass.IndirectOffsetOnAxis(g.place[:, k:k + 1], 0), tok[:, k, :], None).then_inc(g.scattered, 16)
        pool.wait_ge(g.scattered, 16 * TILES)

    @block.sync
    def _(sp):
        for e in range(E_COUNT):
            sp.dma_start(w1[:, e, :], w["W1"][e]).then_inc(w_in, 16)
        sp.dma_start(w2[:, :, :, :].rearrange("p e f d -> p (e f) d"), w["W2"].rearrange("e (f p) d -> p (e f) d", p=P)).then_inc(w_in, 16)
        sp.dma_start(b1[:, :, :].rearrange("p e f -> p (e f)"), w["b1"].rearrange("e f -> (e f)").unsqueeze(0).partition_broadcast(P)).then_inc(w_in, 16)
        sp.dma_start(b2[:, :, :].rearrange("p e f -> p (e f)"), w["b2"].rearrange("e f -> (e f)").unsqueeze(0).partition_broadcast(P)).then_inc(w_in, 16)
        for y in y_out:
            sp.sem_inc(y, 16)
        sp.wait_ge(g.scattered, 16 * TILES)

        def load(t, slot):
            sp.dma_start(xin[:, slot, :], g.x_sorted[bass.ds(t * P, P), :]).then_inc(x_in[slot], 16)
        for t in range(3):
            load(t, t)

        def step(i, c):
            m = 4 * i + c
            if not isinstance(i, int) or m + 3 < SLOTS:
                if not (isinstance(i, int) and m < 1):
                    sp.wait_ge(x_mm, m)
                load(m + 3, (c + 3) % 4)
            if there(i, c, 4):
                sp.wait_ge(y_done, m + (START - 3))
                sp.dma_start(g.y_sorted[bass.ds((m - 4) * P, P), :], yo[:, c, :]).then_inc(y_out[c], 16)

        slot_loop(sp, step, 4)
        for y in y_out:
            sp.wait_ge(y, 16 * (SLOTS // 4 + 1))

    @block.tensor
    def _(pe):
        pe.wait_ge(w_in, 16 * (E_COUNT + 3))

        def step(i, c):
            m = 4 * i + c
            p, q = c % 2, (c - 1) % 2
            if there(i, c, 0):
                pe.wait_ge(x_in[c], i * 16 + 16)
                pe.wait_ge(xT_done, m + START)
                pe.transpose(bank[:, X, 0:P], xin[:, c, :], ident[:, :]).then_inc(x_mm, 1)
            if there(i, c, 1):
                e = expert_of(pe, m - 1)
                pe.wait_ge(xT_done, m + START)
                pe.wait_ge(hb_done, m + (START - 2))
                pe.matmul(bank[:, H[q], :], xT[:, q, :], w1[:, bass.ds(e, 1), :].rearrange("p a f -> p (a f)"), start=True, stop=True).then_inc(h_mm, 1)
            if there(i, c, 2):
                pe.wait_ge(hg_done, m + (START - 1))
                pe.wait_ge(hT_done, m + (START - 3))
                for f in range(EF):
                    mm = pe.transpose(bank[:, HT_[p], f * P:(f + 1) * P], hg[:, p, f * P:(f + 1) * P], ident[:, :])
                mm.then_inc(ht_mm, 1)
            if there(i, c, 3):
                e = expert_of(pe, m - 3)
                pe.wait_ge(hT_done, m + (START - 2))
                pe.wait_ge(y_done, m + (START - 4))
                for f in range(EF):
                    mm = pe.matmul(bank[:, Y[q], 0:D], hT[:, q, f, :], w2[:, bass.ds(e, 1), f, :].rearrange("p a d -> p (a d)"), start=(f == 0), stop=(f == EF - 1))
                mm.then_inc(y_mm, 1)

        slot_loop(pe, step, 3)

    @block.vector
    def _(dve):
        for x in (xT_done, hb_done, y_done):
            dve.sem_inc(x, START)
        dve.wait_ge(w_in, 16 * (E_COUNT + 3))

        def step(i, c):
            m = 4 * i + c
            p, q = c % 2, (c - 1) % 2
            if there(i, c, 0):
                dve.wait_ge(x_mm, m + 1)
                if not (isinstance(i, int) and m < 2):
                    dve.wait_ge(h_mm, m - 1)
                dve.tensor_copy(xT[:, p, :], bank[:, X, 0:P]).then_inc(xT_done, 1)
            if there(i, c, 1):
                e = expert_of(dve, m - 1)
                dve.wait_ge(h_mm, m)
                dve.wait_ge(hg_done, m + (START - 2))
                dve.tensor_tensor(hb[:, q, :], bank[:, H[q], :], b1[:, bass.ds(e, 1), :].rearrange("p a f -> p (a f)"), ALU.add).then_inc(hb_done, 1)
            if there(i, c, 3):
                e = expert_of(dve, m - 3)
                dve.wait_ge(y_mm, m - 2)
                slot = (c - 3) % 4
                dve.wait_ge(y_out[slot], (i + (c - 3) // 4) * 16 + 16)
                dve.tensor_tensor(yo[:, slot, :], bank[:, Y[q], 0:D], b2[:, bass.ds(e, 1), :].rearrange("p a f -> p (a f)"), ALU.add).then_inc(y_done, 1)

        slot_loop(dve, step, 3)

    @block.scalar
    def _(act):
        act.sem_inc(hg_done, START)
        act.sem_inc(hT_done, START)
        nc.scalar.preload_act_table_set("gelu_and_others")

        def step(i, c):
            m = 4 * i + c
            p, q = c % 2, (c - 1) % 2
            if there(i, c, 2):
                act.wait_ge(ht_mm, m - 1)
                if not (isinstance(i, int) and m < 4):
                    act.wait_ge(y_mm, m - 3)
                act.copy(hT[:, p, :, :], bank[:, HT_[p], :].rearrange("p (f t) -> p f t", t=P)).then_inc(hT_done, 1)
            if there(i, c, 1):
                act.wait_ge(hb_done, m + START)
                if not (isinstance(i, int) and m < 3):
                    act.wait_ge(ht_mm, m - 2)
                act.activation(hg[:, q, :], hb[:, q, :], ACT.Gelu).then_inc(hg_done, 1)

        slot_loop(act, step, 2)


def gather_and_norm(nc, ctx, g):
    def sb(name, shape):
        return ctx.enter_context(nc.sbuf_tensor("gn_" + name, shape, F32))

    def sem(name):
        return phase_semaphore(nc, g, "gn_" + name)

    x_all, xw, ident, bank = g.x, g.xw, g.ident, g.bank
    back = g.x[:, :, :].rearrange("p n (c d) -> p (n c) d", d=D)
    y = sb("y", [P, 2, C, D])
    st = sb("st", [P, 2, C, 6])
    mv = sb("mv", [P, 2, C, 2])
    ve = sb("ve", [P, 2, C])
    mhalf = sb("mhalf", [P, C])
    rstd = sb("rstd", [P, 2, C])
    xn = sb("xn", [P, 2, C, D])
    mh_done = sem("mh_done")
    y_done = sem("y_done")
    bn_done = sem("bn_done")
    mv_done = sem("mv_done")
    ve_done = sem("ve_done")
    rstd_done = sem("rstd_done")
    xn_done = sem("xn_done")
    back_mm = sem("back_mm")
    x_done = sem("x_done")
    AHEAD, taken = len(g.taken), g.taken
    BACK = (2, 3)
    block = ctx.enter_context(nc.Block())

    def there(i, c, lag):
        return not isinstance(i, int) or 0 <= 2 * i + c - lag < B

    @block.gpsimd
    def _(pool):
        pool.wait_ge(mh_done, 1)
        for n in range(B + 2):
            if n < B:
                for k in range(C * n, C * n + C):
                    if k >= AHEAD:
                        pool.wait_ge(taken[k % AHEAD], 16 * (k // AHEAD))
                    pool.indirect_dma_start(back[:, k, :], None, g.y_sorted, bass.IndirectOffsetOnAxis(g.place[:, k:k + 1], 0)).then_inc(taken[k % AHEAD], 16)
            if n >= 2:
                m = n - 2
                pool.wait_ge(mv_done, m + 1)
                if m:
                    pool.wait_ge(xn_done, m + (START - 1))
                pool.tensor_scalar(ve[:, m % 2, :], mv[:, m % 2, :, 1], EPS_OUT, None, ALU.add).then_inc(ve_done, 1)
                pool.wait_ge(ve_done, m + 1)
                pool.tensor_tensor(rstd[:, m % 2, :], ve[:, m % 2, :], mhalf[:, :], ALU.pow).then_inc(rstd_done, 1)

    @block.vector
    def _(dve):
        dve.sem_inc(xn_done, START)
        dve.memset(mhalf[:, :], -0.5).then_inc(mh_done, 1)

        def step(i, c):
            n = 2 * i + c
            p, q = c % 2, (c - 1) % 2
            if there(i, c, 0):
                dve.wait_ge(xn_done, n + (START - 1))
                for k in range(C):
                    dve.wait_ge(taken[p * C + k], i * 16 + 16)
                    t = n * C + k
                    x = dve.scalar_tensor_tensor(out=y[:, p, k:k + 1, :], in0=back[:, bass.ds(t, 1), :], scalar=g.pmax[:, bass.ds(t, 1)],
                                                 in1=xw[:, n, k * D:(k + 1) * D].unsqueeze(1), op0=ALU.mult, op1=ALU.add)
                x.then_inc(y_done, 1)
                dve.wait_ge(y_done, n + 1)
                if not (isinstance(i, int) and n < 2):
                    dve.wait_ge(ve_done, n - 1)
                apart(dve, g)
                layer_stats(dve, g, y[:, p], st[:, p], mv[:, p], bn_done, n + 1, mv_done)
            if there(i, c, 1):
                dve.wait_ge(rstd_done, n)
                if not (isinstance(i, int) and n < 3):
                    dve.wait_ge(back_mm, n - 2)
                for k in range(C):
                    x = dve.tensor_scalar(xn[:, q, k, :], y[:, q, k, :], mv[:, q, k, 0:1], rstd[:, q, k:k + 1], ALU.subtract, ALU.mult)
                x.then_inc(xn_done, 1)

        pair_loop(dve, step, 1)

    @block.tensor
    def _(pe):
        def step(i, c):
            n = 2 * i + c
            q = (c - 1) % 2
            if there(i, c, 1):
                pe.wait_ge(xn_done, n + START)
                pe.wait_ge(x_done, n + (START - 2))
                for k in range(C):
                    mm = pe.transpose(bank[:, BACK[q], k * P:(k + 1) * P], xn[:, q, k, :], ident[:, :])
                mm.then_inc(back_mm, 1)

        pair_loop(pe, step, 1)

    @block.scalar
    def _(act):
        act.sem_inc(x_done, START)

        def step(i, c):
            if there(i, c, 1):
                n = 2 * i + c
                q = (c - 1) % 2
                act.wait_ge(back_mm, n)
                apart(act, g)
                act.copy(x_all[:, n - 1, :], bank[:, BACK[q], :])
                act.copy(xw[:, n - 1, :], bank[:, BACK[q], :]).then_inc(x_done, 1)

        pair_loop(act, step, 1)


def program(nc, w, out):
    with ExitStack() as ctx:
        sb = lambda name, shape: ctx.enter_context(nc.sbuf_tensor(name, shape, F32))
        ident = sb("ident_sb", [P, P])
        ident_in = ctx.enter_context(nc.semaphore("ident_in"))
        g = Shared()
        g.ident = ident
        g.x = sb("x_all", [P, B, T])
        g.xw = sb("xw_all", [P, B, T])
        g.bank = ctx.enter_context(nc.psum_tensor("bank", [P, 8, T], F32))
        g.place = ctx.enter_context(nc.sbuf_tensor("place_all", [P, TILES], mybir.dt.int32))
        g.tile_expert = ctx.enter_context(nc.sbuf_tensor("tile_expert", [P, SLOTS], mybir.dt.int32))
        g.pmax = sb("pmax_all", [P, TILES])
        g.x_sorted = nc.dram_tensor("x_sorted", (SLOTS * P, D), F32, kind="Internal").ap()
        g.y_sorted = nc.dram_tensor("y_sorted", (SLOTS * P, D), F32, kind="Internal").ap()
        g.passed = ctx.enter_context(nc.semaphore("passed"))
        g.scattered = ctx.enter_context(nc.semaphore("scattered"))
        g.taken = [ctx.enter_context(nc.semaphore("taken%d" % k)) for k in range(8)]
        with nc.Block() as block:
            @block.sync
            def _(sp):
                sp.dma_start(ident[:, :], w["ident"]).then_inc(ident_in, 16)
                sp.wait_ge(ident_in, 16)

        def part(prefix, *tables):
            own = {k[len(prefix):]: v for k, v in w.items() if k.startswith(prefix)}
            own.update({k: w[k] for k in tables})
            return own

        l0 = part("L0_attn_", "rtab", "tri", "diag", "heads")
        l0["x"] = w["L0_attn_hidden_states"]
        run_phase(nc, g, l0_retention, l0)
        run_phase(nc, g, norm_and_route, part("L0_ffn_", *MOE_TABLES))
        run_phase(nc, g, l0_experts, part("L0_ffn_"))
        run_phase(nc, g, gather_and_norm)
        run_phase(nc, g, l1_attention, part("L1_attn_"))
        run_phase(nc, g, outer_norm, "n2_")
        run_phase(nc, g, l1_local, part("L1_ffn_", "tab", "band"))
        run_phase(nc, g, outer_norm, "n3_", out)


def kernel(**inputs):
    import concourse.bacc as bacc
    from concourse.bass_utils import run_bass_kernel_spmd

    nc = bacc.Bacc("TRN2", target_bir_lowering=False, num_devices=1)
    arrays = {name: np.ascontiguousarray(a) for name, a in inputs.items()}
    arrays["ident"] = np.eye(P, dtype=np.float32)
    arrays["tab"], arrays["band"] = local_tables()
    arrays["rtab"], arrays["tri"], arrays["diag"], arrays["heads"] = retention_tables()
    arrays.update(moe_tables())
    w = {name: nc.dram_tensor("in_" + name, a.shape, F32, kind="ExternalInput").ap() for name, a in arrays.items()}
    out = nc.dram_tensor("out_x", (B, T, D), F32, kind="ExternalOutput").ap()
    program(nc, w, out)
    r = run_bass_kernel_spmd(nc, [{"in_" + name: a for name, a in arrays.items()}], core_ids=[0])
    return r.results[0]["out_x"]
```
